# Optimizing a Trainium2 kernel written in Bass

```python
import numpy as np
import jax
import jax.numpy as jnp

def _softmax(x, axis=-1):
    return jax.nn.softmax(x, axis=axis)

def _gelu(x):
    return jax.nn.gelu(x, approximate=True)

def _silu(x):
    return jax.nn.silu(x)

def _sigmoid(x):
    return jax.nn.sigmoid(x)

def _layernorm(x, axis=-1, eps=1e-05):
    m = jnp.mean(x, axis=axis, keepdims=True)
    v = jnp.var(x, axis=axis, keepdims=True)
    return (x - m) / jnp.sqrt(v + eps)

def _scatter_add(tgt, idx, src, axis=0):
    return tgt.at[idx].add(src)

def _segment_sum(src, seg, n):
    return jax.ops.segment_sum(src, seg, n)
kernel_name = 'mk_decoder_preln_d4_seqx_r8_1126f1'

def setup_inputs(seed: int=0):
    np.random.seed(seed)
    _w = jnp.asarray

    def _rec_inputs():
        import jax
        import jax.numpy as jnp
        _rk = jax.random.key(seed)
        x = -0.0002928 + 1 * jax.random.normal(jax.random.fold_in(_rk, 1), (32, 128, 128), jnp.float32)
        _lenS = 128 - jax.random.randint(jax.random.fold_in(_rk, 7), (32,), 0, max(1, 128 // 4) + 1, jnp.int32)
        _lenS2 = 128 - jax.random.randint(jax.random.fold_in(_rk, 8), (32,), 0, max(1, 128 // 4) + 1, jnp.int32)
        _ctx_1024P = jax.random.normal(jax.random.fold_in(_rk, 11), (32, 16, 128), jnp.float32)
        _ctx_1024c = jax.random.dirichlet(jax.random.fold_in(_rk, 511), 0.3 * jnp.ones((16,), jnp.float32), (32, 128))
        _ctx_1024t = jnp.einsum('bsk,bkd->bsd', _ctx_1024c, _ctx_1024P)
        _ctx_1024t = _ctx_1024t * jax.lax.rsqrt(jnp.mean(jnp.square(_ctx_1024t)) + 1e-12) * 0.953939
        ctx_1024 = -1.39393e-06 + 0.999914 * (_ctx_1024t + 0.3 * jax.random.normal(jax.random.fold_in(_rk, 611), (32, 128, 128), jnp.float32))
        return (x, ctx_1024)
    x, ctx_1024 = _rec_inputs()

    def _L0_attn_setup():
        import jax, jax.numpy as jnp
        import numpy as np
        DIM = 128
        HEADS = 16
        HEAD_DIM = DIM // HEADS
        RANK = 16
        LORA_ALPHA = 1
        SCALING = LORA_ALPHA / RANK
        SCALE = HEAD_DIM ** (-0.5)
        B, N = (8, 128)

        def _lora_linear(x, W, A, Blo, bias=None):
            y = x @ W.T + x @ A.T @ Blo.T * SCALING
            if bias is not None:
                y = y + bias
            return y

        def _split_heads(t, b, n):
            return t.reshape(b, n, HEADS, HEAD_DIM).transpose(0, 2, 1, 3)
        key = jax.random.key(seed)
        ks = jax.random.split(key, 15)
        s = 1.0 / np.sqrt(DIM)
        inp = {'x': jax.random.normal(ks[0], (B, N, DIM), jnp.float32), 'Wq': jax.random.normal(ks[1], (DIM, DIM), jnp.float32) * s, 'Wk': jax.random.normal(ks[2], (DIM, DIM), jnp.float32) * s, 'Wv': jax.random.normal(ks[3], (DIM, DIM), jnp.float32) * s, 'Wo': jax.random.normal(ks[4], (DIM, DIM), jnp.float32) * s, 'bo': jnp.zeros((DIM,), jnp.float32), 'Aq': jax.random.normal(ks[5], (RANK, DIM), jnp.float32) * s, 'Bq': jax.random.normal(ks[6], (DIM, RANK), jnp.float32) * s, 'Ak': jax.random.normal(ks[7], (RANK, DIM), jnp.float32) * s, 'Bk': jax.random.normal(ks[8], (DIM, RANK), jnp.float32) * s, 'Av': jax.random.normal(ks[9], (RANK, DIM), jnp.float32) * s, 'Bv': jax.random.normal(ks[10], (DIM, RANK), jnp.float32) * s, 'Ao': jax.random.normal(ks[11], (RANK, DIM), jnp.float32) * s, 'Bo': jax.random.normal(ks[12], (DIM, RANK), jnp.float32) * s}
        return inp
    _L0_attn_all = _L0_attn_setup()
    _L0_attn_in = {k: v for k, v in _L0_attn_all.items() if k in ('Wq', 'Wk', 'Wv', 'Wo', 'bo', 'Aq', 'Bq', 'Ak', 'Bk', 'Av', 'Bv', 'Ao', 'Bo')}
    del _L0_attn_all

    def _L0_xattn_setup():
        import jax, jax.numpy as jnp
        import numpy as np
        import math
        D_MODEL = 128
        N_HEAD = 16
        B = 2
        L = 256

        def _linear(x, W, b):
            return jnp.einsum('bld,od->blo', x, W) + b
        key = jax.random.key(seed)
        ks = jax.random.split(key, 11)
        s = 1.0 / math.sqrt(D_MODEL)
        inp = {'q': jax.random.normal(ks[0], (B, L, D_MODEL), jnp.float32), 'k': jax.random.normal(ks[1], (B, L, D_MODEL), jnp.float32), 'v': jax.random.normal(ks[2], (B, L, D_MODEL), jnp.float32), 'wq': jax.random.normal(ks[3], (D_MODEL, D_MODEL), jnp.float32) * s, 'bq': jnp.zeros((D_MODEL,), jnp.float32), 'wk': jax.random.normal(ks[4], (D_MODEL, D_MODEL), jnp.float32) * s, 'bk': jnp.zeros((D_MODEL,), jnp.float32), 'wv': jax.random.normal(ks[5], (D_MODEL, D_MODEL), jnp.float32) * s, 'bv': jnp.zeros((D_MODEL,), jnp.float32), 'wo': jax.random.normal(ks[6], (D_MODEL, D_MODEL), jnp.float32) * s, 'bo': jnp.zeros((D_MODEL,), jnp.float32)}
        return inp
    _L0_xattn_all = _L0_xattn_setup()
    _L0_xattn_in = {k: v for k, v in _L0_xattn_all.items() if k in ('wq', 'bq', 'wk', 'bk', 'wv', 'bv', 'wo', 'bo')}
    del _L0_xattn_all

    def _L0_ffn_setup():
        import jax, jax.numpy as jnp
        import numpy as np
        T, Z, D_DIM = (8, 256, 128)
        N_EXP, P_SLOT, H = (64, 32, 128)
        LN_EPS = 1e-05
        key = jax.random.key(seed)
        k = jax.random.split(key, 5)
        s = 0.02
        return {'x': jax.random.normal(k[0], (T, Z, D_DIM), dtype=jnp.float32), 'phi_w': jax.random.normal(k[1], (N_EXP * P_SLOT, D_DIM), dtype=jnp.float32) * s, 'phi_b': jax.random.normal(k[2], (N_EXP * P_SLOT,), dtype=jnp.float32) * s, 'expert_w': jax.random.normal(k[3], (N_EXP, D_DIM, H), dtype=jnp.float32) * s, 'expert_b': jax.random.normal(k[4], (N_EXP, H), dtype=jnp.float32) * s}
    _L0_ffn_all = _L0_ffn_setup()
    _L0_ffn_in = {k: v for k, v in _L0_ffn_all.items() if k in ('phi_w', 'phi_b', 'expert_w', 'expert_b')}
    del _L0_ffn_all

    def _L1_attn_setup():
        import jax, jax.numpy as jnp
        import numpy as np
        import math
        KSIZE = 4
        EPS_NORM = 1e-12
        EPS_LN = 1e-05

        def short_conv(x, w):
            b, l, c = x.shape
            K = w.shape[1]
            xp = jnp.pad(x, ((0, 0), (K - 1, 0), (0, 0)))
            y = x
            for j in range(K):
                y = y + xp[:, j:j + l, :] * w[:, j]
            return y

        def l2norm(x):
            return x * jax.lax.rsqrt(jnp.sum(x * x, axis=-1, keepdims=True) + EPS_NORM)

        def titans_forward(hidden_states, Wq, Wk, Wv, conv_q, conv_k, conv_v, W_init, ln_gamma, ln_beta, Wg, Wo, num_heads=16, chunk_size=16):
            b, l, dim = hidden_states.shape
            h = num_heads
            dk = dim // h
            cs = chunk_size
            nc = l // cs
            q = l2norm(jax.nn.silu(short_conv(hidden_states @ Wq.T, conv_q)).reshape(b, l, h, dk))
            k = l2norm(jax.nn.silu(short_conv(hidden_states @ Wk.T, conv_k)).reshape(b, l, h, dk))
            v = jax.nn.silu(short_conv(hidden_states @ Wv.T, conv_v)).reshape(b, l, h, dk)
            qc = q.reshape(b, nc, cs, h, dk).transpose(1, 0, 2, 3, 4)
            kc = k.reshape(b, nc, cs, h, dk).transpose(1, 0, 2, 3, 4)
            vc = v.reshape(b, nc, cs, h, dk).transpose(1, 0, 2, 3, 4)
            mask = jnp.tril(jnp.ones((cs, cs), q.dtype))
            W0 = jnp.broadcast_to(W_init, (b, h, dk, dk))

            def step(W, chunk):
                q_c, k_c, v_c = chunk
                inter = jnp.einsum('bqhk,bhkv->bqhv', q_c, W)
                qk = jnp.einsum('bqhd,bkhd->bhqk', q_c, k_c) * mask
                intra = jnp.einsum('bhqk,bkhv->bqhv', qk, v_c)
                W_new = W + jnp.einsum('bchk,bchv->bhkv', k_c, v_c)
                return (W_new, inter + intra)
            _, o = jax.lax.scan(step, W0, (qc, kc, vc))
            o = o.transpose(1, 0, 2, 3, 4).reshape(b, l, h, dk)
            mu = jnp.mean(o, axis=-1, keepdims=True)
            var = jnp.mean((o - mu) ** 2, axis=-1, keepdims=True)
            o = (o - mu) * jax.lax.rsqrt(var + EPS_LN) * ln_gamma + ln_beta
            o = o.reshape(b, l, dim)
            gate = hidden_states @ Wg.T
            return o * gate @ Wo.T
        key = jax.random.key(seed)
        ks = jax.random.split(key, 12)
        b, l, dim = (4, 256, 128)
        h = 16
        dk = dim // h
        s = 1.0 / math.sqrt(dim)
        inp = {'hidden_states': jax.random.normal(ks[0], (b, l, dim), jnp.float32), 'Wq': jax.random.normal(ks[1], (dim, dim), jnp.float32) * s, 'Wk': jax.random.normal(ks[2], (dim, dim), jnp.float32) * s, 'Wv': jax.random.normal(ks[3], (dim, dim), jnp.float32) * s, 'conv_q': jax.random.normal(ks[4], (dim, KSIZE), jnp.float32) * 0.1, 'conv_k': jax.random.normal(ks[5], (dim, KSIZE), jnp.float32) * 0.1, 'conv_v': jax.random.normal(ks[6], (dim, KSIZE), jnp.float32) * 0.1, 'W_init': jax.random.normal(ks[7], (1, h, dk, dk), jnp.float32) / math.sqrt(dk), 'ln_gamma': jnp.ones((dk,), jnp.float32), 'ln_beta': jnp.zeros((dk,), jnp.float32), 'Wg': jax.random.normal(ks[8], (dim, dim), jnp.float32) * s, 'Wo': jax.random.normal(ks[9], (dim, dim), jnp.float32) * s}
        return inp
    _L1_attn_all = _L1_attn_setup()
    _L1_attn_in = {k: v for k, v in _L1_attn_all.items() if k in ('Wq', 'Wk', 'Wv', 'conv_q', 'conv_k', 'conv_v', 'W_init', 'ln_gamma', 'ln_beta', 'Wg', 'Wo')}
    del _L1_attn_all

    def _L1_xattn_setup():
        import jax, jax.numpy as jnp
        import numpy as np
        import math
        DIM_MODEL = 128
        N_HEAD = 16
        NUM_NEURON = 64
        MAX_LEN = 256
        B, S = (4, 256)

        def _split_heads(x):
            b, s, _ = x.shape
            return x.reshape(b, s, N_HEAD, NUM_NEURON).transpose(0, 2, 1, 3)
        key = jax.random.key(seed)
        ks = jax.random.split(key, 11)
        d, p = (DIM_MODEL, N_HEAD * NUM_NEURON)
        sc_in = 1.0 / math.sqrt(d)
        sc_p = 1.0 / math.sqrt(p)
        return {'q': jax.random.normal(ks[0], (B, S, d), jnp.float32), 'k': jax.random.normal(ks[1], (B, S, d), jnp.float32), 'v': jax.random.normal(ks[2], (B, S, d), jnp.float32), 'Wq': jax.random.normal(ks[3], (d, p), jnp.float32) * sc_in, 'bq': jnp.zeros((p,), jnp.float32), 'Wk': jax.random.normal(ks[4], (d, p), jnp.float32) * sc_in, 'bk': jnp.zeros((p,), jnp.float32), 'Wv': jax.random.normal(ks[5], (d, p), jnp.float32) * sc_in, 'bv': jnp.zeros((p,), jnp.float32), 'Wf': jax.random.normal(ks[6], (p, d), jnp.float32) * sc_p, 'bf': jnp.zeros((d,), jnp.float32)}
    _L1_xattn_all = _L1_xattn_setup()
    _L1_xattn_in = {k: v for k, v in _L1_xattn_all.items() if k in ('Wq', 'bq', 'Wk', 'bk', 'Wv', 'bv', 'Wf', 'bf')}
    del _L1_xattn_all

    def _L1_ffn_setup():
        import jax, jax.numpy as jnp
        import numpy as np
        BLOCK_SIZE = 32
        FP6_E2M3_MAX = 7.5

        def _build_fp6_e2m3_grid():
            vals = set()
            for bits in range(64):
                s = bits >> 5 & 1
                e = bits >> 3 & 3
                m = bits & 7
                v = m / 8.0 if e == 0 else (1.0 + m / 8.0) * 2.0 ** (e - 1)
                vals.add(-v if s else v)
            return np.array(sorted(vals), dtype=np.float32)
        _GRID = jnp.asarray(_build_fp6_e2m3_grid())

        def _nearest_on_grid(x, grid):
            idx = jnp.clip(jnp.searchsorted(grid, x), 0, grid.shape[0] - 1)
            idx_lo = jnp.maximum(idx - 1, 0)
            v_hi = grid[idx]
            v_lo = grid[idx_lo]
            return jnp.where(jnp.abs(x - v_lo) <= jnp.abs(x - v_hi), v_lo, v_hi)

        def _mx_quantize(t, eps=1e-30):
            rows, K = t.shape
            blocks = t.reshape(rows, K // BLOCK_SIZE, BLOCK_SIZE)
            scales = jnp.maximum(jnp.max(jnp.abs(blocks), axis=-1) / FP6_E2M3_MAX, eps)
            q = _nearest_on_grid(blocks / scales[..., None], _GRID)
            return (q, scales)
        key = jax.random.key(seed)
        k1, k2, k3 = jax.random.split(key, 3)
        x = jax.random.normal(k1, (8, 1024, 128), dtype=jnp.float32)
        weight = jax.random.normal(k2, (128, 128), dtype=jnp.float32) * 0.02
        bias = jax.random.normal(k3, (128,), dtype=jnp.float32) * 0.02
        return {'x': x, 'weight': weight, 'bias': bias}
    _L1_ffn_all = _L1_ffn_setup()
    _L1_ffn_in = {k: v for k, v in _L1_ffn_all.items() if k in ('weight', 'bias')}
    del _L1_ffn_all

    def _L2_attn_setup():
        import jax, jax.numpy as jnp
        import numpy as np
        D_MODEL = 128
        N_HEADS = 16
        D_HEAD = D_MODEL // N_HEADS
        EPS = 1e-06

        def _phi(x):
            return jax.nn.elu(x) + 1.0
        key = jax.random.key(seed)
        k1, k2, k3 = jax.random.split(key, 3)
        x = jax.random.normal(k1, (4, 512, D_MODEL), dtype=jnp.float32)
        s = 1.0 / np.sqrt(D_MODEL)
        w_qkv = jax.random.uniform(k2, (3 * D_MODEL, D_MODEL), minval=-s, maxval=s, dtype=jnp.float32)
        w_out = jax.random.uniform(k3, (D_MODEL, D_MODEL), minval=-s, maxval=s, dtype=jnp.float32)
        return {'x': x, 'w_qkv': w_qkv, 'w_out': w_out}
    _L2_attn_all = _L2_attn_setup()
    _L2_attn_in = {k: v for k, v in _L2_attn_all.items() if k in ('w_qkv', 'w_out')}
    del _L2_attn_all

    def _L2_xattn_setup():
        import jax, jax.numpy as jnp
        import numpy as np
        D_MODEL = 128
        NHEAD = 16
        D_K = D_MODEL // NHEAD

        def _split_heads(x):
            B, S, _ = x.shape
            return x.reshape(B, S, NHEAD, D_K).transpose(0, 2, 1, 3)
        key = jax.random.key(seed)
        ks = jax.random.split(key, 11)
        B, S = (4, 256)
        s = 1.0 / np.sqrt(D_MODEL)
        return {'query': jax.random.normal(ks[0], (B, S, D_MODEL), jnp.float32), 'key': jax.random.normal(ks[1], (B, S, D_MODEL), jnp.float32), 'value': jax.random.normal(ks[2], (B, S, D_MODEL), jnp.float32), 'Wq': jax.random.normal(ks[3], (D_MODEL, D_MODEL), jnp.float32) * s, 'bq': jnp.zeros((D_MODEL,), jnp.float32), 'Wk': jax.random.normal(ks[4], (D_MODEL, D_MODEL), jnp.float32) * s, 'bk': jnp.zeros((D_MODEL,), jnp.float32), 'Wv': jax.random.normal(ks[5], (D_MODEL, D_MODEL), jnp.float32) * s, 'bv': jnp.zeros((D_MODEL,), jnp.float32), 'Wo': jax.random.normal(ks[6], (D_MODEL, D_MODEL), jnp.float32) * s, 'bo': jnp.zeros((D_MODEL,), jnp.float32)}
    _L2_xattn_all = _L2_xattn_setup()
    _L2_xattn_in = {k: v for k, v in _L2_xattn_all.items() if k in ('Wq', 'bq', 'Wk', 'bk', 'Wv', 'bv', 'Wo', 'bo')}
    del _L2_xattn_all

    def _L2_ffn_setup():
        import jax, jax.numpy as jnp
        import numpy as np
        TOPK = 4
        key = jax.random.key(seed)
        ks = jax.random.split(key, 9)
        B, T, D = (4, 256, 128)
        E, H = (32, 128)
        HS = H * TOPK
        s = lambda k, shape, fan: jax.random.normal(k, shape, dtype=jnp.float32) / np.sqrt(fan)
        return {'x': jax.random.normal(ks[0], (B, T, D), dtype=jnp.float32), 'router_w': s(ks[1], (E, D), D), 'router_bias': jnp.zeros((E,), dtype=jnp.float32), 'gate_w': s(ks[2], (E, H, D), D), 'up_w': s(ks[3], (E, H, D), D), 'down_w': s(ks[4], (E, D, H), H), 'sgate_w': s(ks[5], (HS, D), D), 'sup_w': s(ks[6], (HS, D), D), 'sdown_w': s(ks[7], (D, HS), HS)}
    _L2_ffn_all = _L2_ffn_setup()
    _L2_ffn_in = {k: v for k, v in _L2_ffn_all.items() if k in ('router_w', 'router_bias', 'gate_w', 'up_w', 'down_w', 'sgate_w', 'sup_w', 'sdown_w')}
    del _L2_ffn_all

    def _L3_attn_setup():
        import jax, jax.numpy as jnp
        import numpy as np
        B, S, D = (2, 256, 128)
        H, DQ, DV = (16, 64, 64)
        key = jax.random.key(seed)
        k1, k2, k3, k4, k5 = jax.random.split(key, 5)
        scale = 0.02
        return {'x': jax.random.normal(k1, (B, S, D), dtype=jnp.float32), 'w_q': jax.random.normal(k2, (H, DQ, D), dtype=jnp.float32) * scale, 'w_k': jax.random.normal(k3, (H, DQ, D), dtype=jnp.float32) * scale, 'w_v': jax.random.normal(k4, (H, DV, D), dtype=jnp.float32) * scale, 'w_o': jax.random.normal(k5, (D, H * DV), dtype=jnp.float32) * scale}
    _L3_attn_all = _L3_attn_setup()
    _L3_attn_in = {k: v for k, v in _L3_attn_all.items() if k in ('w_q', 'w_k', 'w_v', 'w_o')}
    del _L3_attn_all

    def _L3_xattn_setup():
        import jax, jax.numpy as jnp
        import numpy as np
        DIM = 128
        HEADS = 8
        HEAD_DIM = DIM // HEADS
        TAU = HEAD_DIM ** 0.5
        BS, SEQ = (1, 256)
        key = jax.random.key(seed)
        kq, kk, kv, kb = jax.random.split(key, 4)
        q = jax.random.normal(kq, (BS, SEQ, DIM), jnp.float32)
        k = jax.random.normal(kk, (BS, SEQ, DIM), jnp.float32)
        v = jax.random.normal(kv, (BS, SEQ, DIM), jnp.float32)
        Wi_w = jnp.zeros((HEADS, 3 * DIM), jnp.float32)
        Wi_b = 0.1 * jax.random.normal(kb, (HEADS,), jnp.float32)
        Wf_w = jnp.zeros((HEADS, 3 * DIM), jnp.float32)
        Wf_b = jnp.linspace(3.0, 6.0, HEADS, dtype=jnp.float32)
        gn_w = jnp.ones((DIM,), jnp.float32)
        gn_b = jnp.zeros((DIM,), jnp.float32)
        return {'q': q, 'k': k, 'v': v, 'Wi_w': Wi_w, 'Wi_b': Wi_b, 'Wf_w': Wf_w, 'Wf_b': Wf_b, 'gn_w': gn_w, 'gn_b': gn_b}
    _L3_xattn_all = _L3_xattn_setup()
    _L3_xattn_in = {k: v for k, v in _L3_xattn_all.items() if k in ('Wi_w', 'Wi_b', 'Wf_w', 'Wf_b', 'gn_w', 'gn_b')}
    del _L3_xattn_all

    def _L3_ffn_setup():
        import jax, jax.numpy as jnp
        import numpy as np
        from jax import lax
        N_HEADS = 16
        TOP_K = 2
        N_EXPERTS = 8

        def layer_norm(x, w, b, eps=1e-05):
            mu = jnp.mean(x, axis=-1, keepdims=True)
            var = jnp.mean(jnp.square(x - mu), axis=-1, keepdims=True)
            return (x - mu) * lax.rsqrt(var + eps) * w + b

        def attention(x, w_qkv, b_qkv, w_o, b_o):
            B, T, D = x.shape
            dh = D // N_HEADS
            qkv = x @ w_qkv + b_qkv
            q, k, v = jnp.split(qkv, 3, axis=-1)
            q = q.reshape(B, T, N_HEADS, dh)
            k = k.reshape(B, T, N_HEADS, dh)
            v = v.reshape(B, T, N_HEADS, dh)
            scores = jnp.einsum('bqhd,bkhd->bhqk', q, k) / jnp.sqrt(jnp.float32(dh)).astype(x.dtype)
            probs = jax.nn.softmax(scores, axis=-1)
            ctx = jnp.einsum('bhqk,bkhd->bqhd', probs, v).reshape(B, T, D)
            return ctx @ w_o + b_o

        def moe_ff(x, w_gate, w1, b1, w2, b2):
            B, T, D = x.shape
            t = x.reshape(B * T, D)
            probs = jax.nn.softmax(t @ w_gate, axis=-1)
            tw, ti = lax.top_k(probs, TOP_K)
            tw = tw / jnp.sum(tw, axis=-1, keepdims=True)
            out = jnp.zeros_like(t)
            for e in range(N_EXPERTS):
                we = jnp.sum(jnp.where(ti == e, tw, 0.0), axis=-1)
                h = jax.nn.gelu(t @ w1[e] + b1[e]) @ w2[e] + b2[e]
                out = out + we[:, None] * h
            return out.reshape(B, T, D)
        key = jax.random.key(seed)
        ks = jax.random.split(key, 8)
        B, T, D, H, E = (4, 64, 128, 512, 8)
        s = lambda d: 1.0 / np.sqrt(d)
        return {'x': jax.random.normal(ks[0], (B, T, D), jnp.float32), 'ln1_w': jnp.ones((D,), jnp.float32), 'ln1_b': jnp.zeros((D,), jnp.float32), 'ln2_w': jnp.ones((D,), jnp.float32), 'ln2_b': jnp.zeros((D,), jnp.float32), 'w_qkv': jax.random.normal(ks[1], (D, 3 * D), jnp.float32) * s(D), 'b_qkv': jnp.zeros((3 * D,), jnp.float32), 'w_o': jax.random.normal(ks[2], (D, D), jnp.float32) * s(D), 'b_o': jnp.zeros((D,), jnp.float32), 'w_gate': jax.random.normal(ks[3], (D, E), jnp.float32) * s(D), 'w1': jax.random.normal(ks[4], (E, D, H), jnp.float32) * s(D), 'b1': jnp.zeros((E, H), jnp.float32), 'w2': jax.random.normal(ks[5], (E, H, D), jnp.float32) * s(H), 'b2': jnp.zeros((E, D), jnp.float32)}
    _L3_ffn_all = _L3_ffn_setup()
    _L3_ffn_in = {k: v for k, v in _L3_ffn_all.items() if k in ('ln1_w', 'ln1_b', 'ln2_w', 'ln2_b', 'w_qkv', 'b_qkv', 'w_o', 'b_o', 'w_gate', 'w1', 'b1', 'w2', 'b2')}
    del _L3_ffn_all
    return {'x': x, 'ctx_1024': ctx_1024, 'L0_attn_Wq': _L0_attn_in['Wq'], 'L0_attn_Wk': _L0_attn_in['Wk'], 'L0_attn_Wv': _L0_attn_in['Wv'], 'L0_attn_Wo': _L0_attn_in['Wo'], 'L0_attn_bo': _L0_attn_in['bo'], 'L0_attn_Aq': _L0_attn_in['Aq'], 'L0_attn_Bq': _L0_attn_in['Bq'], 'L0_attn_Ak': _L0_attn_in['Ak'], 'L0_attn_Bk': _L0_attn_in['Bk'], 'L0_attn_Av': _L0_attn_in['Av'], 'L0_attn_Bv': _L0_attn_in['Bv'], 'L0_attn_Ao': _L0_attn_in['Ao'], 'L0_attn_Bo': _L0_attn_in['Bo'], 'L0_xattn_wq': _L0_xattn_in['wq'], 'L0_xattn_bq': _L0_xattn_in['bq'], 'L0_xattn_wk': _L0_xattn_in['wk'], 'L0_xattn_bk': _L0_xattn_in['bk'], 'L0_xattn_wv': _L0_xattn_in['wv'], 'L0_xattn_bv': _L0_xattn_in['bv'], 'L0_xattn_wo': _L0_xattn_in['wo'], 'L0_xattn_bo': _L0_xattn_in['bo'], 'L0_ffn_phi_w': _L0_ffn_in['phi_w'], 'L0_ffn_phi_b': _L0_ffn_in['phi_b'], 'L0_ffn_expert_w': _L0_ffn_in['expert_w'], 'L0_ffn_expert_b': _L0_ffn_in['expert_b'], 'L1_attn_Wq': _L1_attn_in['Wq'], 'L1_attn_Wk': _L1_attn_in['Wk'], 'L1_attn_Wv': _L1_attn_in['Wv'], 'L1_attn_conv_q': _L1_attn_in['conv_q'], 'L1_attn_conv_k': _L1_attn_in['conv_k'], 'L1_attn_conv_v': _L1_attn_in['conv_v'], 'L1_attn_W_init': _L1_attn_in['W_init'], 'L1_attn_ln_gamma': _L1_attn_in['ln_gamma'], 'L1_attn_ln_beta': _L1_attn_in['ln_beta'], 'L1_attn_Wg': _L1_attn_in['Wg'], 'L1_attn_Wo': _L1_attn_in['Wo'], 'L1_xattn_Wq': _L1_xattn_in['Wq'], 'L1_xattn_bq': _L1_xattn_in['bq'], 'L1_xattn_Wk': _L1_xattn_in['Wk'], 'L1_xattn_bk': _L1_xattn_in['bk'], 'L1_xattn_Wv': _L1_xattn_in['Wv'], 'L1_xattn_bv': _L1_xattn_in['bv'], 'L1_xattn_Wf': _L1_xattn_in['Wf'], 'L1_xattn_bf': _L1_xattn_in['bf'], 'L1_ffn_weight': _L1_ffn_in['weight'], 'L1_ffn_bias': _L1_ffn_in['bias'], 'L2_attn_w_qkv': _L2_attn_in['w_qkv'], 'L2_attn_w_out': _L2_attn_in['w_out'], 'L2_xattn_Wq': _L2_xattn_in['Wq'], 'L2_xattn_bq': _L2_xattn_in['bq'], 'L2_xattn_Wk': _L2_xattn_in['Wk'], 'L2_xattn_bk': _L2_xattn_in['bk'], 'L2_xattn_Wv': _L2_xattn_in['Wv'], 'L2_xattn_bv': _L2_xattn_in['bv'], 'L2_xattn_Wo': _L2_xattn_in['Wo'], 'L2_xattn_bo': _L2_xattn_in['bo'], 'L2_ffn_router_w': _L2_ffn_in['router_w'], 'L2_ffn_router_bias': _L2_ffn_in['router_bias'], 'L2_ffn_gate_w': _L2_ffn_in['gate_w'], 'L2_ffn_up_w': _L2_ffn_in['up_w'], 'L2_ffn_down_w': _L2_ffn_in['down_w'], 'L2_ffn_sgate_w': _L2_ffn_in['sgate_w'], 'L2_ffn_sup_w': _L2_ffn_in['sup_w'], 'L2_ffn_sdown_w': _L2_ffn_in['sdown_w'], 'L3_attn_w_q': _L3_attn_in['w_q'], 'L3_attn_w_k': _L3_attn_in['w_k'], 'L3_attn_w_v': _L3_attn_in['w_v'], 'L3_attn_w_o': _L3_attn_in['w_o'], 'L3_xattn_Wi_w': _L3_xattn_in['Wi_w'], 'L3_xattn_Wi_b': _L3_xattn_in['Wi_b'], 'L3_xattn_Wf_w': _L3_xattn_in['Wf_w'], 'L3_xattn_Wf_b': _L3_xattn_in['Wf_b'], 'L3_xattn_gn_w': _L3_xattn_in['gn_w'], 'L3_xattn_gn_b': _L3_xattn_in['gn_b'], 'L3_ffn_ln1_w': _L3_ffn_in['ln1_w'], 'L3_ffn_ln1_b': _L3_ffn_in['ln1_b'], 'L3_ffn_ln2_w': _L3_ffn_in['ln2_w'], 'L3_ffn_ln2_b': _L3_ffn_in['ln2_b'], 'L3_ffn_w_qkv': _L3_ffn_in['w_qkv'], 'L3_ffn_b_qkv': _L3_ffn_in['b_qkv'], 'L3_ffn_w_o': _L3_ffn_in['w_o'], 'L3_ffn_b_o': _L3_ffn_in['b_o'], 'L3_ffn_w_gate': _L3_ffn_in['w_gate'], 'L3_ffn_w1': _L3_ffn_in['w1'], 'L3_ffn_b1': _L3_ffn_in['b1'], 'L3_ffn_w2': _L3_ffn_in['w2'], 'L3_ffn_b2': _L3_ffn_in['b2']}

def reference(x, ctx_1024, L0_attn_Wq, L0_attn_Wk, L0_attn_Wv, L0_attn_Wo, L0_attn_bo, L0_attn_Aq, L0_attn_Bq, L0_attn_Ak, L0_attn_Bk, L0_attn_Av, L0_attn_Bv, L0_attn_Ao, L0_attn_Bo, L0_xattn_wq, L0_xattn_bq, L0_xattn_wk, L0_xattn_bk, L0_xattn_wv, L0_xattn_bv, L0_xattn_wo, L0_xattn_bo, L0_ffn_phi_w, L0_ffn_phi_b, L0_ffn_expert_w, L0_ffn_expert_b, L1_attn_Wq, L1_attn_Wk, L1_attn_Wv, L1_attn_conv_q, L1_attn_conv_k, L1_attn_conv_v, L1_attn_W_init, L1_attn_ln_gamma, L1_attn_ln_beta, L1_attn_Wg, L1_attn_Wo, L1_xattn_Wq, L1_xattn_bq, L1_xattn_Wk, L1_xattn_bk, L1_xattn_Wv, L1_xattn_bv, L1_xattn_Wf, L1_xattn_bf, L1_ffn_weight, L1_ffn_bias, L2_attn_w_qkv, L2_attn_w_out, L2_xattn_Wq, L2_xattn_bq, L2_xattn_Wk, L2_xattn_bk, L2_xattn_Wv, L2_xattn_bv, L2_xattn_Wo, L2_xattn_bo, L2_ffn_router_w, L2_ffn_router_bias, L2_ffn_gate_w, L2_ffn_up_w, L2_ffn_down_w, L2_ffn_sgate_w, L2_ffn_sup_w, L2_ffn_sdown_w, L3_attn_w_q, L3_attn_w_k, L3_attn_w_v, L3_attn_w_o, L3_xattn_Wi_w, L3_xattn_Wi_b, L3_xattn_Wf_w, L3_xattn_Wf_b, L3_xattn_gn_w, L3_xattn_gn_b, L3_ffn_ln1_w, L3_ffn_ln1_b, L3_ffn_ln2_w, L3_ffn_ln2_b, L3_ffn_w_qkv, L3_ffn_b_qkv, L3_ffn_w_o, L3_ffn_b_o, L3_ffn_w_gate, L3_ffn_w1, L3_ffn_b1, L3_ffn_w2, L3_ffn_b2):
    import jax
    import jax.numpy as jnp

    def _L0_attn_ref(x, Wq, Wk, Wv, Wo, bo, Aq, Bq, Ak, Bk, Av, Bv, Ao, Bo):
        import jax, jax.numpy as jnp
        import numpy as np
        DIM = 128
        HEADS = 16
        HEAD_DIM = DIM // HEADS
        RANK = 16
        LORA_ALPHA = 1
        SCALING = LORA_ALPHA / RANK
        SCALE = HEAD_DIM ** (-0.5)
        B, N = (8, 128)

        def _lora_linear(x, W, A, Blo, bias=None):
            y = x @ W.T + x @ A.T @ Blo.T * SCALING
            if bias is not None:
                y = y + bias
            return y

        def _split_heads(t, b, n):
            return t.reshape(b, n, HEADS, HEAD_DIM).transpose(0, 2, 1, 3)
        b, n, c = x.shape
        q = _split_heads(_lora_linear(x, Wq, Aq, Bq), b, n)
        k = _split_heads(_lora_linear(x, Wk, Ak, Bk), b, n)
        v = _split_heads(_lora_linear(x, Wv, Av, Bv), b, n)
        attn = jnp.einsum('bhnd,bhmd->bhnm', q, k) * SCALE
        attn = jax.nn.softmax(attn, axis=-1)
        out = jnp.einsum('bhnm,bhmd->bhnd', attn, v)
        out = out.transpose(0, 2, 1, 3).reshape(b, n, c)
        return _lora_linear(out, Wo, Ao, Bo, bias=bo)

    def _L0_xattn_ref(q, k, v, wq, bq, wk, bk, wv, bv, wo, bo):
        import jax, jax.numpy as jnp
        import numpy as np
        import math
        D_MODEL = 128
        N_HEAD = 16
        B = 2
        L = 256

        def _linear(x, W, b):
            return jnp.einsum('bld,od->blo', x, W) + b
        b, l, d_model = q.shape
        h = N_HEAD
        d = d_model // h
        qh = _linear(q, wq, bq).reshape(b, h, l, d)
        kh = _linear(k, wk, bk).reshape(b, h, l, d)
        vh = _linear(v, wv, bv).reshape(b, h, l, d)
        kt = kh.reshape(b, h, d, l)
        score = jnp.einsum('bhij,bhjk->bhik', qh, kt) / math.sqrt(d)
        attn = jax.nn.softmax(score, axis=-1)
        out = jnp.einsum('bhls,bhsd->bhld', attn, vh).reshape(b, l, d_model)
        return _linear(out, wo, bo)

    def _L0_ffn_ref(x, phi_w, phi_b, expert_w, expert_b):
        import jax, jax.numpy as jnp
        import numpy as np
        T, Z, D_DIM = (8, 256, 128)
        N_EXP, P_SLOT, H = (64, 32, 128)
        LN_EPS = 1e-05
        t, z, d = x.shape
        n = expert_w.shape[0]
        p = phi_w.shape[0] // n
        logits = (jnp.einsum('tzd,ed->tze', x, phi_w) + phi_b).reshape(t, z, n, p)
        D = jax.nn.softmax(logits, axis=3)
        C = jax.nn.softmax(logits, axis=2)
        X_tilde = jnp.einsum('tznp,tzd->npd', D, x)
        X_tilde = jnp.clip(X_tilde, -33000.0, 65000.0)
        mu = jnp.mean(X_tilde, axis=-1, keepdims=True)
        var = jnp.mean(jnp.square(X_tilde - mu), axis=-1, keepdims=True)
        X_tilde = (X_tilde - mu) * jax.lax.rsqrt(var + LN_EPS)
        X_tilde = jnp.tanh(X_tilde)
        Y_tilde = jnp.einsum('npd,ndH->npH', X_tilde, expert_w) + expert_b[:, None, :]
        Y = jnp.einsum('tznp,npH->tzH', C, Y_tilde)
        return Y

    def _L1_attn_ref(hidden_states, Wq, Wk, Wv, conv_q, conv_k, conv_v, W_init, ln_gamma, ln_beta, Wg, Wo):
        import jax, jax.numpy as jnp
        import numpy as np
        import math
        KSIZE = 4
        EPS_NORM = 1e-12
        EPS_LN = 1e-05

        def short_conv(x, w):
            b, l, c = x.shape
            K = w.shape[1]
            xp = jnp.pad(x, ((0, 0), (K - 1, 0), (0, 0)))
            y = x
            for j in range(K):
                y = y + xp[:, j:j + l, :] * w[:, j]
            return y

        def l2norm(x):
            return x * jax.lax.rsqrt(jnp.sum(x * x, axis=-1, keepdims=True) + EPS_NORM)

        def titans_forward(hidden_states, Wq, Wk, Wv, conv_q, conv_k, conv_v, W_init, ln_gamma, ln_beta, Wg, Wo, num_heads=16, chunk_size=16):
            b, l, dim = hidden_states.shape
            h = num_heads
            dk = dim // h
            cs = chunk_size
            nc = l // cs
            q = l2norm(jax.nn.silu(short_conv(hidden_states @ Wq.T, conv_q)).reshape(b, l, h, dk))
            k = l2norm(jax.nn.silu(short_conv(hidden_states @ Wk.T, conv_k)).reshape(b, l, h, dk))
            v = jax.nn.silu(short_conv(hidden_states @ Wv.T, conv_v)).reshape(b, l, h, dk)
            qc = q.reshape(b, nc, cs, h, dk).transpose(1, 0, 2, 3, 4)
            kc = k.reshape(b, nc, cs, h, dk).transpose(1, 0, 2, 3, 4)
            vc = v.reshape(b, nc, cs, h, dk).transpose(1, 0, 2, 3, 4)
            mask = jnp.tril(jnp.ones((cs, cs), q.dtype))
            W0 = jnp.broadcast_to(W_init, (b, h, dk, dk))

            def step(W, chunk):
                q_c, k_c, v_c = chunk
                inter = jnp.einsum('bqhk,bhkv->bqhv', q_c, W)
                qk = jnp.einsum('bqhd,bkhd->bhqk', q_c, k_c) * mask
                intra = jnp.einsum('bhqk,bkhv->bqhv', qk, v_c)
                W_new = W + jnp.einsum('bchk,bchv->bhkv', k_c, v_c)
                return (W_new, inter + intra)
            _, o = jax.lax.scan(step, W0, (qc, kc, vc))
            o = o.transpose(1, 0, 2, 3, 4).reshape(b, l, h, dk)
            mu = jnp.mean(o, axis=-1, keepdims=True)
            var = jnp.mean((o - mu) ** 2, axis=-1, keepdims=True)
            o = (o - mu) * jax.lax.rsqrt(var + EPS_LN) * ln_gamma + ln_beta
            o = o.reshape(b, l, dim)
            gate = hidden_states @ Wg.T
            return o * gate @ Wo.T
        return titans_forward(hidden_states, Wq, Wk, Wv, conv_q, conv_k, conv_v, W_init, ln_gamma, ln_beta, Wg, Wo)

    def _L1_xattn_ref(q, k, v, Wq, bq, Wk, bk, Wv, bv, Wf, bf):
        import jax, jax.numpy as jnp
        import numpy as np
        import math
        DIM_MODEL = 128
        N_HEAD = 16
        NUM_NEURON = 64
        MAX_LEN = 256
        B, S = (4, 256)

        def _split_heads(x):
            b, s, _ = x.shape
            return x.reshape(b, s, N_HEAD, NUM_NEURON).transpose(0, 2, 1, 3)
        qh = _split_heads(q @ Wq + bq)
        kh = _split_heads(k @ Wk + bk)
        vh = _split_heads(v @ Wv + bv)
        scores = jnp.einsum('bhqd,bhkd->bhqk', qh, kh) / math.sqrt(MAX_LEN)
        s = scores.shape[-1]
        causal = jnp.tril(jnp.ones((s, s), bool))
        scores = jnp.where(causal[None, None], scores, -jnp.inf)
        attn = jax.nn.softmax(scores, axis=-1)
        out = jnp.einsum('bhqk,bhkd->bhqd', attn, vh)
        c = out.transpose(0, 2, 1, 3).reshape(out.shape[0], out.shape[2], N_HEAD * NUM_NEURON)
        return c @ Wf + bf

    def _L1_ffn_ref(x, weight, bias):
        import jax, jax.numpy as jnp
        import numpy as np
        BLOCK_SIZE = 32
        FP6_E2M3_MAX = 7.5

        def _build_fp6_e2m3_grid():
            vals = set()
            for bits in range(64):
                s = bits >> 5 & 1
                e = bits >> 3 & 3
                m = bits & 7
                v = m / 8.0 if e == 0 else (1.0 + m / 8.0) * 2.0 ** (e - 1)
                vals.add(-v if s else v)
            return np.array(sorted(vals), dtype=np.float32)
        _GRID = jnp.asarray(_build_fp6_e2m3_grid())

        def _nearest_on_grid(x, grid):
            idx = jnp.clip(jnp.searchsorted(grid, x), 0, grid.shape[0] - 1)
            idx_lo = jnp.maximum(idx - 1, 0)
            v_hi = grid[idx]
            v_lo = grid[idx_lo]
            return jnp.where(jnp.abs(x - v_lo) <= jnp.abs(x - v_hi), v_lo, v_hi)

        def _mx_quantize(t, eps=1e-30):
            rows, K = t.shape
            blocks = t.reshape(rows, K // BLOCK_SIZE, BLOCK_SIZE)
            scales = jnp.maximum(jnp.max(jnp.abs(blocks), axis=-1) / FP6_E2M3_MAX, eps)
            q = _nearest_on_grid(blocks / scales[..., None], _GRID)
            return (q, scales)
        batch_shape = x.shape[:-1]
        in_features = x.shape[-1]
        x2 = x.astype(jnp.float32).reshape(-1, in_features)
        w2 = weight.astype(jnp.float32)
        xq, xs = _mx_quantize(x2)
        wq, ws = _mx_quantize(w2)
        xd = (xq * xs[..., None]).reshape(x2.shape)
        wd = (wq * ws[..., None]).reshape(w2.shape)
        out = xd @ wd.T + bias
        return out.reshape(*batch_shape, -1)

    def _L2_attn_ref(x, w_qkv, w_out):
        import jax, jax.numpy as jnp
        import numpy as np
        D_MODEL = 128
        N_HEADS = 16
        D_HEAD = D_MODEL // N_HEADS
        EPS = 1e-06

        def _phi(x):
            return jax.nn.elu(x) + 1.0
        B, L, D = x.shape
        H, dh = (N_HEADS, D_HEAD)
        qkv = jnp.einsum('bld,ed->ble', x, w_qkv)
        qkv = qkv.reshape(B, L, 3, H, dh).transpose(2, 0, 3, 1, 4)
        q, k, v = (_phi(qkv[0]), _phi(qkv[1]), qkv[2])
        qT = q.transpose(2, 0, 1, 3)
        kT = k.transpose(2, 0, 1, 3)
        vT = v.transpose(2, 0, 1, 3)
        S0 = jnp.zeros((B, H, dh, dh), dtype=x.dtype)
        z0 = jnp.zeros((B, H, dh), dtype=x.dtype)

        def step(carry, inp):
            S, z = carry
            q_t, k_t, v_t = inp
            S = S + k_t[..., :, None] * v_t[..., None, :]
            z = z + k_t
            num = jnp.einsum('bhde,bhd->bhe', S, q_t)
            den = jnp.maximum(jnp.sum(z * q_t, axis=-1, keepdims=True), EPS)
            return ((S, z), num / den)
        _, out = jax.lax.scan(step, (S0, z0), (qT, kT, vT))
        out = out.transpose(1, 0, 2, 3).reshape(B, L, D)
        return jnp.einsum('bld,ed->ble', out, w_out)

    def _L2_xattn_ref(query, key, value, Wq, bq, Wk, bk, Wv, bv, Wo, bo):
        import jax, jax.numpy as jnp
        import numpy as np
        D_MODEL = 128
        NHEAD = 16
        D_K = D_MODEL // NHEAD

        def _split_heads(x):
            B, S, _ = x.shape
            return x.reshape(B, S, NHEAD, D_K).transpose(0, 2, 1, 3)
        q = _split_heads(query @ Wq.T + bq)
        k = _split_heads(key @ Wk.T + bk)
        v = _split_heads(value @ Wv.T + bv)
        scale = 1.0 / np.sqrt(D_K).astype(np.float32)
        scores = jnp.einsum('bhqd,bhkd->bhqk', q, k) * scale
        attn = jax.nn.softmax(scores, axis=-1)
        out = jnp.einsum('bhqk,bhkd->bhqd', attn, v)
        B, H, S, dk = out.shape
        out = out.transpose(0, 2, 1, 3).reshape(B, S, H * dk)
        return out @ Wo.T + bo

    def _L2_ffn_ref(x, router_w, router_bias, gate_w, up_w, down_w, sgate_w, sup_w, sdown_w):
        import jax, jax.numpy as jnp
        import numpy as np
        TOPK = 4
        B, T, D = x.shape
        flat = x.reshape(B * T, D)
        logits = flat.astype(jnp.float32) @ router_w.T + router_bias
        scores = jax.nn.softmax(logits, axis=-1)
        topk_scores, topk_idx = jax.lax.top_k(scores, TOPK)
        topk_scores = topk_scores / jnp.clip(topk_scores.sum(axis=-1, keepdims=True), 1e-12, None)
        h = jax.nn.silu(jnp.einsum('nd,ehd->neh', flat, gate_w)) * jnp.einsum('nd,ehd->neh', flat, up_w)
        expert_out = jnp.einsum('neh,edh->ned', h, down_w)
        sel = jnp.take_along_axis(expert_out, topk_idx[:, :, None], axis=1)
        out = (sel * topk_scores.astype(flat.dtype)[:, :, None]).sum(axis=1)
        out = out + jax.nn.silu(flat @ sgate_w.T) * (flat @ sup_w.T) @ sdown_w.T
        return out.reshape(B, T, D)

    def _L3_attn_ref(x, w_q, w_k, w_v, w_o):
        import jax, jax.numpy as jnp
        import numpy as np
        B, S, D = (2, 256, 128)
        H, DQ, DV = (16, 64, 64)
        b, s, d = x.shape
        q = jnp.einsum('bsd,hqd->bhsq', x, w_q)
        k = jnp.einsum('bsd,hqd->bhsq', x, w_k)
        v = jnp.einsum('bsd,hvd->bhsv', x, w_v)
        scores = jnp.einsum('bhsq,bhtq->bhst', q, k)
        causal = jnp.triu(jnp.ones((s, s), dtype=bool), k=1)
        masked = jnp.where(causal, -jnp.inf, scores)
        dq = w_q.shape[1]
        weights = jax.nn.softmax(masked / jnp.sqrt(jnp.float32(dq)), axis=-1)
        out = jnp.einsum('bhst,bhtv->bhsv', weights, v)
        cat = out.transpose(0, 2, 1, 3).reshape(b, s, -1)
        return jnp.einsum('bsf,df->bsd', cat, w_o)

    def _L3_xattn_ref(q, k, v, Wi_w, Wi_b, Wf_w, Wf_b, gn_w, gn_b):
        import jax, jax.numpy as jnp
        import numpy as np
        DIM = 128
        HEADS = 8
        HEAD_DIM = DIM // HEADS
        TAU = HEAD_DIM ** 0.5
        BS, SEQ = (1, 256)
        bs, seq, dim = q.shape
        gate_in = jnp.concatenate([q, k, v], axis=-1)
        itilde = jnp.einsum('bsd,hd->bhs', gate_in, Wi_w) + Wi_b[None, :, None]
        ftilde = jnp.einsum('bsd,hd->bhs', gate_in, Wf_w) + Wf_b[None, :, None]
        csum = jnp.cumsum(jax.nn.log_sigmoid(ftilde), axis=-1)
        Fmat = csum[..., :, None] - csum[..., None, :]
        mask = jnp.tril(jnp.ones((seq, seq), dtype=bool))
        F_act = jnp.where(mask, Fmat, -jnp.inf)
        Dtilde = F_act + itilde[..., None, :]
        max_d = jnp.max(Dtilde, axis=-1, keepdims=True)
        D = jnp.exp(Dtilde - max_d)
        qh = q.reshape(bs, seq, HEADS, HEAD_DIM).transpose(0, 2, 1, 3)
        kh = k.reshape(bs, seq, HEADS, HEAD_DIM).transpose(0, 2, 1, 3)
        vh = v.reshape(bs, seq, HEADS, HEAD_DIM).transpose(0, 2, 1, 3)
        Ctilde = jnp.einsum('bhid,bhjd->bhij', qh, kh) * D / TAU
        maxit = jnp.maximum(jnp.abs(jnp.sum(Ctilde, axis=-1, keepdims=True)), jnp.exp(-max_d))
        Htilde = jnp.einsum('bhij,bhjd->bhid', Ctilde, vh) / (maxit + 1e-06)
        x = Htilde.transpose(0, 2, 1, 3).reshape(bs * seq, HEADS, HEAD_DIM)
        mean = jnp.mean(x, axis=-1, keepdims=True)
        var = jnp.var(x, axis=-1, keepdims=True)
        xn = (x - mean) / jnp.sqrt(var + 1e-05)
        out = xn.reshape(bs * seq, DIM) * gn_w + gn_b
        return out.reshape(bs, seq, DIM)

    def _L3_ffn_ref(x, ln1_w, ln1_b, ln2_w, ln2_b, w_qkv, b_qkv, w_o, b_o, w_gate, w1, b1, w2, b2):
        import jax, jax.numpy as jnp
        import numpy as np
        from jax import lax
        N_HEADS = 16
        TOP_K = 2
        N_EXPERTS = 8

        def layer_norm(x, w, b, eps=1e-05):
            mu = jnp.mean(x, axis=-1, keepdims=True)
            var = jnp.mean(jnp.square(x - mu), axis=-1, keepdims=True)
            return (x - mu) * lax.rsqrt(var + eps) * w + b

        def attention(x, w_qkv, b_qkv, w_o, b_o):
            B, T, D = x.shape
            dh = D // N_HEADS
            qkv = x @ w_qkv + b_qkv
            q, k, v = jnp.split(qkv, 3, axis=-1)
            q = q.reshape(B, T, N_HEADS, dh)
            k = k.reshape(B, T, N_HEADS, dh)
            v = v.reshape(B, T, N_HEADS, dh)
            scores = jnp.einsum('bqhd,bkhd->bhqk', q, k) / jnp.sqrt(jnp.float32(dh)).astype(x.dtype)
            probs = jax.nn.softmax(scores, axis=-1)
            ctx = jnp.einsum('bhqk,bkhd->bqhd', probs, v).reshape(B, T, D)
            return ctx @ w_o + b_o

        def moe_ff(x, w_gate, w1, b1, w2, b2):
            B, T, D = x.shape
            t = x.reshape(B * T, D)
            probs = jax.nn.softmax(t @ w_gate, axis=-1)
            tw, ti = lax.top_k(probs, TOP_K)
            tw = tw / jnp.sum(tw, axis=-1, keepdims=True)
            out = jnp.zeros_like(t)
            for e in range(N_EXPERTS):
                we = jnp.sum(jnp.where(ti == e, tw, 0.0), axis=-1)
                h = jax.nn.gelu(t @ w1[e] + b1[e]) @ w2[e] + b2[e]
                out = out + we[:, None] * h
            return out.reshape(B, T, D)
        h = x + attention(layer_norm(x, ln1_w, ln1_b), w_qkv, b_qkv, w_o, b_o)
        return h + moe_ff(layer_norm(h, ln2_w, ln2_b), w_gate, w1, b1, w2, b2)
    x = x + _L0_attn_ref(_layernorm(x, axis=-1), L0_attn_Wq, L0_attn_Wk, L0_attn_Wv, L0_attn_Wo, L0_attn_bo, L0_attn_Aq, L0_attn_Bq, L0_attn_Ak, L0_attn_Bk, L0_attn_Av, L0_attn_Bv, L0_attn_Ao, L0_attn_Bo)
    x = x + _L0_xattn_ref(_layernorm(x, axis=-1), ctx_1024, ctx_1024, L0_xattn_wq, L0_xattn_bq, L0_xattn_wk, L0_xattn_bk, L0_xattn_wv, L0_xattn_bv, L0_xattn_wo, L0_xattn_bo)
    x = x + _L0_ffn_ref(_layernorm(x, axis=-1), L0_ffn_phi_w, L0_ffn_phi_b, L0_ffn_expert_w, L0_ffn_expert_b)
    x = x + _L1_attn_ref(_layernorm(x, axis=-1), L1_attn_Wq, L1_attn_Wk, L1_attn_Wv, L1_attn_conv_q, L1_attn_conv_k, L1_attn_conv_v, L1_attn_W_init, L1_attn_ln_gamma, L1_attn_ln_beta, L1_attn_Wg, L1_attn_Wo)
    x = x + _L1_xattn_ref(_layernorm(x, axis=-1), ctx_1024, ctx_1024, L1_xattn_Wq, L1_xattn_bq, L1_xattn_Wk, L1_xattn_bk, L1_xattn_Wv, L1_xattn_bv, L1_xattn_Wf, L1_xattn_bf)
    x = x + _L1_ffn_ref(_layernorm(x, axis=-1), L1_ffn_weight, L1_ffn_bias)
    x = x + _L2_attn_ref(_layernorm(x, axis=-1), L2_attn_w_qkv, L2_attn_w_out)
    x = x + _L2_xattn_ref(_layernorm(x, axis=-1), ctx_1024, ctx_1024, L2_xattn_Wq, L2_xattn_bq, L2_xattn_Wk, L2_xattn_bk, L2_xattn_Wv, L2_xattn_bv, L2_xattn_Wo, L2_xattn_bo)
    x = x + _L2_ffn_ref(_layernorm(x, axis=-1), L2_ffn_router_w, L2_ffn_router_bias, L2_ffn_gate_w, L2_ffn_up_w, L2_ffn_down_w, L2_ffn_sgate_w, L2_ffn_sup_w, L2_ffn_sdown_w)
    x = x + _L3_attn_ref(_layernorm(x, axis=-1), L3_attn_w_q, L3_attn_w_k, L3_attn_w_v, L3_attn_w_o)
    x = x + _L3_xattn_ref(_layernorm(x, axis=-1), ctx_1024, ctx_1024, L3_xattn_Wi_w, L3_xattn_Wi_b, L3_xattn_Wf_w, L3_xattn_Wf_b, L3_xattn_gn_w, L3_xattn_gn_b)
    x = x + _L3_ffn_ref(_layernorm(x, axis=-1), L3_ffn_ln1_w, L3_ffn_ln1_b, L3_ffn_ln2_w, L3_ffn_ln2_b, L3_ffn_w_qkv, L3_ffn_b_qkv, L3_ffn_w_o, L3_ffn_b_o, L3_ffn_w_gate, L3_ffn_w1, L3_ffn_b1, L3_ffn_w2, L3_ffn_b2)
    return x

_drawn_inputs = setup_inputs


def setup_inputs(seed=0):
    import zlib

    import numpy as np

    out = dict(_drawn_inputs(seed))
    spreads = {'L0_attn_bo': (0.0, 0.1),
     'L0_xattn_bq': (0.0, 0.1),
     'L0_xattn_bk': (0.0, 0.1),
     'L0_xattn_bv': (0.0, 0.1),
     'L0_xattn_bo': (0.0, 0.1),
     'L1_attn_ln_gamma': (1.0, 0.2),
     'L1_attn_ln_beta': (0.0, 0.1),
     'L1_xattn_bq': (0.0, 0.396),
     'L1_xattn_bk': (0.0, 2.0),
     'L1_xattn_bv': (0.0, 0.1),
     'L1_xattn_bf': (0.0, 0.1),
     'L2_xattn_bq': (0.0, 0.289),
     'L2_xattn_bk': (0.0, 2.0),
     'L2_xattn_bv': (0.0, 0.1),
     'L2_xattn_bo': (0.0, 0.1),
     'L2_ffn_router_bias': (0.0, 0.1),
     'L3_xattn_Wi_w': (0.0, 0.1),
     'L3_xattn_Wf_w': (0.0, 0.1),
     'L3_xattn_gn_w': (1.0, 0.2),
     'L3_xattn_gn_b': (0.0, 0.1),
     'L3_ffn_ln1_w': (1.0, 0.2),
     'L3_ffn_ln1_b': (0.0, 0.1),
     'L3_ffn_ln2_w': (1.0, 0.2),
     'L3_ffn_ln2_b': (0.0, 0.1),
     'L3_ffn_b_qkv': (0.0, 0.1),
     'L3_ffn_b_o': (0.0, 0.1),
     'L3_ffn_b1': (0.0, 0.562),
     'L3_ffn_b2': (0.0, 0.384)}
    factors = {'L0_attn_Aq': 4.1,
     'L0_attn_Bq': 4.088,
     'L0_attn_Ak': 3.92,
     'L0_attn_Bk': 3.779,
     'L0_attn_Av': 3.677,
     'L0_attn_Bv': 3.663,
     'L0_attn_Ao': 3.996,
     'L0_attn_Bo': 3.956,
     'L0_ffn_phi_b': 5.31,
     'L3_attn_w_q': 8.0,
     'L3_attn_w_k': 8.0,
     'L3_xattn_Wi_b': 64.0}
    for name, (base, spread) in spreads.items():
        noise = np.random.default_rng([zlib.crc32(name.encode()), seed]).standard_normal(out[name].shape)
        drawn = base * np.exp(spread * noise) if base else spread * noise
        out[name] = jnp.asarray(drawn.astype(out[name].dtype))
    for name, factor in factors.items():
        out[name] = (out[name] * factor).astype(out[name].dtype)
    return out
```

```python
from contextlib import ExitStack

import numpy as np

import concourse.bass as bass
from concourse import mybir

F32 = mybir.dt.float32
ALU = mybir.AluOpType
ACT = mybir.ActivationFunctionType
AXX = mybir.AxisListType.X

P = 128
NB = 32
DM = 128
LN_EPS = 1e-5
NEG = -1.0e30
PAIRS = (NB - 2) // 2



def shift(b, d):
    return b + d if isinstance(b, int) else (b[0], b[1] + d)


def count(b, per, off):
    if isinstance(b, int):
        return per * b + off
    return b[0] * (2 * per) + (per * b[1] + off)


def count_own(b, per, off):
    if isinstance(b, int):
        return per * (b // 2) + off
    return b[0] * per + (per * (b[1] // 2) + off)


def wait(eng, sem, value):
    if isinstance(value, int) and value <= 0:
        return
    eng.wait_ge(sem, value)


def settle(eng, pad):
    eng.sem_inc(pad, 1)


def tile_of(t, b, width=DM):
    if isinstance(b, int):
        return t[:, b * width:(b + 1) * width]
    return t[:, bass.ts(b[0] * 2 + b[1], width)]


def dram_of(t, b):
    if isinstance(b, int):
        return t[b]
    return t[bass.ds(b[0] * 2 + b[1], 1)].rearrange("a p n -> (a p) n")


def pipeline(eng, step):
    step(0, 0, False, True, True)
    with eng.Fori(0, PAIRS) as i:
        step((i, 1), 1, True, True, True)
        step((i, 2), 0, True, True, True)
    step(NB - 1, 1, True, True, False)
    step(NB, 0, True, False, False)


class Sems:

    def __init__(self, nc, ctx, n):
        self.nc = nc
        self.pool = [ctx.enter_context(nc.semaphore(f"stage_sem_{i}")) for i in range(n)]
        self.used = 0

    def __call__(self, n):
        got = self.pool[self.used:self.used + n]
        assert len(got) == n
        self.used += n
        return got

    def clear(self):
        for s in self.pool[:self.used]:
            self.nc.gpsimd.sem_clear(s)
        self.used = 0
        self.nc.all_engine_barrier()


def bcast_mid(ap2, n):
    return ap2.unsqueeze(1).to_broadcast([ap2.shape[0], n, ap2.shape[1]])


def bcast_in(ap2, n):
    return ap2.unsqueeze(2).to_broadcast([ap2.shape[0], ap2.shape[1], n])


def row_bcast(dram, n):
    return dram.rearrange("(a n) -> a n", a=1).to_broadcast([P, n])


def col(dram):
    return dram.rearrange("(p a) -> p a", a=1)


def each(eng, f):
    f(0, 0)
    with eng.Fori(0, PAIRS) as i:
        f((i, 1), 1)
        f((i, 2), 0)
    f(NB - 1, 1)


def dram_mid(t, b):
    if isinstance(b, int):
        return t[:, b, :]
    return t[:, bass.ds(b[0] * 2 + b[1], 1), :].rearrange("p a n -> p (a n)")


def small_head_attention(nc, C, sems, tag, *, src, dests, wq, wk, wv, wo4, scale,
                         ctx_dram=None, q_bias=None, k_bias=None, out_bias=None, affine=None,
                         permuted=None):
    with ExitStack() as x:
        sb = lambda n, shape: x.enter_context(nc.sbuf_tensor(f"{tag}_{n}", shape, F32))
        ps = lambda n: x.enter_context(nc.psum_tensor(f"{tag}_{n}", [P, 512], F32))
        stat = sb("stat", [P, 2, 6])
        mv = sb("mv", [P, 2, 2])
        ve = sb("ve", [P, 2, 2])
        xn = sb("xn", [P, 2, DM])
        xnT = sb("xnT", [P, 2, P])
        ctxT = sb("ctxT", [P, 2, P])
        qkv = sb("qkv", [P, 2, 3 * P])
        Kexp = sb("Kexp", [P, 2, 16, P])
        mx = sb("mx", [P, 2, 4])
        Sx = sb("Sx", [P, 2, 4, P])
        Pr = sb("Pr", [P, 2, 4, P])
        PT = sb("PT", [P, 2, 16, P])
        rd = sb("rd", [P, 512])
        on = sb("on", [P, 4, P])
        qin = sb("qin", [P, 2, P])
        osb = sb("osb", [P, 2, P])
        A = ps("A")
        S = [ps("S0"), ps("S1")]
        TP = [ps("TP0"), ps("TP1")]
        NUM, DEN, O = ps("NUM"), ps("DEN"), ps("O")
        (pad, stats_done, stat_done, ve_done, rstd_done, xn_done, xnt_mm, xnt_done, ctx_in0, ctx_in1, qkv_mm,
         qkv_done, kexp_done, s_mm, max_done, sub_done, exp_done, tp_mm, pt_done, pv_mm, rd_done,
         on_done, out_mm, x_done, stored) = sems(25)
        ctx_in = [ctx_in0, ctx_in1]

        with nc.Block() as block:

            @block.sync
            def _(sp):
                def load_ctx(b, s):
                    wait(sp, qkv_mm, count(b, 1, -1))
                    sp.dma_start(ctxT[:, s, :], dram_of(ctx_dram, b)).then_inc(ctx_in[s], 16)
                    if permuted is not None:
                        wait(sp, pv_mm, count(b, 1, -1))
                        sp.dma_start(qin[:, s, :], dram_mid(permuted[0], b)).then_inc(ctx_in[s], 16)
                        sp.dma_start(qkv[:, s, 2 * P:3 * P], dram_mid(permuted[1], b)).then_inc(ctx_in[s], 16)

                def store(b, s):
                    wait(sp, x_done, count(b, 1, 1))
                    sp.dma_start(dram_mid(permuted[2], b), osb[:, s, :]).then_inc(stored, 16)

                def step(b, s, tail, head, front):
                    if front:
                        load_ctx(shift(b, 1), 1 - s)
                    if tail and permuted is not None:
                        store(shift(b, -1), 1 - s)
                if ctx_dram is not None:
                    load_ctx(0, 0)
                    pipeline(sp, step)
                if permuted is not None:
                    wait(sp, stored, 16 * NB)

            @block.gpsimd
            def _(pool):
                def rstd(b, s):
                    wait(pool, stat_done, count(b, 1, 1))
                    pool.tensor_tensor(ve[:, s, 0:1], mv[:, s, 1:2], C.eps, ALU.add).then_inc(ve_done, 1)
                    wait(pool, ve_done, count(b, 1, 1))
                    pool.tensor_tensor(ve[:, s, 1:2], ve[:, s, 0:1], C.neghalf, ALU.pow).then_inc(rstd_done, 1)

                def spread(b, s):
                    wait(pool, s_mm, count(b, 4, -4))
                    wait(pool, qkv_done, count(b, 1, 1))
                    pool.tensor_tensor(Kexp[:, s, :, :], bcast_mid(qkv[:, s, P:2 * P], 16),
                                       bcast_in(C.hmask, P), ALU.mult).then_inc(kexp_done, 1)

                def step(b, s, tail, head, front):
                    if front:
                        if permuted is None:
                            rstd(shift(b, 1), 1 - s)
                        spread(shift(b, 1), 1 - s)
                if permuted is None:
                    rstd(0, 0)
                spread(0, 0)
                pipeline(pool, step)

            @block.tensor
            def _(pe):
                def normed_T(b, s):
                    if permuted is not None:
                        return
                    wait(pe, qkv_done, count(b, 1, 0))
                    wait(pe, xn_done, count(b, 1, 1))
                    nc.tensor.transpose(A[:, 0:P], xn[:, s, :], C.ident).then_inc(xnt_mm, 1)

                def project(b, s):
                    if permuted is not None:
                        wait(pe, qkv_done, count(b, 1, 0))
                        wait(pe, ctx_in[s], count_own(b, 48, 48))
                        nc.tensor.transpose(A[:, P:2 * P], qin[:, s, :], C.ident)
                        nc.tensor.matmul(A[:, 2 * P:3 * P], C.ones[0:1, :], k_bias, start=True, stop=False)
                        nc.tensor.matmul(A[:, 2 * P:3 * P], ctxT[:, s, :], wk, start=False,
                                         stop=True).then_inc(qkv_mm, 1)
                        return
                    if ctx_dram is not None:
                        wait(pe, ctx_in[s], count_own(b, 16, 16))
                    wait(pe, xnt_done, count(b, 1, 1))
                    kv = xnT[:, s, :] if ctx_dram is None else ctxT[:, s, :]
                    nc.tensor.matmul(A[:, P:2 * P], wq, xnT[:, s, :], start=True, stop=True)
                    nc.tensor.matmul(A[:, 2 * P:3 * P], wk, kv, start=True, stop=True)
                    nc.tensor.matmul(A[:, 3 * P:4 * P], kv, wv, start=True, stop=True).then_inc(qkv_mm, 1)

                def scores(b, s, q):
                    if q == 0:
                        wait(pe, kexp_done, count(b, 1, 1))
                    wait(pe, sub_done, count(b, 4, q - 1))
                    nc.tensor.matmul(S[q % 2][:, :], qkv[:, s, 0:P],
                                     Kexp[:, s, 4 * q:4 * q + 4, :].rearrange("p h k -> p (h k)"),
                                     start=True, stop=True).then_inc(s_mm, 1)

                def turn(b, q):
                    wait(pe, pt_done, count(b, 4, q - 1))
                    wait(pe, exp_done, count(b, 4, q + 1))
                    for h in range(4):
                        mm = nc.tensor.transpose(TP[q % 2][:, h * P:(h + 1) * P], Pr[:, q % 2, h, :], C.ident)
                    mm.then_inc(tp_mm, 1)

                def sum_keys(b, s):
                    wait(pe, on_done, count(b, 1, 0))
                    wait(pe, pt_done, count(b, 4, 4))
                    for q in range(4):
                        mm = nc.tensor.matmul(NUM[32 * q:32 * q + 32, :], qkv[:, s, 2 * P + 32 * q:2 * P + 32 * q + 32],
                                              PT[:, s, 4 * q:4 * q + 4, :].rearrange("p h k -> p (h k)"),
                                              start=True, stop=True)
                    for q in range(4):
                        mm = nc.tensor.matmul(DEN[32 * q:32 * q + 32, :], C.ones[:, 0:32],
                                              PT[:, s, 4 * q:4 * q + 4, :].rearrange("p h k -> p (h k)"),
                                              start=True, stop=True)
                    mm.then_inc(pv_mm, 1)

                def project_out(b):
                    wait(pe, x_done, count(b, 1, 0))
                    wait(pe, on_done, count(b, 1, 1))
                    if out_bias is not None:
                        nc.tensor.matmul(O[:, 0:DM], C.ones[0:1, :], out_bias, start=True, stop=False)
                    for j in range(4):
                        mm = nc.tensor.matmul(O[:, 0:DM], on[:, j, :], wo4[:, j, :],
                                              start=(j == 0 and out_bias is None), stop=(j == 3))
                    mm.then_inc(out_mm, 1)

                def step(b, s, tail, head, front):
                    prev, nxt = shift(b, -1), shift(b, 1)
                    if head:
                        scores(b, s, 0)
                    if tail:
                        turn(prev, 3)
                    if head:
                        scores(b, s, 1)
                        turn(b, 0)
                    if front:
                        normed_T(nxt, 1 - s)
                    if tail:
                        sum_keys(prev, 1 - s)
                    if head:
                        scores(b, s, 2)
                        turn(b, 1)
                    if front:
                        project(nxt, 1 - s)
                    if head:
                        scores(b, s, 3)
                        turn(b, 2)
                    if tail:
                        project_out(prev)
                normed_T(0, 0)
                project(0, 0)
                pipeline(pe, step)

            @block.vector
            def _(dve):
                def stats(b, s):
                    if permuted is not None:
                        return
                    nc.vector.bn_stats(stat[:, s, :], tile_of(src, b)).then_inc(stats_done, 1)
                    wait(dve, stats_done, count(b, 1, 1))
                    settle(dve, pad)
                    nc.vector.bn_aggr(mv[:, s, :], stat[:, s, :]).then_inc(stat_done, 1)

                def normed(b, s):
                    if permuted is not None:
                        return
                    wait(dve, xnt_mm, count(b, 1, -1))
                    wait(dve, rstd_done, count(b, 1, 1))
                    nc.vector.tensor_scalar(xn[:, s, :], tile_of(src, b), mv[:, s, 0:1], ve[:, s, 1:2],
                                            ALU.subtract, ALU.mult).then_inc(xn_done, 1)

                def less_max(b, q):
                    wait(dve, s_mm, count(b, 4, q + 1))
                    sc = S[q % 2][:, :].rearrange("p (h k) -> p h k", h=4)
                    nc.vector.tensor_reduce(mx[:, q % 2, :], sc, AXX, ALU.max).then_inc(max_done, 1)
                    wait(dve, exp_done, count(b, 4, q - 1))
                    wait(dve, max_done, count(b, 4, q + 1))
                    nc.vector.tensor_tensor(Sx[:, q % 2, :, :], sc, bcast_in(mx[:, q % 2, :], P),
                                            ALU.subtract).then_inc(sub_done, 1)

                def divide(b):
                    wait(dve, pv_mm, count(b, 1, 1))
                    nc.vector.reciprocal(rd[:, :], DEN[:, :]).then_inc(rd_done, 1)
                    wait(dve, out_mm, count(b, 1, 0))
                    wait(dve, rd_done, count(b, 1, 1))
                    nc.vector.tensor_tensor(on[:, :, :].rearrange("p j q -> p (j q)"), NUM[:, :], rd[:, :],
                                            ALU.mult).then_inc(on_done, 1)

                def add(b, s):
                    wait(dve, out_mm, count(b, 1, 1))
                    if permuted is not None:
                        wait(dve, stored, count(b, 16, 0))
                        nc.vector.tensor_copy(osb[:, s, :], O[:, 0:DM]).then_inc(x_done, 1)
                        return
                    for d in dests:
                        ins = nc.vector.tensor_tensor(tile_of(d, b), tile_of(d, b), O[:, 0:DM], ALU.add)
                    ins.then_inc(x_done, 1)

                def step(b, s, tail, head, front):
                    prev, nxt = shift(b, -1), shift(b, 1)
                    if front:
                        stats(nxt, 1 - s)
                    if head:
                        less_max(b, 0)
                    if front:
                        normed(nxt, 1 - s)
                    if head:
                        less_max(b, 1)
                        less_max(b, 2)
                    if tail:
                        divide(prev)
                    if head:
                        less_max(b, 3)
                    if tail:
                        add(prev, 1 - s)
                stats(0, 0)
                normed(0, 0)
                pipeline(dve, step)

            @block.scalar
            def _(act):
                def copy_normed(b, s):
                    if permuted is not None:
                        return
                    wait(act, qkv_mm, count(b, 1, -1))
                    wait(act, xnt_mm, count(b, 1, 1))
                    if affine is None:
                        nc.scalar.copy(xnT[:, s, :], A[:, 0:P]).then_inc(xnt_done, 1)
                    else:
                        nc.scalar.activation(xnT[:, s, :], A[:, 0:P], ACT.Identity, bias=affine[1],
                                             scale=affine[0]).then_inc(xnt_done, 1)

                def copy_qkv(b, s):
                    wait(act, pv_mm, count(b, 1, -1))
                    wait(act, kexp_done, count(b, 1, -1))
                    wait(act, s_mm, count(b, 4, -4))
                    wait(act, qkv_mm, count(b, 1, 1))
                    if permuted is not None:
                        nc.scalar.copy(qkv[:, s, 0:2 * P], A[:, P:3 * P]).then_inc(qkv_done, 1)
                    elif q_bias is None:
                        nc.scalar.copy(qkv[:, s, :], A[:, P:4 * P]).then_inc(qkv_done, 1)
                    else:
                        nc.scalar.activation(qkv[:, s, 0:P], A[:, P:2 * P], ACT.Identity, bias=q_bias)
                        nc.scalar.activation(qkv[:, s, P:2 * P], A[:, 2 * P:3 * P], ACT.Identity, bias=k_bias)
                        nc.scalar.copy(qkv[:, s, 2 * P:3 * P], A[:, 3 * P:4 * P]).then_inc(qkv_done, 1)

                def exps(b, q):
                    wait(act, tp_mm, count(b, 4, q - 1))
                    wait(act, sub_done, count(b, 4, q + 1))
                    nc.scalar.activation(Pr[:, q % 2, :, :], Sx[:, q % 2, :, :], ACT.Exp,
                                         scale=scale).then_inc(exp_done, 1)

                def copy_turned(b, s, q):
                    if q == 0:
                        wait(act, pv_mm, count(b, 1, -1))
                    wait(act, tp_mm, count(b, 4, q + 1))
                    nc.scalar.copy(PT[:, s, 4 * q:4 * q + 4, :].rearrange("p h k -> p (h k)"),
                                   TP[q % 2][:, :]).then_inc(pt_done, 1)

                def step(b, s, tail, head, front):
                    prev, nxt = shift(b, -1), shift(b, 1)
                    if tail:
                        copy_turned(prev, 1 - s, 3)
                    if head:
                        exps(b, 0)
                        exps(b, 1)
                        copy_turned(b, s, 0)
                    if front:
                        copy_normed(nxt, 1 - s)
                    if head:
                        exps(b, 2)
                        copy_turned(b, s, 1)
                    if front:
                        copy_qkv(nxt, 1 - s)
                    if head:
                        exps(b, 3)
                        copy_turned(b, s, 2)
                copy_normed(0, 0)
                copy_qkv(0, 0)
                pipeline(act, step)
        sems.clear()


class Consts:

    PARTS = {"ident": P, "hmask": 16, "jmask": 4, "ones": P, "eps": 1, "neghalf": 1,
             "tri": P, "causal": P, "l2eps": 1, "hmask16": 8}

    def __init__(self, nc, ctx):
        self.tile = ctx.enter_context(nc.sbuf_tensor("const_tile", [P, sum(self.PARTS.values())], F32))
        starts = dict(zip(self.PARTS, np.cumsum([0] + list(self.PARTS.values()))))
        part = lambda name: self.tile[:, int(starts[name]):int(starts[name]) + self.PARTS[name]]
        self.ident, self.hmask, self.jmask, self.ones = part("ident"), part("hmask"), part("jmask"), part("ones")
        self.eps, self.neghalf, self.l2eps = part("eps"), part("neghalf"), part("l2eps")
        self.hmask16 = part("hmask16")
        self.tri, self.causal = part("tri"), part("causal")

    @classmethod
    def values(cls):
        p = np.arange(P)
        parts = {
            "ident": np.eye(P),
            "hmask": p[:, None] // 8 == np.arange(16)[None],
            "jmask": (p[:, None] % 32) // 8 == np.arange(4)[None],
            "ones": np.ones((P, P)),
            "eps": np.full((P, 1), LN_EPS),
            "neghalf": np.full((P, 1), -0.5),
            "tri": p[:, None] <= p[None],
            "causal": np.where(p[:, None] >= p[None], 0.0, NEG),
            "l2eps": np.full((P, 1), 1e-12),
            "hmask16": 0.25 * (p[:, None] // 16 == np.arange(8)[None]),
        }
        return np.concatenate([parts[n] for n in cls.PARTS], axis=1).astype(np.float32)


class LayerNorm:

    def __init__(self, nc, sb):
        self.stat = sb("ln_stat", [P, 2, 6])
        self.mv = sb("ln_mv", [P, 2, 2])
        self.ve = sb("ln_ve", [P, 2, 2])
        self.xn = sb("ln_xn", [P, 2, DM])

    def sems(self, sems):
        (self.pad, self.stats, self.moments, self.var_eps, self.rstd_done, self.done) = sems(6)

    def rstd(self, pool, b, s, C):
        wait(pool, self.moments, count(b, 1, 1))
        pool.tensor_tensor(self.ve[:, s, 0:1], self.mv[:, s, 1:2], C.eps, ALU.add).then_inc(self.var_eps, 1)
        wait(pool, self.var_eps, count(b, 1, 1))
        pool.tensor_tensor(self.ve[:, s, 1:2], self.ve[:, s, 0:1], C.neghalf, ALU.pow).then_inc(self.rstd_done, 1)

    def moments_of(self, nc, dve, b, s, src):
        nc.vector.bn_stats(self.stat[:, s, :], tile_of(src, b)).then_inc(self.stats, 1)
        wait(dve, self.stats, count(b, 1, 1))
        settle(dve, self.pad)
        nc.vector.bn_aggr(self.mv[:, s, :], self.stat[:, s, :]).then_inc(self.moments, 1)

    def scale(self, nc, dve, b, s, src, reader):
        wait(dve, reader, count(b, 1, -1))
        wait(dve, self.rstd_done, count(b, 1, 1))
        nc.vector.tensor_scalar(self.xn[:, s, :], tile_of(src, b), self.mv[:, s, 0:1], self.ve[:, s, 1:2],
                                ALU.subtract, ALU.mult).then_inc(self.done, 1)

    def normalise(self, nc, dve, b, s, src, reader):
        self.moments_of(nc, dve, b, s, src)
        self.scale(nc, dve, b, s, src, reader)


def masked_out_weights(eng, wo4, woT, C, done):
    eng.tensor_tensor(wo4[:, :, :], bcast_mid(woT, 4), bcast_in(C.jmask, P), ALU.mult).then_inc(done, 1)


def stage_l0_attn(nc, C, sems, d, X):
    with ExitStack() as x:
        sb = lambda n, shape: x.enter_context(nc.sbuf_tensor(f"l0a_{n}", shape, F32))
        w = sb("w", [P, 4, DM])
        la = sb("la", [16, 4, DM])
        lb = sb("lb", [16, 4, DM])
        bo = sb("bo", [1, DM])
        wo4 = sb("wo4", [P, 4, DM])
        with nc.psum_tensor("l0a_fold", [P, 512], F32) as fold, nc.Block() as block:
            w_in, fold_mm, w_done, wo_done = sems(4)

            @block.sync
            def _(sp):
                sp.dma_start(w[:, :, :], d["l0a_w"]).then_inc(w_in, 16)
                sp.dma_start(la[:, :, :], d["l0a_a"]).then_inc(w_in, 16)
                sp.dma_start(lb[:, :, :], d["l0a_b"]).then_inc(w_in, 16)
                sp.dma_start(bo[:, :], d["l0a_bo"]).then_inc(w_in, 16)

            @block.tensor
            def _(pe):
                pe.wait_ge(w_in, 64)
                for n in range(4):
                    mm = nc.tensor.matmul(fold[:, n * DM:(n + 1) * DM], la[:, n, :], lb[:, n, :],
                                          start=True, stop=True)
                mm.then_inc(fold_mm, 1)

            @block.vector
            def _(dve):
                dve.wait_ge(fold_mm, 1)
                nc.vector.scalar_tensor_tensor(w[:, :, :].rearrange("p n c -> p (n c)"), fold[:, :], 1.0 / 16,
                                               w[:, :, :].rearrange("p n c -> p (n c)"),
                                               ALU.mult, ALU.add).then_inc(w_done, 1)
                dve.wait_ge(w_done, 1)
                masked_out_weights(dve, wo4, w[:, 3, :], C, wo_done)
        sems.clear()
        small_head_attention(nc, C, sems, "l0a", src=X, dests=[X], wq=w[:, 0, :], wk=w[:, 1, :], wv=w[:, 2, :],
                             wo4=wo4, scale=8 ** -0.5, out_bias=bo[0:1, :])


def regroup(eng, per, nat, done, back=False):
    n = nat.rearrange("b (h r) (c j) -> r c (b h) j", r=8, c=16)
    p = per.rearrange("(r c) b (h j) -> r c (b h) j", r=8, h=16)
    for r in range(8):
        dst, src = (n, p) if back else (p, n)
        eng.dma_start(dst[r], src[r]).then_inc(done, 16)


def stage_l0_xattn(nc, C, sems, d, X):
    dram = lambda n, *shape: nc.dram_tensor(f"l0x_dram_{n}", shape, F32, kind="Internal").ap()
    q_nat, v_nat, o_nat = [dram(n, NB, P, DM) for n in ("qn", "vn", "on")]
    q_per, v_per, o_per = [dram(n, P, NB, DM) for n in ("qp", "vp", "op")]
    with ExitStack() as x:
        sb = lambda n, shape: x.enter_context(nc.sbuf_tensor(f"l0x_{n}", shape, F32))
        w = sb("w", [P, 4, DM])
        rows = sb("rows", [1, 4, DM])
        id4 = sb("id4", [P, 4, DM])
        with ExitStack() as y:
            sy = lambda n, shape: y.enter_context(nc.sbuf_tensor(f"l0x1_{n}", shape, F32))
            ln = LayerNorm(nc, sy)
            xnT = sy("xnT", [P, 2, P])
            ctxT = sy("ctxT", [P, 2, P])
            qv = sy("qv", [P, 2, 2 * P])
            T = [y.enter_context(nc.psum_tensor(f"l0x1_T{i}", [P, 512], F32)) for i in range(2)]
            Q = [y.enter_context(nc.psum_tensor(f"l0x1_Q{i}", [P, 512], F32)) for i in range(2)]
            (w_in, id_done, xnt_mm, xnt_done, ctx_in0, ctx_in1, qv_mm, qv_done, stored0, stored1, moved) = sems(11)
            ctx_in, stored = [ctx_in0, ctx_in1], [stored0, stored1]
            ln.sems(sems)
            with nc.Block() as block:
                @block.sync
                def _(sp):
                    sp.dma_start(w[:, :, :], d["l0x_w"]).then_inc(w_in, 16)
                    sp.dma_start(rows[:, :, :], d["l0x_b"]).then_inc(w_in, 16)

                    def f(b, s):
                        wait(sp, qv_mm, count(b, 1, -1))
                        sp.dma_start(ctxT[:, s, :], dram_of(d["ctxT"], b)).then_inc(ctx_in[s], 16)
                    each(sp, f)

                @block.gpsimd
                def _(pool):
                    masked_out_weights(pool, id4, C.ident, C, id_done)
                    each(pool, lambda b, s: ln.rstd(pool, b, s, C))

                @block.tensor
                def _(pe):
                    pe.wait_ge(w_in, 32)

                    def f(b, s):
                        wait(pe, xnt_done, count(b, 1, -1))
                        wait(pe, ln.done, count(b, 1, 1))
                        nc.tensor.transpose(T[s][:, 0:P], ln.xn[:, s, :], C.ident).then_inc(xnt_mm, 1)
                        wait(pe, qv_done, count(b, 1, -1))
                        wait(pe, ctx_in[s], count_own(b, 16, 16))
                        nc.tensor.matmul(Q[s][:, P:2 * P], C.ones[0:1, :], rows[:, 2, :], start=True, stop=False)
                        nc.tensor.matmul(Q[s][:, P:2 * P], ctxT[:, s, :], w[:, 2, :], start=False, stop=True)
                        wait(pe, xnt_done, count(b, 1, 1))
                        nc.tensor.matmul(Q[s][:, 0:P], C.ones[0:1, :], rows[:, 0, :], start=True, stop=False)
                        nc.tensor.matmul(Q[s][:, 0:P], xnT[:, s, :], w[:, 0, :], start=False,
                                         stop=True).then_inc(qv_mm, 1)
                    each(pe, f)

                @block.vector
                def _(dve):
                    each(dve, lambda b, s: ln.normalise(nc, dve, b, s, X, xnt_mm))

                @block.scalar
                def _(act):
                    def f(b, s):
                        wait(act, qv_mm, count(b, 1, -1))
                        wait(act, xnt_mm, count(b, 1, 1))
                        nc.scalar.copy(xnT[:, s, :], T[s][:, 0:P]).then_inc(xnt_done, 1)
                        wait(act, qv_mm, count(b, 1, 1))
                        wait(act, stored[s], count_own(b, 32, 0))
                        nc.scalar.copy(qv[:, s, :], Q[s][:, 0:2 * P]).then_inc(qv_done, 1)
                        wait(act, qv_done, count(b, 1, 1))
                        act.dma_start(dram_of(q_nat, b), qv[:, s, 0:P]).then_inc(stored[s], 16)
                        act.dma_start(dram_of(v_nat, b), qv[:, s, P:2 * P]).then_inc(stored[s], 16)
                    each(act, f)
                    for s in stored:
                        wait(act, s, 32 * NB // 2)
                    regroup(act, q_per, q_nat, moved)
                    regroup(act, v_per, v_nat, moved)
                    wait(act, moved, 2 * 8 * 16)
            sems.clear()
        small_head_attention(nc, C, sems, "l0x", src=None, dests=None, wq=None, wk=w[:, 1, :], wv=None, wo4=id4,
                             scale=8 ** -0.5, ctx_dram=d["ctxT"], k_bias=rows[:, 1, :],
                             permuted=(q_per, v_per, o_per))
        with ExitStack() as y:
            sy = lambda n, shape: y.enter_context(nc.sbuf_tensor(f"l0x2_{n}", shape, F32))
            o = sy("o", [P, 2, P])
            oT = sy("oT", [P, 2, P])
            T = [y.enter_context(nc.psum_tensor(f"l0x2_T{i}", [P, 512], F32)) for i in range(2)]
            Y = [y.enter_context(nc.psum_tensor(f"l0x2_Y{i}", [P, 512], F32)) for i in range(2)]
            moved, o_in0, o_in1, t_mm, t_done, y_mm, x_done = sems(7)
            o_in = [o_in0, o_in1]
            with nc.Block() as block:
                @block.sync
                def _(sp):
                    regroup(sp, o_per, o_nat, moved, back=True)
                    wait(sp, moved, 8 * 16)

                    def f(b, s):
                        wait(sp, t_mm, count(b, 1, -1))
                        sp.dma_start(o[:, s, :], dram_of(o_nat, b)).then_inc(o_in[s], 16)
                    each(sp, f)

                @block.tensor
                def _(pe):
                    def f(b, s):
                        wait(pe, t_done, count(b, 1, -1))
                        wait(pe, o_in[s], count_own(b, 16, 16))
                        nc.tensor.transpose(T[s][:, 0:P], o[:, s, :], C.ident).then_inc(t_mm, 1)
                        wait(pe, x_done, count(b, 1, -1))
                        wait(pe, t_done, count(b, 1, 1))
                        nc.tensor.matmul(Y[s][:, 0:P], C.ones[0:1, :], rows[:, 3, :], start=True, stop=False)
                        nc.tensor.matmul(Y[s][:, 0:P], oT[:, s, :], w[:, 3, :], start=False,
                                         stop=True).then_inc(y_mm, 1)
                    each(pe, f)

                @block.scalar
                def _(act):
                    def f(b, s):
                        wait(act, y_mm, count(b, 1, -1))
                        wait(act, t_mm, count(b, 1, 1))
                        nc.scalar.copy(oT[:, s, :], T[s][:, 0:P]).then_inc(t_done, 1)
                    each(act, f)

                @block.vector
                def _(dve):
                    def f(b, s):
                        wait(dve, y_mm, count(b, 1, 1))
                        nc.vector.tensor_tensor(tile_of(X, b), tile_of(X, b), Y[s][:, 0:P],
                                                ALU.add).then_inc(x_done, 1)
                    each(dve, f)
            sems.clear()


SLOTS = 2048
EXPERTS, PER = 64, 32


def slot_softmax(nc, C, sems, tag, X, phiT, phi_b, over, acc=None, xn_keep=None, values=None):
    with ExitStack() as x:
        sb = lambda n, shape: x.enter_context(nc.sbuf_tensor(f"{tag}_{n}", shape, F32))
        ps = lambda n: x.enter_context(nc.psum_tensor(f"{tag}_{n}", [P, 512], F32))
        ln = LayerNorm(nc, sb)
        xnT = sb("xnT", [P, 2, P])
        Z = sb("Z", [P, 2, SLOTS])
        groups = EXPERTS if over == "slots" else PER
        mx = sb("mx", [P, 2, groups])
        sm = sb("sm", [P, 2, groups])
        T = ps("T")
        L = [ps("L0"), ps("L1")]
        if values is not None:
            CT = sb("CT", [P, 2, SLOTS])
            TP = [ps("TP0"), ps("TP1")]
            Y = ps("Y")
        (xnt_mm, xnt_done, l_mm, add_done, max_done, sub_done, exp_done, sum_done, inv_done, w_done, tail_mm,
         tp_mm, ct_done, x_done, zero_mm) = sems(15)
        ln.sems(sems)

        def grouped(s):
            z = Z[:, s, :]
            if over == "slots":
                return z.rearrange("p (g m) -> p g m", m=PER)
            return z.rearrange("p (m g) -> p g m", g=PER)

        def spread(v):
            return bcast_in(v, PER) if over == "slots" else bcast_mid(v, EXPERTS)

        def columns(s):
            return Z[:, s, :].rearrange("p (a m) -> p a m", m=PER)

        with nc.Block() as block:

            @block.gpsimd
            def _(pool):
                def subtract(b, s):
                    wait(pool, max_done, count(b, 1, 1))
                    pool.tensor_tensor(columns(s), columns(s), spread(mx[:, s, :]), ALU.subtract).then_inc(sub_done, 1)

                def normalise(b, s):
                    wait(pool, inv_done, count(b, 1, 1))
                    pool.tensor_tensor(columns(s), columns(s), spread(sm[:, s, :]), ALU.mult).then_inc(w_done, 1)

                def step(b, s, tail, head, front):
                    if tail:
                        normalise(shift(b, -1), 1 - s)
                    if front:
                        ln.rstd(pool, shift(b, 1), 1 - s, C)
                    if head:
                        subtract(b, s)
                ln.rstd(pool, 0, 0, C)
                pipeline(pool, step)

            @block.tensor
            def _(pe):
                def normed_T(b, s):
                    wait(pe, xnt_done, count(b, 1, 0))
                    wait(pe, ln.done, count(b, 1, 1))
                    nc.tensor.transpose(T[:, 0:P], ln.xn[:, s, :], C.ident).then_inc(xnt_mm, 1)

                def logits(b, s):
                    wait(pe, xnt_done, count(b, 1, 1))
                    for q in range(4):
                        wait(pe, add_done, count(b, 4, q - 1))
                        nc.tensor.matmul(L[q % 2][:, :], xnT[:, s, :], phiT[:, q * 512:(q + 1) * 512],
                                         start=True, stop=True).then_inc(l_mm, 1)

                def dispatch(b, s):
                    wait(pe, w_done, count(b, 1, 1))
                    for k in range(16):
                        mm = nc.tensor.matmul(acc[k // 4][:, (k % 4) * P:(k % 4 + 1) * P], Z[:, s, k * P:(k + 1) * P],
                                              ln.xn[:, s, :], start=False, stop=False, skip_group_check=True)
                    mm.then_inc(tail_mm, 1)

                def combine(b, s):
                    wait(pe, w_done, count(b, 1, 1))
                    for q in range(5):
                        if q < 4:
                            wait(pe, ct_done, count(b, 4, max(q - 1, 0)))
                            for k in range(4):
                                mm = nc.tensor.transpose(TP[q % 2][:, k * P:(k + 1) * P],
                                                         Z[:, s, (4 * q + k) * P:(4 * q + k + 1) * P], C.ident)
                            mm.then_inc(tp_mm, 1)
                        if q == 1:
                            wait(pe, x_done, count(b, 1, 0))
                        if q > 0:
                            wait(pe, ct_done, count(b, 4, q))
                            for k in range(4 * q - 4, 4 * q):
                                mm = nc.tensor.matmul(Y[:, 0:DM], CT[:, s, k * P:(k + 1) * P], values[:, k, :],
                                                      start=(k == 0), stop=(k == 15))
                    mm.then_inc(tail_mm, 1)

                def step(b, s, tail, head, front):
                    if head:
                        logits(b, s)
                    if tail:
                        (dispatch if values is None else combine)(shift(b, -1), 1 - s)
                    if front:
                        normed_T(shift(b, 1), 1 - s)
                if acc is not None:
                    for k in range(4):
                        mm = nc.tensor.matmul(acc[k][:, :], xn_keep[:, 0:P], xn_keep[:, :], start=True, stop=False,
                                              skip_group_check=True)
                normed_T(0, 0)
                pipeline(pe, step)

            @block.vector
            def _(dve):
                def add_bias(b, s):
                    wait(dve, tail_mm, count(b, 1, -1))
                    for q in range(4):
                        wait(dve, l_mm, count(b, 4, q + 1))
                        part = slice(q * 512, (q + 1) * 512)
                        nc.vector.tensor_tensor(Z[:, s, part], L[q % 2][:, :], phi_b[:, part],
                                                ALU.add).then_inc(add_done, 1)
                    wait(dve, add_done, count(b, 4, 4))
                    nc.vector.tensor_reduce(mx[:, s, :], grouped(s), AXX, ALU.max).then_inc(max_done, 1)

                def sums(b, s):
                    wait(dve, exp_done, count(b, 1, 1))
                    nc.vector.tensor_reduce(sm[:, s, :], grouped(s), AXX, ALU.add).then_inc(sum_done, 1)
                    wait(dve, sum_done, count(b, 1, 1))
                    nc.vector.reciprocal(sm[:, s, :], sm[:, s, :]).then_inc(inv_done, 1)

                def add_x(b):
                    wait(dve, tail_mm, count(b, 1, 1))
                    nc.vector.tensor_tensor(tile_of(X, b), tile_of(X, b), Y[:, 0:DM], ALU.add).then_inc(x_done, 1)

                def front_(b, s):
                    wait(dve, tail_mm, count(b, 1, -1))
                    ln.scale(nc, dve, b, s, X, xnt_mm)

                def step(b, s, tail, head, front):
                    if tail:
                        sums(shift(b, -1), 1 - s)
                    if front:
                        ln.moments_of(nc, dve, shift(b, 1), 1 - s, X)
                    if head:
                        add_bias(b, s)
                    if tail and values is not None:
                        add_x(shift(b, -1))
                    if front:
                        front_(shift(b, 1), 1 - s)
                ln.moments_of(nc, dve, 0, 0, X)
                front_(0, 0)
                pipeline(dve, step)

            @block.scalar
            def _(act):
                def copy_normed(b, s):
                    wait(act, l_mm, count(b, 4, -4))
                    wait(act, xnt_mm, count(b, 1, 1))
                    nc.scalar.copy(xnT[:, s, :], T[:, 0:P]).then_inc(xnt_done, 1)

                def exps(b, s):
                    wait(act, sub_done, count(b, 1, 1))
                    nc.scalar.activation(Z[:, s, :], Z[:, s, :], ACT.Exp).then_inc(exp_done, 1)

                def copy_turned(b, s):
                    wait(act, tail_mm, count(b, 1, 0))
                    for q in range(4):
                        wait(act, tp_mm, count(b, 4, q + 1))
                        nc.scalar.copy(CT[:, s, q * 512:(q + 1) * 512], TP[q % 2][:, :]).then_inc(ct_done, 1)

                def step(b, s, tail, head, front):
                    if tail and values is not None:
                        copy_turned(shift(b, -1), 1 - s)
                    if front:
                        copy_normed(shift(b, 1), 1 - s)
                    if head:
                        exps(b, s)
                copy_normed(0, 0)
                pipeline(act, step)
        sems.clear()


def stage_l0_ffn(nc, C, sems, d, X):
    with ExitStack() as x:
        sb = lambda n, shape: x.enter_context(nc.sbuf_tensor(f"l0f_{n}", shape, F32))
        phiT = sb("phiT", [P, SLOTS])
        phi_b = sb("phi_b", [P, SLOTS])
        zero = sb("zero", [P, 512])
        val = sb("val", [P, 16, DM])
        with ExitStack() as y:
            sy = lambda n, shape: y.enter_context(nc.sbuf_tensor(f"l0f_{n}", shape, F32))
            ps = lambda n: y.enter_context(nc.psum_tensor(f"l0f_{n}", [P, 512], F32))
            acc = [ps(f"acc{k}") for k in range(4)]
            w_in, z_done = sems(2)
            with nc.Block() as block:
                @block.sync
                def _(sp):
                    sp.dma_start(phiT[:, :], d["l0f_phiT"]).then_inc(w_in, 16)
                    sp.dma_start(phi_b[:, :], row_bcast(d["l0f_phi_b"], SLOTS)).then_inc(w_in, 16)
                    sp.wait_ge(w_in, 32)

                @block.vector
                def _(dve):
                    nc.vector.memset(zero[:, :], 0.0)
            sems.clear()
            slot_softmax(nc, C, sems, "l0f_d", X, phiT, phi_b, "slots", acc=acc, xn_keep=zero)

            T = [ps("T0"), ps("T1")]
            Yp = [ps("Y0"), ps("Y1")]
            ew = sy("ew", [P, EXPERTS, DM])
            eb = sy("eb", [P, 16, DM])
            xt = sy("xt", [P, 16, DM])
            xtT = sy("xtT", [P, 16, P])
            st = sy("st", [P, 16, 6])
            mv = sy("mv", [P, 16, 2])
            r = sy("r", [P, 2, 16])
            (w_in, clip_done, st_done, mv_done, pad, ve_done, r_done, n_done, tanh_done, t_mm, t_done, y_mm,
             y_done) = sems(13)
            with nc.Block() as block:
                @block.sync
                def _(sp):
                    sp.dma_start(ew[:, :, :], d["l0f_ew"]).then_inc(w_in, 16)
                    eb_d = d["l0f_eb"].rearrange("(k a) h -> a k h", a=4)
                    for a in range(4):
                        sp.dma_start(eb[32 * a:32 * a + 32, :, :],
                                     eb_d[a:a + 1].to_broadcast([32, 16, DM])).then_inc(w_in, 16)

                @block.vector
                def _(dve):
                    for q in range(4):
                        nc.vector.tensor_scalar(xt[:, 4 * q:4 * q + 4, :].rearrange("p k n -> p (k n)"), acc[q][:, :],
                                                -33000.0, 65000.0, ALU.max, ALU.min).then_inc(clip_done, 1)
                    dve.wait_ge(clip_done, 4)
                    for k in range(16):
                        ins = nc.vector.bn_stats(st[:, k, :], xt[:, k, :])
                    ins.then_inc(st_done, 1)
                    dve.wait_ge(st_done, 1)
                    for k in range(16):
                        ins = nc.vector.bn_aggr(mv[:, k, :], st[:, k, :])
                    ins.then_inc(mv_done, 1)
                    dve.wait_ge(r_done, 1)
                    for k in range(16):
                        nc.vector.tensor_scalar(xt[:, k, :], xt[:, k, :], mv[:, k, 0:1], r[:, 1, k:k + 1],
                                                ALU.subtract, ALU.mult).then_inc(n_done, 1)
                    for q in range(4):
                        dve.wait_ge(y_mm, q + 1)
                        part = slice(4 * q, 4 * q + 4)
                        if q == 0:
                            dve.wait_ge(w_in, 80)
                        nc.vector.tensor_tensor(val[:, part, :].rearrange("p k h -> p (k h)"), Yp[q % 2][:, :],
                                                eb[:, part, :].rearrange("p k h -> p (k h)"),
                                                ALU.add).then_inc(y_done, 1)

                @block.gpsimd
                def _(pool):
                    pool.wait_ge(mv_done, 1)
                    pool.tensor_tensor(r[:, 0, :], mv[:, :, 1], C.eps.to_broadcast([P, 16]), ALU.add).then_inc(ve_done, 1)
                    pool.wait_ge(ve_done, 1)
                    pool.tensor_tensor(r[:, 1, :], r[:, 0, :], C.neghalf.to_broadcast([P, 16]),
                                       ALU.pow).then_inc(r_done, 1)

                @block.scalar
                def _(act):
                    for q in range(5):
                        if q < 4:
                            act.wait_ge(n_done, 4 * q + 4)
                            part = xt[:, 4 * q:4 * q + 4, :]
                            nc.scalar.activation(part, part, ACT.Tanh).then_inc(tanh_done, 1)
                        if q > 0:
                            act.wait_ge(t_mm, q)
                            nc.scalar.copy(xtT[:, 4 * q - 4:4 * q, :].rearrange("p k n -> p (k n)"),
                                           T[(q - 1) % 2][:, :]).then_inc(t_done, 1)

                @block.tensor
                def _(pe):
                    for q in range(5):
                        if q < 4:
                            pe.wait_ge(tanh_done, q + 1)
                            if q >= 2:
                                pe.wait_ge(t_done, q - 1)
                            for k in range(4):
                                mm = nc.tensor.transpose(T[q % 2][:, k * P:(k + 1) * P], xt[:, 4 * q + k, :], C.ident)
                            mm.then_inc(t_mm, 1)
                        if q > 0:
                            pe.wait_ge(t_done, q)
                            if q == 1:
                                pe.wait_ge(w_in, 80)
                            if q >= 3:
                                pe.wait_ge(y_done, q - 2)
                            for k in range(4):
                                for a in range(4):
                                    n = 16 * (q - 1) + 4 * k + a
                                    mm = nc.tensor.matmul(Yp[(q - 1) % 2][32 * a:32 * a + 32, k * P:(k + 1) * P],
                                                          xtT[:, n // 4, 32 * a:32 * a + 32], ew[:, n, :],
                                                          start=True, stop=True)
                            mm.then_inc(y_mm, 1)
            sems.clear()
        slot_softmax(nc, C, sems, "l0f_c", X, phiT, phi_b, "experts", values=val)


def linear_attention(nc, C, sems, tag, X, w, woT, id4, kind, w0=None, wg=None, gamma=None, beta=None):
    delta = kind == "delta"
    with ExitStack() as x:
        sb = lambda n, shape: x.enter_context(nc.sbuf_tensor(f"{tag}_{n}", shape, F32))
        ps = lambda n: x.enter_context(nc.psum_tensor(f"{tag}_{n}", [P, 512], F32))
        ln = LayerNorm(nc, sb)
        xb = sb("xb", [P, 2, 3 + P])
        raw = sb("raw", [P, 2, 3 * P])
        low = sb("low", [P, 2 * P])
        inv = sb("inv", [P, 2, 32])
        qkT = sb("qkT", [P, 2, 2 * P])
        gate = sb("gate", [P, 2, P])
        Qexp = sb("Qexp", [P, 2, 16, P])
        PT = sb("PT", [P, 2, 16, P])
        nd = sb("nd", [P, 2, 4, P])
        small = sb("small", [P, 4, 16])
        oc = sb("oc", [P, P])
        osq = sb("osq", [P, P])
        oT = sb("oT", [P, P])
        A, T, S, NUM, DEN, O, Y = ps("A"), ps("T"), [ps("S0"), ps("S1")], ps("NUM"), ps("DEN"), ps("O"), ps("Y")
        (xnt_mm, xnt_done, proj_mm, raw_done, sq_done, ssum_done, inv1_done, inv_done, unit_done, qkt_mm,
         qk_done, low_done, low_exp, qexp_done, s_mm, p_done, pv_mm, nd_done, o_mm, mean_done, oc_done,
         osq_done, var_done, r1_done, r_done, on_done, ot_mm, ot_done, y_mm, x_done, zeros_done, chain, affine) = sems(33)
        ln.sems(sems)
        heads = lambda ap: ap.rearrange("p (h n) -> p h n", n=8)

        with nc.Block() as block:

            @block.gpsimd
            def _(pool):
                def unit(b, s):
                    wait(pool, raw_done, count(b, 1, 1))
                    wait(pool, ssum_done, count(b, 1, 0))
                    pool.tensor_tensor(low[:, :], raw[:, s, 0:2 * P], raw[:, s, 0:2 * P], ALU.mult).then_inc(sq_done, 1)
                    wait(pool, ssum_done, count(b, 1, 1))
                    pool.tensor_tensor(inv[:, s, :], inv[:, s, :], C.l2eps.to_broadcast([P, 32]),
                                       ALU.add).then_inc(inv1_done, 1)
                    wait(pool, inv1_done, count(b, 1, 1))
                    pool.tensor_tensor(inv[:, s, :], inv[:, s, :], C.neghalf.to_broadcast([P, 32]),
                                       ALU.pow).then_inc(inv_done, 1)

                def spread(b, s):
                    wait(pool, s_mm, count(b, 4, -4))
                    if delta:
                        wait(pool, pv_mm, count(b, 1, -1))
                    wait(pool, qk_done, count(b, 1, 1))
                    pool.tensor_tensor(Qexp[:, s, :, :], bcast_mid(qkT[:, s, 0:P], 16), bcast_in(C.hmask, P),
                                       ALU.mult).then_inc(qexp_done, 1)

                def head_norm(b, s):
                    wait(pool, oc_done, count(b, 1, 1))
                    pool.tensor_tensor(osq[:, :], oc[:, :], oc[:, :], ALU.mult).then_inc(osq_done, 1)
                    wait(pool, var_done, count(b, 1, 1))
                    settle(pool, chain)
                    pool.tensor_scalar(small[:, 2, :], small[:, 1, :], 1.0 / 8, LN_EPS, ALU.mult,
                                       ALU.add).then_inc(r1_done, 1)
                    wait(pool, r1_done, count(b, 1, 1))
                    pool.tensor_tensor(small[:, 3, :], small[:, 2, :], C.neghalf.to_broadcast([P, 16]),
                                       ALU.pow).then_inc(r_done, 1)
                    o8 = heads(oc[:, :])
                    wait(pool, r_done, count(b, 1, 1))
                    pool.tensor_tensor(o8, o8, bcast_in(small[:, 3, :], 8), ALU.mult).then_inc(affine, 1)
                    wait(pool, affine, count(b, 3, 1))
                    pool.tensor_tensor(o8, o8, bcast_mid(gamma, 16), ALU.mult).then_inc(affine, 1)
                    wait(pool, affine, count(b, 3, 2))
                    pool.tensor_tensor(o8, o8, bcast_mid(beta, 16), ALU.add).then_inc(affine, 1)
                    wait(pool, affine, count(b, 3, 3))
                    pool.tensor_tensor(oc[:, :], oc[:, :], gate[:, s, :], ALU.mult).then_inc(on_done, 1)

                def step(b, s, tail, head, front):
                    if front:
                        ln.rstd(pool, shift(b, 1), 1 - s, C)
                    if tail and delta:
                        head_norm(shift(b, -1), 1 - s)
                    if front:
                        if delta:
                            unit(shift(b, 1), 1 - s)
                        spread(shift(b, 1), 1 - s)
                ln.rstd(pool, 0, 0, C)
                if delta:
                    unit(0, 0)
                spread(0, 0)
                pipeline(pool, step)

            @block.tensor
            def _(pe):
                def normed_T(b, s):
                    wait(pe, xnt_done, count(b, 1, 0))
                    wait(pe, qk_done, count(b, 1, 0))
                    wait(pe, ln.done, count(b, 1, 1))
                    nc.tensor.transpose(T[:, 0:P], ln.xn[:, s, :], C.ident).then_inc(xnt_mm, 1)

                def project(b, s):
                    wait(pe, raw_done, count(b, 1, 0))
                    wait(pe, xnt_done, count(b, 1, 1))
                    xT = xb[:, s, 3:3 + P]
                    if delta:
                        if isinstance(b, int) and b == 0:
                            pe.wait_ge(zeros_done, 1)
                        nc.tensor.matmul(A[:, 3 * P:4 * P], xT, wg, start=True, stop=True)
                        for j in range(4):
                            mm = nc.tensor.matmul(A[:, 0:3 * P], xb[:, s, j:j + P], w[:, j, :], start=(j == 0),
                                                  stop=(j == 3))
                    else:
                        nc.tensor.matmul(A[:, 0:P], w[:, 0:P], xT, start=True, stop=True)
                        nc.tensor.matmul(A[:, P:2 * P], w[:, P:2 * P], xT, start=True, stop=True)
                        mm = nc.tensor.matmul(A[:, 2 * P:3 * P], xT, w[:, 2 * P:3 * P], start=True, stop=True)
                    mm.then_inc(proj_mm, 1)

                def turn_qk(b, s):
                    wait(pe, unit_done, count(b, 1, 1))
                    nc.tensor.transpose(T[:, P:2 * P], raw[:, s, 0:P], C.ident)
                    nc.tensor.transpose(T[:, 2 * P:3 * P], raw[:, s, P:2 * P], C.ident).then_inc(qkt_mm, 1)

                def weights(b, s, q):
                    if q == 0:
                        wait(pe, qexp_done, count(b, 1, 1))
                    wait(pe, p_done, count(b, 4, q - 1))
                    nc.tensor.matmul(S[q % 2][:, :], qkT[:, s, P:2 * P],
                                     Qexp[:, s, 4 * q:4 * q + 4, :].rearrange("p h k -> p (h k)"),
                                     start=True, stop=True).then_inc(s_mm, 1)

                def sum_keys(b, s):
                    wait(pe, nd_done, count(b, 1, 0))
                    wait(pe, p_done, count(b, 4, 4))
                    quad = lambda t, q: t[:, s, 4 * q:4 * q + 4, :].rearrange("p h k -> p (h k)")
                    for q in range(4):
                        mm = nc.tensor.matmul(NUM[32 * q:32 * q + 32, :],
                                              raw[:, s, 2 * P + 32 * q:2 * P + 32 * q + 32],
                                              quad(PT, q), start=True, stop=not delta)
                    for q in range(4):
                        if delta:
                            mm = nc.tensor.matmul(NUM[32 * q:32 * q + 32, :], w0[:, 32 * q:32 * q + 32],
                                                  quad(Qexp, q), start=False, stop=True)
                        else:
                            mm = nc.tensor.matmul(DEN[32 * q:32 * q + 32, :], C.ones[:, 0:32], quad(PT, q),
                                                  start=True, stop=True)
                    mm.then_inc(pv_mm, 1)

                def gather_heads(b):
                    wait(pe, on_done, count(b, 1, 0))
                    wait(pe, nd_done, count(b, 1, 1))
                    for n in range(1 if delta else 2):
                        for j in range(4):
                            mm = nc.tensor.matmul(O[:, n * P:(n + 1) * P], nd[:, n, j, :], id4[:, j, :],
                                                  start=(j == 0), stop=(j == 3))
                    mm.then_inc(o_mm, 1)

                def project_out(b):
                    wait(pe, x_done, count(b, 1, 0))
                    wait(pe, on_done, count(b, 1, 1))
                    nc.tensor.transpose(Y[:, 0:P], oc[:, :], C.ident).then_inc(ot_mm, 1)
                    wait(pe, ot_done, count(b, 1, 1))
                    nc.tensor.matmul(Y[:, P:2 * P], oT[:, :], woT, start=True, stop=True).then_inc(y_mm, 1)

                def step(b, s, tail, head, front):
                    prev, nxt = shift(b, -1), shift(b, 1)
                    if head:
                        weights(b, s, 0)
                        weights(b, s, 1)
                    if tail:
                        sum_keys(prev, 1 - s)
                    if front:
                        normed_T(nxt, 1 - s)
                    if head:
                        weights(b, s, 2)
                    if tail:
                        gather_heads(prev)
                    if head:
                        weights(b, s, 3)
                    if front:
                        project(nxt, 1 - s)
                    if tail:
                        project_out(prev)
                    if front and delta:
                        turn_qk(nxt, 1 - s)
                normed_T(0, 0)
                project(0, 0)
                if delta:
                    turn_qk(0, 0)
                pipeline(pe, step)

            @block.vector
            def _(dve):
                def unit(b, s):
                    wait(dve, sq_done, count(b, 1, 1))
                    nc.vector.tensor_reduce(inv[:, s, :], heads(low[:, :]), AXX, ALU.add).then_inc(ssum_done, 1)
                    wait(dve, inv_done, count(b, 1, 1))
                    qk = heads(raw[:, s, 0:2 * P])
                    nc.vector.tensor_tensor(qk, qk, bcast_in(inv[:, s, :], 8), ALU.mult).then_inc(unit_done, 1)

                def phi(b, s):
                    wait(dve, raw_done, count(b, 1, 1))
                    nc.vector.tensor_scalar(low[:, :], raw[:, s, 0:2 * P], 0.0, None, ALU.min).then_inc(low_done, 1)
                    wait(dve, s_mm, count(b, 4, -4))
                    wait(dve, qexp_done, count(b, 1, -1))
                    wait(dve, low_exp, count(b, 1, 1))
                    nc.vector.scalar_tensor_tensor(qkT[:, s, :], raw[:, s, 0:2 * P], 0.0, low[:, :], ALU.max,
                                                   ALU.add).then_inc(qk_done, 1)

                def mask(b, s, q):
                    if q == 0:
                        wait(dve, pv_mm, count(b, 1, -1))
                    wait(dve, s_mm, count(b, 4, q + 1))
                    nc.vector.tensor_tensor(PT[:, s, 4 * q:4 * q + 4, :],
                                            S[q % 2][:, :].rearrange("p (h k) -> p h k", h=4),
                                            bcast_mid(C.tri, 4), ALU.mult).then_inc(p_done, 1)

                def divide(b):
                    wait(dve, o_mm, count(b, 1, 1))
                    nc.vector.tensor_scalar(small[:, 0, :], heads(O[:, P:2 * P])[:, :, 0], 1e-6, None,
                                            ALU.max).then_inc(mean_done, 1)
                    wait(dve, mean_done, count(b, 1, 1))
                    nc.vector.reciprocal(small[:, 1, :], small[:, 0, :]).then_inc(var_done, 1)
                    wait(dve, ot_mm, count(b, 1, 0))
                    wait(dve, var_done, count(b, 1, 1))
                    nc.vector.tensor_tensor(heads(oc[:, :]), heads(O[:, 0:P]), bcast_in(small[:, 1, :], 8),
                                            ALU.mult).then_inc(on_done, 1)

                def centre(b):
                    wait(dve, o_mm, count(b, 1, 1))
                    nc.vector.tensor_reduce(small[:, 0, :], heads(O[:, 0:P]), AXX, ALU.add).then_inc(mean_done, 1)
                    wait(dve, ot_mm, count(b, 1, 0))
                    wait(dve, mean_done, count(b, 1, 1))
                    nc.vector.scalar_tensor_tensor(heads(oc[:, :]), bcast_in(small[:, 0, :], 8), -1.0 / 8,
                                                   heads(O[:, 0:P]), ALU.mult, ALU.add).then_inc(oc_done, 1)

                def variance(b):
                    wait(dve, osq_done, count(b, 1, 1))
                    nc.vector.tensor_reduce(small[:, 1, :], heads(osq[:, :]), AXX, ALU.add).then_inc(var_done, 1)

                def add(b):
                    wait(dve, y_mm, count(b, 1, 1))
                    nc.vector.tensor_tensor(tile_of(X, b), tile_of(X, b), Y[:, P:2 * P], ALU.add).then_inc(x_done, 1)

                def step(b, s, tail, head, front):
                    prev, nxt = shift(b, -1), shift(b, 1)
                    if front:
                        ln.moments_of(nc, dve, nxt, 1 - s, X)
                    if head:
                        mask(b, s, 0)
                        mask(b, s, 1)
                    if front:
                        ln.scale(nc, dve, nxt, 1 - s, X, xnt_mm)
                    if head:
                        mask(b, s, 2)
                    if tail:
                        (centre if delta else divide)(prev)
                    if head:
                        mask(b, s, 3)
                    if tail and delta:
                        variance(prev)
                    if front and not delta:
                        phi(nxt, 1 - s)
                    if tail:
                        add(prev)
                    if front and delta:
                        unit(nxt, 1 - s)
                if delta:
                    nc.vector.memset(xb[:, :, 0:3], 0.0).then_inc(zeros_done, 1)
                ln.moments_of(nc, dve, 0, 0, X)
                ln.scale(nc, dve, 0, 0, X, xnt_mm)
                (unit if delta else phi)(0, 0)
                pipeline(dve, step)

            @block.scalar
            def _(act):
                def copy_normed(b, s):
                    wait(act, proj_mm, count(b, 1, -1))
                    wait(act, xnt_mm, count(b, 1, 1))
                    nc.scalar.copy(xb[:, s, 3:3 + P], T[:, 0:P]).then_inc(xnt_done, 1)

                def copy_raw(b, s):
                    wait(act, pv_mm, count(b, 1, -1))
                    wait(act, proj_mm, count(b, 1, 1))
                    if delta:
                        wait(act, on_done, count(b, 1, -1))
                        wait(act, qkt_mm, count(b, 1, -1))
                        nc.scalar.copy(gate[:, s, :], A[:, 3 * P:4 * P])
                        nc.scalar.activation(raw[:, s, :], A[:, 0:3 * P], ACT.Silu).then_inc(raw_done, 1)
                    else:
                        wait(act, qk_done, count(b, 1, -1))
                        nc.scalar.copy(raw[:, s, :], A[:, 0:3 * P]).then_inc(raw_done, 1)

                def exp_low(b):
                    wait(act, low_done, count(b, 1, 1))
                    nc.scalar.activation(low[:, :], low[:, :], ACT.Exp).then_inc(low_exp, 1)

                def copy_qk(b, s):
                    wait(act, s_mm, count(b, 4, -4))
                    wait(act, qexp_done, count(b, 1, -1))
                    wait(act, qkt_mm, count(b, 1, 1))
                    nc.scalar.copy(qkT[:, s, :], T[:, P:3 * P]).then_inc(qk_done, 1)

                def copy_sums(b):
                    wait(act, o_mm, count(b, 1, 0))
                    wait(act, pv_mm, count(b, 1, 1))
                    flat = lambda t: t.rearrange("p j q -> p (j q)")
                    ins = nc.scalar.copy(flat(nd[:, 0, :, :]), NUM[:, :])
                    if not delta:
                        ins = nc.scalar.copy(flat(nd[:, 1, :, :]), DEN[:, :])
                    ins.then_inc(nd_done, 1)

                def copy_out(b):
                    wait(act, y_mm, count(b, 1, 0))
                    wait(act, ot_mm, count(b, 1, 1))
                    nc.scalar.copy(oT[:, :], Y[:, 0:P]).then_inc(ot_done, 1)

                def step(b, s, tail, head, front):
                    prev, nxt = shift(b, -1), shift(b, 1)
                    if tail:
                        copy_sums(prev)
                    if front:
                        copy_normed(nxt, 1 - s)
                    if tail and delta:
                        copy_out(prev)
                    if front:
                        copy_raw(nxt, 1 - s)
                        if delta:
                            copy_qk(nxt, 1 - s)
                        else:
                            exp_low(nxt)
                    if tail and not delta:
                        copy_out(prev)
                copy_normed(0, 0)
                copy_raw(0, 0)
                if delta:
                    copy_qk(0, 0)
                else:
                    exp_low(0)
                pipeline(act, step)
        sems.clear()


def stage_l1_attn(nc, C, sems, d, X):
    with ExitStack() as x:
        sb = lambda n, shape: x.enter_context(nc.sbuf_tensor(f"l1a_{n}", shape, F32))
        w = sb("w", [P, 5, DM])
        taps = sb("taps", [P, 4, 3 * DM])
        conv = sb("conv", [P, 4, 3 * DM])
        w0 = sb("w0", [P, P])
        gb = sb("gb", [P, 2, 8])
        id4 = sb("id4", [P, 4, DM])
        w_in, t_done, id_done = sems(3)
        with nc.Block() as block:
            @block.sync
            def _(sp):
                sp.dma_start(w[:, :, :], d["l1a_w"]).then_inc(w_in, 16)
                sp.dma_start(conv[:, :, :].rearrange("p j n -> p (j n)"), row_bcast(d["l1a_conv"], 12 * DM)).then_inc(w_in, 16)
                sp.dma_start(w0[:, :], d["l1a_w0"]).then_inc(w_in, 16)
                sp.dma_start(gb[:, :, :].rearrange("p j n -> p (j n)"), row_bcast(d["l1a_gb"], 16)).then_inc(w_in, 16)

            @block.gpsimd
            def _(pool):
                masked_out_weights(pool, id4, C.ident, C, id_done)

            @block.vector
            def _(dve):
                dve.wait_ge(w_in, 64)
                wt = w[:, 0:3, :].rearrange("p n c -> p (n c)")
                for j in range(4):
                    ins = nc.vector.tensor_tensor(taps[:, j, :], wt, conv[:, j, :], ALU.mult)
                ins.then_inc(t_done, 1)
                dve.wait_ge(t_done, 1)
                nc.vector.tensor_tensor(taps[:, 3, :], taps[:, 3, :], wt, ALU.add)
        sems.clear()
        linear_attention(nc, C, sems, "l1a", X, taps, w[:, 4, :], id4, "delta", w0=w0, wg=w[:, 3, :],
                         gamma=gb[:, 0, :], beta=gb[:, 1, :])


def stage_l2_attn(nc, C, sems, d, X):
    with ExitStack() as x:
        sb = lambda n, shape: x.enter_context(nc.sbuf_tensor(f"l2a_{n}", shape, F32))
        w = sb("w", [P, 4 * DM])
        id4 = sb("id4", [P, 4, DM])
        w_in, id_done = sems(2)
        with nc.Block() as block:
            @block.sync
            def _(sp):
                sp.dma_start(w[:, :], d["l2a_w"]).then_inc(w_in, 16)
                sp.wait_ge(w_in, 16)

            @block.gpsimd
            def _(pool):
                masked_out_weights(pool, id4, C.ident, C, id_done)
        sems.clear()
        linear_attention(nc, C, sems, "l2a", X, w, w[:, 3 * DM:4 * DM], id4, "phi")


def wide_head_attention(nc, C, sems, tag, X, wq, wk, wv, wf, scale, out_bias=None, ctx_dram=None,
                        q_bias=None, k_bias=None):
    with ExitStack() as x:
        sb = lambda n, shape: x.enter_context(nc.sbuf_tensor(f"{tag}_{n}", shape, F32))
        ps = lambda n: x.enter_context(nc.psum_tensor(f"{tag}_{n}", [P, 512], F32))
        ln = LayerNorm(nc, sb)
        xnT = sb("xnT", [P, 2, P])
        ctxT = sb("ctxT", [P, 2, P])
        qT = sb("qT", [P, 2, 8, P])
        Kexp = sb("Kexp", [P, 2, 8, 2, P])
        V = sb("V", [P, 2, 8 * P])
        Sx = sb("Sx", [P, 2, 16, P])
        mx = sb("mx", [P, 2, 16])
        sm = sb("sm", [P, 2, 16])
        PT = sb("PT", [P, 2, 4, P])
        oT = sb("oT", [P, 8, P])
        A, S, TP, NUM, TO = [ps("A0"), ps("A1")], [ps("S0"), ps("S1")], ps("TP"), [ps("N0"), ps("N1")], ps("TO")
        (zeros_done, xnt_mm, xnt_done, ctx_in0, ctx_in1, proj_mm, q_done, k_done, v_done, s_mm, add_done, max_done,
         sub_done, exp_done, sum_done, inv_done, w_done, tp_mm, pt_done, pv_mm, num_done, y_mm, x_done) = sems(23)
        ctx_in = [ctx_in0, ctx_in1]
        ln.sems(sems)
        flat = lambda t: t.rearrange("p h k -> p (h k)")
        quad = lambda t, s, q: t[:, s, 4 * q:4 * q + 4, :]

        with nc.Block() as block:

            @block.sync
            def _(sp):
                def load_ctx(b, s):
                    wait(sp, proj_mm, count(b, 6, -6))
                    sp.dma_start(ctxT[:, s, :], dram_of(ctx_dram, b)).then_inc(ctx_in[s], 16)
                if ctx_dram is not None:
                    each(sp, load_ctx)

            @block.gpsimd
            def _(pool):
                def subtract(b, s, q):
                    wait(pool, max_done, count(b, 4, q + 1))
                    pool.tensor_tensor(quad(Sx, s, q), quad(Sx, s, q), bcast_in(mx[:, s, 4 * q:4 * q + 4], P),
                                       ALU.subtract).then_inc(sub_done, 1)

                def normalise(b, s, q):
                    wait(pool, inv_done, count(b, 4, q + 1))
                    pool.tensor_tensor(quad(Sx, s, q), quad(Sx, s, q), bcast_in(sm[:, s, 4 * q:4 * q + 4], P),
                                       ALU.mult).then_inc(w_done, 1)

                def step(b, s, tail, head, front):
                    if front:
                        ln.rstd(pool, shift(b, 1), 1 - s, C)
                    for q in range(4):
                        if tail:
                            normalise(shift(b, -1), 1 - s, q)
                        if head:
                            subtract(b, s, q)
                pool.memset(Kexp[:, :, :, :, :], 0.0).then_inc(zeros_done, 1)
                ln.rstd(pool, 0, 0, C)
                pipeline(pool, step)

            @block.tensor
            def _(pe):
                def normed_T(b, s):
                    wait(pe, x_done, count(b, 1, -1))
                    wait(pe, ln.done, count(b, 1, 1))
                    nc.tensor.transpose(TO[:, P:2 * P], ln.xn[:, s, :], C.ident).then_inc(xnt_mm, 1)

                def project(b, s):
                    kv = xnT[:, s, :] if ctx_dram is None else ctxT[:, s, :]
                    wait(pe, xnt_done, count(b, 1, 1))
                    wait(pe, v_done, count(b, 2, 0))
                    for n in range(2):
                        for c in range(4 * n, 4 * n + 4):
                            mm = nc.tensor.matmul(A[n][:, (c % 4) * P:(c % 4 + 1) * P], wq[:, c * P:(c + 1) * P],
                                                  xnT[:, s, :], start=True, stop=True)
                        mm.then_inc(proj_mm, 1)
                    if ctx_dram is not None:
                        wait(pe, ctx_in[s], count_own(b, 16, 16))
                    for n in range(2):
                        wait(pe, q_done, count(b, 2, n + 1))
                        for c in range(4 * n, 4 * n + 4):
                            mm = nc.tensor.matmul(A[n][:, (c % 4) * P:(c % 4 + 1) * P], wk[:, c * P:(c + 1) * P],
                                                  kv, start=True, stop=True)
                        mm.then_inc(proj_mm, 1)
                    for n in range(2):
                        wait(pe, k_done, count(b, 2, n + 1))
                        nc.tensor.matmul(A[n][:, :], kv, wv[:, n * 512:(n + 1) * 512], start=True,
                                         stop=True).then_inc(proj_mm, 1)

                def scores(b, s, q):
                    wait(pe, add_done, count(b, 4, q - 1))
                    for c in (2 * q, 2 * q + 1):
                        mm = nc.tensor.matmul(S[q % 2][:, (c % 2) * 256:(c % 2) * 256 + 256], qT[:, s, c, :],
                                              Kexp[:, s, c, :, :].rearrange("p h k -> p (h k)"), start=True, stop=True)
                    mm.then_inc(s_mm, 1)

                def turn(b, s, q):
                    wait(pe, pt_done, count(b, 4, q))
                    wait(pe, w_done, count(b, 4, q + 1))
                    for h in range(4):
                        mm = nc.tensor.transpose(TP[:, h * P:(h + 1) * P], Sx[:, s, 4 * q + h, :], C.ident)
                    mm.then_inc(tp_mm, 1)

                def sum_keys(b, s, q):
                    if q == 0:
                        wait(pe, num_done, count(b, 2, 0))
                    wait(pe, pt_done, count(b, 4, q + 1))
                    for h in range(4 * q, 4 * q + 4):
                        r, c = 64 * (h % 2), h // 2
                        mm = nc.tensor.matmul(NUM[q // 2][r:r + 64, (c % 4) * P:(c % 4 + 1) * P],
                                              V[:, s, h * 64:h * 64 + 64], PT[:, q % 2, h % 4, :],
                                              start=True, stop=True)
                    mm.then_inc(pv_mm, 1)

                def project_out(b):
                    wait(pe, xnt_done, min(b + 2, NB) if isinstance(b, int) else count(b, 1, 2))
                    wait(pe, num_done, count(b, 2, 2))
                    if out_bias is not None:
                        nc.tensor.matmul(TO[:, 0:P], C.ones[0:1, :], out_bias, start=True, stop=False)
                    for c in range(8):
                        mm = nc.tensor.matmul(TO[:, 0:P], oT[:, c, :], wf[:, c, :],
                                              start=(c == 0 and out_bias is None), stop=(c == 7))
                    mm.then_inc(y_mm, 1)

                def step(b, s, tail, head, front):
                    prev, nxt = shift(b, -1), shift(b, 1)
                    for q in range(4):
                        if head:
                            scores(b, s, q)
                        if tail:
                            turn(prev, 1 - s, q)
                            if q > 0:
                                sum_keys(prev, 1 - s, q - 1)
                    if tail:
                        sum_keys(prev, 1 - s, 3)
                        project_out(prev)
                    if front:
                        normed_T(nxt, 1 - s)
                        project(nxt, 1 - s)
                normed_T(0, 0)
                project(0, 0)
                pipeline(pe, step)

            @block.vector
            def _(dve):
                def copy_keys(b, s):
                    wait(dve, s_mm, count(b, 4, -4))
                    if isinstance(b, int) and b == 0:
                        dve.wait_ge(zeros_done, 1)
                    for n in range(2):
                        wait(dve, proj_mm, count(b, 6, 3 + n))
                        for h in range(2):
                            rows = slice(64 * h, 64 * h + 64)
                            src = A[n][rows, :].rearrange("p (c k) -> p c k", c=4)
                            dst = Kexp[rows, s, 4 * n:4 * n + 4, h, :]
                            if k_bias is None:
                                ins = nc.vector.tensor_copy(dst, src)
                            else:
                                ins = nc.vector.tensor_tensor(dst, src, bcast_in(k_bias[rows, 4 * n:4 * n + 4], P),
                                                              ALU.add)
                        ins.then_inc(k_done, 1)

                def mask_max(b, s, q):
                    if q == 0:
                        wait(dve, tp_mm, count(b, 4, -4))
                    wait(dve, s_mm, count(b, 4, q + 1))
                    nc.vector.tensor_tensor(quad(Sx, s, q), S[q % 2][:, :].rearrange("p (h k) -> p h k", h=4),
                                            bcast_mid(C.causal, 4), ALU.add).then_inc(add_done, 1)
                    wait(dve, add_done, count(b, 4, q + 1))
                    nc.vector.tensor_reduce(mx[:, s, 4 * q:4 * q + 4], quad(Sx, s, q), AXX,
                                            ALU.max).then_inc(max_done, 1)

                def sums(b, s, q):
                    wait(dve, exp_done, count(b, 4, q + 1))
                    part = sm[:, s, 4 * q:4 * q + 4]
                    nc.vector.tensor_reduce(part, quad(Sx, s, q), AXX, ALU.add).then_inc(sum_done, 1)
                    wait(dve, sum_done, count(b, 4, q + 1))
                    nc.vector.reciprocal(part, part).then_inc(inv_done, 1)

                def add(b):
                    wait(dve, y_mm, count(b, 1, 1))
                    nc.vector.tensor_tensor(tile_of(X, b), tile_of(X, b), TO[:, 0:P], ALU.add).then_inc(x_done, 1)

                def step(b, s, tail, head, front):
                    prev, nxt = shift(b, -1), shift(b, 1)
                    if front:
                        ln.moments_of(nc, dve, nxt, 1 - s, X)
                    for q in range(4):
                        if tail:
                            sums(prev, 1 - s, q)
                        if head:
                            mask_max(b, s, q)
                    if front:
                        ln.scale(nc, dve, nxt, 1 - s, X, xnt_mm)
                    if tail:
                        add(prev)
                    if front:
                        copy_keys(nxt, 1 - s)
                ln.moments_of(nc, dve, 0, 0, X)
                ln.scale(nc, dve, 0, 0, X, xnt_mm)
                copy_keys(0, 0)
                pipeline(dve, step)

            @block.scalar
            def _(act):
                def copy_normed(b, s):
                    wait(act, proj_mm, count(b, 6, -6))
                    wait(act, xnt_mm, count(b, 1, 1))
                    nc.scalar.copy(xnT[:, s, :], TO[:, P:2 * P]).then_inc(xnt_done, 1)

                def copy_qv(b, s):
                    wait(act, s_mm, count(b, 4, -4))
                    for n in range(2):
                        wait(act, proj_mm, count(b, 6, 1 + n))
                        if q_bias is None:
                            ins = nc.scalar.copy(flat(qT[:, s, 4 * n:4 * n + 4, :]), A[n][:, :])
                        else:
                            for c in range(4 * n, 4 * n + 4):
                                ins = nc.scalar.activation(qT[:, s, c, :], A[n][:, (c % 4) * P:(c % 4 + 1) * P],
                                                           ACT.Identity, bias=q_bias[:, c:c + 1])
                        ins.then_inc(q_done, 1)
                    wait(act, pv_mm, count(b, 4, -4))
                    for n in range(2):
                        wait(act, proj_mm, count(b, 6, 5 + n))
                        nc.scalar.copy(V[:, s, n * 512:(n + 1) * 512], A[n][:, :]).then_inc(v_done, 1)

                def exps(b, s, q):
                    wait(act, sub_done, count(b, 4, q + 1))
                    nc.scalar.activation(quad(Sx, s, q), quad(Sx, s, q), ACT.Exp, scale=scale).then_inc(exp_done, 1)

                def copy_turned(b, q):
                    wait(act, pv_mm, count(b, 4, max(q - 1, 0)))
                    wait(act, tp_mm, count(b, 4, q + 1))
                    nc.scalar.copy(flat(PT[:, q % 2, :, :]), TP[:, :]).then_inc(pt_done, 1)

                def copy_sum(b, n):
                    wait(act, y_mm, count(b, 1, 0))
                    wait(act, pv_mm, count(b, 4, 2 * n + 2))
                    nc.scalar.copy(flat(oT[:, 4 * n:4 * n + 4, :]), NUM[n][:, :]).then_inc(num_done, 1)

                def step(b, s, tail, head, front):
                    prev, nxt = shift(b, -1), shift(b, 1)
                    for q in range(4):
                        if tail:
                            copy_turned(prev, q)
                            if q == 3:
                                copy_sum(prev, 0)
                        if head:
                            exps(b, s, q)
                    if tail:
                        copy_sum(prev, 1)
                    if front:
                        copy_normed(nxt, 1 - s)
                        copy_qv(nxt, 1 - s)
                copy_normed(0, 0)
                copy_qv(0, 0)
                pipeline(act, step)
        sems.clear()


def stage_l1_xattn(nc, C, sems, d, X):
    with ExitStack() as x:
        sb = lambda n, shape: x.enter_context(nc.sbuf_tensor(f"l1x_{n}", shape, F32))
        w = sb("w", [P, 3, 8 * DM])
        wf = sb("wf", [P, 8, DM])
        b = sb("b", [P, 3, 8])
        bf = sb("bf", [1, DM])
        w_in, b_mm, b_done = sems(3)
        with nc.psum_tensor("l1x_pb", [P, 512], F32) as pb, nc.Block() as block:
            @block.sync
            def _(sp):
                sp.dma_start(w[:, :, :], d["l1x_w"]).then_inc(w_in, 16)
                sp.dma_start(wf[:, :, :], d["l1x_wf"]).then_inc(w_in, 16)
                sp.dma_start(b[:, :, :], d["l1x_b"]).then_inc(w_in, 16)
                sp.dma_start(bf[:, :], d["l1x_bf"]).then_inc(w_in, 16)

            @block.tensor
            def _(pe):
                pe.wait_ge(w_in, 64)
                for c in range(8):
                    mm = nc.tensor.matmul(pb[0:1, 0:DM], b[:, 2, c:c + 1], wf[:, c, :], start=(c == 0), stop=(c == 7))
                mm.then_inc(b_mm, 1)

            @block.vector
            def _(dve):
                dve.wait_ge(b_mm, 1)
                nc.vector.tensor_tensor(bf[:, :], bf[:, :], pb[0:1, 0:DM], ALU.add).then_inc(b_done, 1)
        sems.clear()
        wide_head_attention(nc, C, sems, "l1x", X, w[:, 0, :], w[:, 1, :], w[:, 2, :], wf, 1.0 / 16,
                            out_bias=bf[0:1, :], ctx_dram=d["ctxT"], q_bias=b[:, 0, :], k_bias=b[:, 1, :])


def stage_l3_attn(nc, C, sems, d, X):
    with ExitStack() as x:
        sb = lambda n, shape: x.enter_context(nc.sbuf_tensor(f"l3a_{n}", shape, F32))
        w = sb("w", [P, 3, 8 * DM])
        wf = sb("wf", [P, 8, DM])
        (w_in,) = sems(1)
        with nc.Block() as block:
            @block.sync
            def _(sp):
                sp.dma_start(w[:, :, :], d["l3a_w"]).then_inc(w_in, 16)
                sp.dma_start(wf[:, :, :], d["l3a_wf"]).then_inc(w_in, 16)
                sp.wait_ge(w_in, 32)
        sems.clear()
        wide_head_attention(nc, C, sems, "l3a", X, w[:, 0, :], w[:, 1, :], w[:, 2, :], wf, 1.0 / 8)


def stage_l2_xattn(nc, C, sems, d, X):
    with ExitStack() as x:
        sb = lambda n, shape: x.enter_context(nc.sbuf_tensor(f"l2x_{n}", shape, F32))
        w = sb("w", [P, 4, DM])
        b = sb("b", [P, 3])
        bo = sb("bo", [1, DM])
        wo4 = sb("wo4", [P, 4, DM])
        w_in, b_mm, wo_done, b_done = sems(4)
        with nc.psum_tensor("l2x_pb", [P, 512], F32) as pb, nc.Block() as block:
            @block.sync
            def _(sp):
                sp.dma_start(w[:, :, :], d["l2x_w"]).then_inc(w_in, 16)
                sp.dma_start(b[:, :], d["l2x_b"]).then_inc(w_in, 16)
                sp.dma_start(bo[:, :], d["l2x_bo"]).then_inc(w_in, 16)

            @block.tensor
            def _(pe):
                pe.wait_ge(w_in, 48)
                nc.tensor.matmul(pb[0:1, 0:DM], b[:, 2:3], w[:, 3, :], start=True, stop=True).then_inc(b_mm, 1)

            @block.vector
            def _(dve):
                dve.wait_ge(b_mm, 1)
                nc.vector.tensor_tensor(bo[:, :], bo[:, :], pb[0:1, 0:DM], ALU.add).then_inc(b_done, 1)
                masked_out_weights(dve, wo4, w[:, 3, :], C, wo_done)
        sems.clear()
        small_head_attention(nc, C, sems, "l2x", src=X, dests=[X], wq=w[:, 0, :], wk=w[:, 1, :], wv=w[:, 2, :],
                             wo4=wo4, scale=8 ** -0.5, out_bias=bo[0:1, :], ctx_dram=d["ctxT"],
                             q_bias=b[:, 0:1], k_bias=b[:, 1:2])


class Chain:

    def __init__(self, eng, done):
        self.eng, self.done, self.steps = eng, done, 0

    def add(self, ins):
        ins.then_inc(self.done, 1)
        self.steps += 1

    def wait(self):
        self.eng.wait_ge(self.done, self.steps)


def running(nc, chain, a, b, c, op):
    n, dist, other = a.shape[-1], 1, c
    while dist < n:
        chain.wait()
        chain.add(nc.vector.tensor_copy(b[:, :, 0:dist], a[:, :, 0:dist]))
        chain.add(nc.vector.tensor_tensor(b[:, :, dist:n], a[:, :, dist:n], a[:, :, 0:n - dist], op))
        a, b, other, dist = b, other, b, 2 * dist
    return a


def normalise_all(nc, C, sems, tag, src, dst):
    with ExitStack() as x:
        sb = lambda n, shape: x.enter_context(nc.sbuf_tensor(f"{tag}_{n}", shape, F32))
        stat = sb("stat", [P, NB, 6])
        mv = sb("mv", [P, NB, 2])
        ve = sb("ve", [P, NB])
        rstd = sb("rstd", [P, NB])
        stats_done, moments_done, ve_done, rstd_done, centred = sems(5)
        with nc.Block() as block:
            @block.vector
            def _(dve):
                for b in range(NB):
                    nc.vector.bn_stats(stat[:, b, :], tile_of(src, b)).then_inc(stats_done, 1)
                dve.wait_ge(stats_done, NB)
                for b in range(NB):
                    nc.vector.bn_aggr(mv[:, b, :], stat[:, b, :]).then_inc(moments_done, 1)
                dve.wait_ge(moments_done, NB)
                for q in range(4):
                    part = slice(q * 8 * DM, (q + 1) * 8 * DM)
                    nc.vector.tensor_tensor(dst[:, part].rearrange("p (b k) -> p b k", k=DM),
                                            src[:, part].rearrange("p (b k) -> p b k", k=DM),
                                            bcast_in(mv[:, 8 * q:8 * q + 8, 0], DM), ALU.subtract).then_inc(centred, 1)

            @block.gpsimd
            def _(pool):
                pool.wait_ge(moments_done, NB)
                pool.tensor_tensor(ve[:, :], mv[:, :, 1], C.eps.to_broadcast([P, NB]), ALU.add).then_inc(ve_done, 1)
                pool.wait_ge(ve_done, 1)
                pool.tensor_tensor(rstd[:, :], ve[:, :], C.neghalf.to_broadcast([P, NB]), ALU.pow).then_inc(rstd_done, 1)
                pool.wait_ge(rstd_done, 1)
                for q in range(4):
                    pool.wait_ge(centred, q + 1)
                    part = dst[:, q * 8 * DM:(q + 1) * 8 * DM].rearrange("p (b k) -> p b k", k=DM)
                    pool.tensor_tensor(part, part, bcast_in(rstd[:, 8 * q:8 * q + 8], DM), ALU.mult)
        sems.clear()


def turn_all(nc, C, sems, tag, src, dst, affine=None):
    with ExitStack() as x:
        T = [x.enter_context(nc.psum_tensor(f"{tag}_T{i}", [P, 512], F32)) for i in range(2)]
        t_mm, t_done = sems(2)
        with nc.Block() as block:
            @block.tensor
            def _(pe):
                for g in range(NB // 4):
                    wait(pe, t_done, g - 1)
                    for k in range(4):
                        mm = nc.tensor.transpose(T[g % 2][:, k * P:(k + 1) * P], tile_of(src, 4 * g + k), C.ident)
                    mm.then_inc(t_mm, 1)

            @block.scalar
            def _(act):
                for g in range(NB // 4):
                    act.wait_ge(t_mm, g + 1)
                    if affine is None:
                        nc.scalar.copy(dst[:, g * 512:(g + 1) * 512], T[g % 2][:, :]).then_inc(t_done, 1)
                    else:
                        nc.scalar.activation(dst[:, g * 512:(g + 1) * 512], T[g % 2][:, :], ACT.Identity,
                                             bias=affine[1], scale=affine[0]).then_inc(t_done, 1)
        sems.clear()


QUANT_STEPS = 17


def quantise(nc, dve, chain, v, m, r, t):
    n = v.shape[1]
    blocks = lambda a: a.rearrange("p (c k) -> p c k", k=32)
    y, z, c = [t[:, i, 0:n] for i in range(3)]

    def step(f, *args):
        chain.wait()
        chain.add(f(*args))
    step(nc.vector.tensor_reduce, m, blocks(v), AXX, ALU.max, True)
    step(nc.vector.tensor_scalar, m, m, 1 / 7.5, 1e-30, ALU.mult, ALU.max)
    step(nc.vector.reciprocal, r, m)
    step(nc.vector.tensor_tensor, blocks(y), blocks(v), bcast_in(r, 32), ALU.mult)
    step(nc.vector.tensor_tensor, v, y, y, ALU.mult)
    step(nc.vector.tensor_scalar, c, v, 16.0, 1.0, ALU.is_ge, ALU.mult)
    chain.add(nc.vector.tensor_scalar(z, v, 4.0, 1.0, ALU.is_ge, ALU.mult))
    chain.wait()
    chain.add(nc.vector.scalar_tensor_tensor(v, c, 2.0, z, ALU.mult, ALU.add))
    step(nc.vector.scalar_tensor_tensor, z, z, 2.0, c, ALU.mult, ALU.add)
    chain.add(nc.vector.tensor_scalar(v, v, 1.0, 0.125, ALU.add, ALU.mult))
    step(nc.vector.tensor_scalar, z, z, -2.0, 8.0, ALU.mult, ALU.add)
    step(nc.vector.tensor_tensor, z, y, z, ALU.mult)
    step(nc.vector.tensor_scalar, y, z, 12582912.0, -12582912.0, ALU.add, ALU.add)
    step(nc.vector.tensor_tensor, z, y, z, ALU.subtract)
    step(nc.vector.scalar_tensor_tensor, y, z, 0.5, y, ALU.is_ge, ALU.subtract)
    step(nc.vector.scalar_tensor_tensor, v, y, -1.0, v, ALU.mult, ALU.mult)
    step(nc.vector.tensor_tensor, blocks(v), blocks(v), bcast_in(m, 32), ALU.mult)


def stage_l1_ffn(nc, C, sems, d, X):
    with ExitStack() as x:
        sb = lambda n, shape: x.enter_context(nc.sbuf_tensor(f"l1f_{n}", shape, F32))
        w = sb("w", [P, DM])
        wT = sb("wT", [P, DM])
        bias = sb("bias", [P, DM])
        XN = sb("XN", [P, NB * DM])
        XT = sb("XT", [P, NB * DM])
        CH = 8 * DM
        m = sb("m", [P, CH // 32])
        r = sb("r", [P, CH // 32])
        t = sb("t", [P, 3, CH])
        normalise_all(nc, C, sems, "l1f_n", X, XN)
        w_in, steps, x_biased, w_mm, wt_done = sems(5)
        with nc.psum_tensor("l1f_W", [P, 512], F32) as W, nc.Block() as block:
            @block.sync
            def _(sp):
                sp.dma_start(w[:, :], d["l1f_w"]).then_inc(w_in, 16)
                sp.dma_start(bias[:, :], row_bcast(d["l1f_b"], DM)).then_inc(w_in, 16)

            @block.vector
            def _(dve):
                chain = Chain(dve, steps)
                dve.wait_ge(w_in, 32)
                quantise(nc, dve, chain, w[:, :], m[:, 0:4], r[:, 0:4], t)
                for q in range(4):
                    quantise(nc, dve, chain, XN[:, q * CH:(q + 1) * CH], m[:, :], r[:, :], t)
                dve.wait_ge(w_mm, 1)
                nc.vector.tensor_copy(wT[:, :], W[:, 0:P]).then_inc(wt_done, 1)

            @block.gpsimd
            def _(pool):
                pool.wait_ge(w_in, 32)
                for q in range(4):
                    part = X[:, q * CH:(q + 1) * CH].rearrange("p (b k) -> p b k", k=DM)
                    pool.tensor_tensor(part, part, bcast_mid(bias[:, :], 8), ALU.add).then_inc(x_biased, 1)

            @block.tensor
            def _(pe):
                pe.wait_ge(steps, QUANT_STEPS)
                nc.tensor.transpose(W[:, 0:P], w[:, :], C.ident).then_inc(w_mm, 1)
        sems.clear()
        turn_all(nc, C, sems, "l1f_t", XN, XT)
        y_mm, x_done = sems(2)
        Y = [x.enter_context(nc.psum_tensor(f"l1f_Y{i}", [P, 512], F32)) for i in range(2)]
        with nc.Block() as block:
            @block.tensor
            def _(pe):
                for g in range(NB // 4):
                    wait(pe, x_done, g - 1)
                    for k in range(4):
                        mm = nc.tensor.matmul(Y[g % 2][:, k * P:(k + 1) * P], tile_of(XT, 4 * g + k), wT[:, :],
                                              start=True, stop=True)
                    mm.then_inc(y_mm, 1)

            @block.vector
            def _(dve):
                for g in range(NB // 4):
                    dve.wait_ge(y_mm, g + 1)
                    part = X[:, g * 512:(g + 1) * 512]
                    nc.vector.tensor_tensor(part, part, Y[g % 2][:, :], ALU.add).then_inc(x_done, 1)
        sems.clear()


def route(nc, C, sems, tag, XT, wr, bias, share, experts, k):
    n = NB * experts
    with ExitStack() as x:
        sb = lambda nm, shape: x.enter_context(nc.sbuf_tensor(f"{tag}_{nm}", shape, F32))
        s, eq, cum, cum2 = [sb(nm, [P, NB, experts]) for nm in ("s", "eq", "cum", "cum2")]
        top = sb("top", [P, NB, 8])
        mx = sb("mx", [P, NB])
        left = sb("left", [P, NB])
        per = 512 // experts
        banks = -(-NB // per)
        L = [x.enter_context(nc.psum_tensor(f"{tag}_L{i}", [P, 512], F32)) for i in range(banks)]
        l_mm, steps, exp_done = sems(3)
        with nc.Block() as block:
            @block.tensor
            def _(pe):
                for b in range(NB):
                    nc.tensor.matmul(L[b // per][:, (b % per) * experts:(b % per + 1) * experts], tile_of(XT, b), wr,
                                     start=True, stop=True).then_inc(l_mm, 1)

            @block.vector
            def _(dve):
                chain = Chain(dve, steps)

                def step(f, *args):
                    chain.wait()
                    chain.add(f(*args))
                dve.wait_ge(l_mm, NB)
                for i in range(banks):
                    b0, b1 = i * per, min(NB, (i + 1) * per)
                    logits = L[i][:, 0:(b1 - b0) * experts].rearrange("p (b e) -> p b e", e=experts)
                    if bias is None:
                        chain.add(nc.vector.tensor_copy(s[:, b0:b1, :], logits))
                    else:
                        chain.add(nc.vector.tensor_tensor(s[:, b0:b1, :], logits, bcast_mid(bias, b1 - b0), ALU.add))
                flat = lambda a: a[:, :, :].rearrange("p b e -> p (b e)")
                step(nc.vector.tensor_reduce, mx[:, :], s[:, :, :], AXX, ALU.max)
                step(nc.vector.tensor_tensor, s[:, :, :], s[:, :, :], bcast_in(mx[:, :], experts), ALU.subtract)
                chain.wait()
                dve.wait_ge(exp_done, 1)
                chain.add(nc.vector.tensor_reduce(mx[:, :], s[:, :, :], AXX, ALU.add))
                step(nc.vector.reciprocal, mx[:, :], mx[:, :])
                step(nc.vector.tensor_tensor, s[:, :, :], s[:, :, :], bcast_in(mx[:, :], experts), ALU.mult)
                chain.wait()
                for b in range(NB):
                    chain.add(nc.vector.max(top[:, b, :], s[:, b, :]))
                chain.wait()
                kth = bcast_in(top[:, :, k - 1], experts)
                chain.add(nc.vector.tensor_tensor(eq[:, :, :], s[:, :, :], kth, ALU.is_equal))
                chain.add(nc.vector.tensor_tensor(share, s[:, :, :], kth, ALU.is_gt))
                chain.wait()
                chain.add(nc.vector.tensor_reduce(left[:, :], share, AXX, ALU.add))
                step(nc.vector.tensor_scalar, left[:, :], left[:, :], -1.0, float(k), ALU.mult, ALU.add)
                a = running(nc, chain, eq, cum, cum2, ALU.add)
                b_ = cum2 if a is cum else cum
                step(nc.vector.tensor_tensor, b_[:, :, :], a[:, :, :], bcast_in(left[:, :], experts), ALU.is_le)
                step(nc.vector.tensor_tensor, flat(eq), flat(eq), flat(b_), ALU.mult)
                step(nc.vector.tensor_tensor, share, share, eq[:, :, :], ALU.add)
                step(nc.vector.tensor_tensor, share, share, s[:, :, :], ALU.mult)
                step(nc.vector.tensor_reduce, left[:, :], share, AXX, ALU.add)
                step(nc.vector.tensor_scalar, left[:, :], left[:, :], 1e-12, 0.0, ALU.max, ALU.add)
                step(nc.vector.reciprocal, left[:, :], left[:, :])
                step(nc.vector.tensor_tensor, share, share, bcast_in(left[:, :], experts), ALU.mult)
                chain.wait()
            @block.scalar
            def _(act):
                act.wait_ge(steps, banks + 2)
                nc.scalar.activation(s[:, :, :], s[:, :, :], ACT.Exp).then_inc(exp_done, 1)
        sems.clear()


def experts_sum(nc, C, sems, tag, X, XT, share, n_experts, chunks, w1, wu, w2, b1=None):
    units = n_experts * chunks
    GROUPS = NB // 4
    with ExitStack() as x:
        sb = lambda n, shape: x.enter_context(nc.sbuf_tensor(f"{tag}_{n}", shape, F32))
        ps = lambda n: x.enter_context(nc.psum_tensor(f"{tag}_{n}", [P, 512], F32))
        G, U, Y = [ps("G0"), ps("G1")], [ps("U0"), ps("U1")], [ps("Y0"), ps("Y1")]
        sg = sb("sg", [P, 2, 512])
        h = sb("h", [P, 2, 512])
        u_mm, silu_done, h_done, down_mm, x_done = sems(5)

        with nc.Block() as block:

            @block.tensor
            def _(pe):
                def up(i, n):
                    pe.wait_ge(h_done, i * units + (n + 1))
                    rhs = XT[:, bass.ts(i, 512)]
                    mm = nc.tensor.matmul(G[n % 2][:, :], w1[:, n, :], rhs, start=True, stop=True)
                    if wu is not None:
                        mm = nc.tensor.matmul(U[n % 2][:, :], wu[:, n, :], rhs, start=True, stop=True)
                    mm.then_inc(u_mm, 1)

                def down(i, n):
                    e, c = n // chunks, n % chunks
                    if c == 0:
                        pe.wait_ge(x_done, i * n_experts + (e + 1))
                    pe.wait_ge(h_done, i * units + (n + 3))
                    for k in range(4):
                        mm = nc.tensor.matmul(Y[e % 2][:, k * P:(k + 1) * P], h[:, n % 2, k * P:(k + 1) * P],
                                              w2[:, n, :], start=(c == 0 and k == 0), stop=(c == chunks - 1),
                                              skip_group_check=True)
                    mm.then_inc(down_mm, 1)
                with pe.Fori(0, GROUPS) as i:
                    up(i, 0)
                    for n in range(1, units):
                        up(i, n)
                        down(i, n - 1)
                    down(i, units - 1)

            @block.scalar
            def _(act):
                if wu is None:
                    act.sem_inc(h_done, 2)

                def hidden(i, n):
                    act.wait_ge(u_mm, i * units + (n + 1))
                    if wu is None:
                        act.wait_ge(down_mm, i * units + (n + 1))
                        nc.scalar.activation(h[:, n % 2, :], G[n % 2][:, :], ACT.Gelu_apprx_tanh,
                                             bias=b1[:, n:n + 1]).then_inc(h_done, 1)
                    else:
                        act.wait_ge(h_done, i * units + (n + 1))
                        nc.scalar.activation(sg[:, n % 2, :], G[n % 2][:, :], ACT.Silu).then_inc(silu_done, 1)
                with act.Fori(0, GROUPS) as i:
                    for n in range(units):
                        hidden(i, n)

            @block.gpsimd
            def _(pool):
                pool.sem_inc(down_mm, 2)
                pool.sem_inc(x_done, 2)

            @block.vector
            def _(dve):
                if wu is not None:
                    dve.sem_inc(h_done, 2)

                def product(i, n):
                    dve.wait_ge(down_mm, i * units + (n + 1))
                    dve.wait_ge(silu_done, i * units + (n + 1))
                    nc.vector.tensor_tensor(h[:, n % 2, :], sg[:, n % 2, :], U[n % 2][:, :],
                                            ALU.mult).then_inc(h_done, 1)

                def add(i, e):
                    dve.wait_ge(x_done, i * n_experts + (e + 2))
                    dve.wait_ge(down_mm, i * units + (chunks * (e + 1) + 2))
                    for k in range(4):
                        dst = X[:, bass.ds(i * 512 + k * P, P)]
                        ins = nc.vector.scalar_tensor_tensor(dst, Y[e % 2][:, k * P:(k + 1) * P],
                                                             share[:, bass.ds(i * 4 + k, 1), e], dst,
                                                             ALU.mult, ALU.add)
                    ins.then_inc(x_done, 1)
                with dve.Fori(0, GROUPS) as i:
                    for n in range(units):
                        if wu is not None:
                            product(i, n)
                        if n >= 2 and (n - 1) % chunks == 0:
                            add(i, (n - 1) // chunks - 1)
                    for e in range((units - 2) // chunks, n_experts):
                        add(i, e)
        sems.clear()


def stage_l2_ffn(nc, C, sems, d, X):
    E, SHARED = 32, 4
    with ExitStack() as x:
        sb = lambda n, shape: x.enter_context(nc.sbuf_tensor(f"l2f_{n}", shape, F32))
        XT = sb("XT", [P, NB * DM])
        share = sb("share", [P, NB, E + SHARED])
        wr = sb("wr", [P, E])
        rb = sb("rb", [P, E])
        w_in, ones_done = sems(2)
        with nc.Block() as block:
            @block.sync
            def _(sp):
                sp.dma_start(wr[:, :], d["l2f_wr"]).then_inc(w_in, 16)
                sp.dma_start(rb[:, :], row_bcast(d["l2f_rb"], E)).then_inc(w_in, 16)
                sp.wait_ge(w_in, 32)

            @block.gpsimd
            def _(pool):
                pool.memset(share[:, :, E:E + SHARED], 1.0).then_inc(ones_done, 1)
        sems.clear()
        with nc.sbuf_tensor("l2f_XN", [P, NB * DM], F32) as XN:
            normalise_all(nc, C, sems, "l2f_n", X, XN)
            turn_all(nc, C, sems, "l2f_t", XN, XT)
            route(nc, C, sems, "l2f_r", XT, wr[:, :], rb[:, :], share[:, :, 0:E], E, 4)
        wg, wu, wd = [sb(n, [P, E + SHARED, DM]) for n in ("wg", "wu", "wd")]
        with nc.Block() as block:
            @block.sync
            def _(sp):
                (w_in,) = sems(1)
                for w, n in ((wg, "l2f_wg"), (wu, "l2f_wu"), (wd, "l2f_wd")):
                    sp.dma_start(w[:, :, :], d[n]).then_inc(w_in, 16)
                sp.wait_ge(w_in, 48)
        sems.clear()
        experts_sum(nc, C, sems, "l2f_e", X, XT, share, E + SHARED, 1, wg, wu, wd)


def stage_l3_ffn(nc, C, sems, d, X):
    E, CH = 8, 4
    with ExitStack() as x:
        sb = lambda n, shape: x.enter_context(nc.sbuf_tensor(f"l3f_{n}", shape, F32))
        H = sb("H", [P, NB * DM])
        v = sb("v", [P, 7])
        bo = sb("bo", [1, DM])
        normalise_all(nc, C, sems, "l3f_u", X, H)
        with ExitStack() as y:
            w = y.enter_context(nc.sbuf_tensor("l3f_w", [P, 4, DM], F32))
            wo4 = y.enter_context(nc.sbuf_tensor("l3f_wo4", [P, 4, DM], F32))
            w_in, b_mm, wo_done, b_done, x_done = sems(5)
            with nc.psum_tensor("l3f_pb", [P, 512], F32) as pb, nc.Block() as block:
                @block.sync
                def _(sp):
                    sp.dma_start(w[:, :, :], d["l3f_w"]).then_inc(w_in, 16)
                    sp.dma_start(v[:, :], d["l3f_v"]).then_inc(w_in, 16)
                    sp.dma_start(bo[:, :], d["l3f_bo"]).then_inc(w_in, 16)

                @block.tensor
                def _(pe):
                    pe.wait_ge(w_in, 48)
                    nc.tensor.matmul(pb[0:1, 0:DM], v[:, 6:7], w[:, 3, :], start=True, stop=True).then_inc(b_mm, 1)

                @block.gpsimd
                def _(pool):
                    pool.tensor_tensor(X[:, :], X[:, :], H[:, :], ALU.add).then_inc(x_done, 1)

                @block.vector
                def _(dve):
                    dve.wait_ge(b_mm, 1)
                    nc.vector.tensor_tensor(bo[:, :], bo[:, :], pb[0:1, 0:DM], ALU.add).then_inc(b_done, 1)
                    masked_out_weights(dve, wo4, w[:, 3, :], C, wo_done)
            sems.clear()
            small_head_attention(nc, C, sems, "l3f", src=H, dests=[X, H], wq=w[:, 0, :], wk=w[:, 1, :],
                                 wv=w[:, 2, :], wo4=wo4, scale=8 ** -0.5, out_bias=bo[0:1, :],
                                 q_bias=v[:, 4:5], k_bias=v[:, 5:6], affine=(v[:, 0:1], v[:, 1:2]))
        XT = sb("XT", [P, NB * DM])
        share = sb("share", [P, NB, E])
        wg = sb("wg", [P, E])
        b2 = sb("b2", [E, DM])
        w1 = sb("w1", [P, E * CH, DM])
        w2 = sb("w2", [P, E * CH, DM])
        b1 = sb("b1", [P, E * CH])
        (w_in,) = sems(1)
        with nc.Block() as block:
            @block.sync
            def _(sp):
                for w, n in ((wg[:, :], "wg"), (b2[:, :], "b2"), (w1[:, :, :], "w1"), (w2[:, :, :], "w2"),
                             (b1[:, :], "b1")):
                    sp.dma_start(w, d["l3f_" + n]).then_inc(w_in, 16)
                sp.wait_ge(w_in, 80)
        sems.clear()
        normalise_all(nc, C, sems, "l3f_n", H, H)
        turn_all(nc, C, sems, "l3f_t", H, XT, affine=(v[:, 2:3], v[:, 3:4]))
        route(nc, C, sems, "l3f_r", XT, wg[:, :], None, share[:, :, :], E, 2)
        t_mm, t_done, y_mm, x_done = sems(4)
        with ExitStack() as y:
            T, Y = [[y.enter_context(nc.psum_tensor(f"l3f_{n}{i}", [P, 512], F32)) for i in range(2)] for n in "TY"]
            sT = y.enter_context(nc.sbuf_tensor("l3f_sT", [E, NB, P], F32))
            with nc.Block() as block:
                @block.tensor
                def _(pe):
                    for g in range(NB // 4):
                        wait(pe, t_done, g - 1)
                        for k in range(4):
                            mm = nc.tensor.transpose(T[g % 2][0:E, k * P:(k + 1) * P], share[:, 4 * g + k, :], C.ident)
                        mm.then_inc(t_mm, 1)
                    for g in range(NB // 4):
                        wait(pe, x_done, g - 1)
                        pe.wait_ge(t_done, g + 1)
                        for k in range(4):
                            mm = nc.tensor.matmul(Y[g % 2][:, k * P:(k + 1) * P], sT[:, 4 * g + k, :], b2[:, :],
                                                  start=True, stop=True)
                        mm.then_inc(y_mm, 1)

                @block.scalar
                def _(act):
                    for g in range(NB // 4):
                        act.wait_ge(t_mm, g + 1)
                        nc.scalar.copy(sT[:, 4 * g:4 * g + 4, :].rearrange("e b t -> e (b t)"),
                                       T[g % 2][0:E, :]).then_inc(t_done, 1)

                @block.vector
                def _(dve):
                    for g in range(NB // 4):
                        dve.wait_ge(y_mm, g + 1)
                        part = X[:, g * 512:(g + 1) * 512]
                        nc.vector.tensor_tensor(part, part, Y[g % 2][:, :], ALU.add).then_inc(x_done, 1)
            sems.clear()
        experts_sum(nc, C, sems, "l3f_e", X, XT, share, E, CH, w1, None, w2, b1)


def stage_l3_xattn(nc, C, sems, d, X):
    HEADS, HD = 8, 16
    ROWS = NB * HEADS
    g_dram = nc.dram_tensor("l3x_dram_gates", (2 * HEADS, NB * P), F32, kind="Internal").ap()
    m_dram = nc.dram_tensor("l3x_dram_max", (NB, HEADS * P), F32, kind="Internal").ap()
    with ExitStack() as x:
        sb = lambda n, shape: x.enter_context(nc.sbuf_tensor(f"l3x_{n}", shape, F32))
        XT = sb("XT", [P, NB * DM])
        wg = sb("wg", [P, 3, 2 * HEADS])
        gb = sb("gb", [2 * HEADS, 1])
        gn = sb("gn", [P, 2, DM])
        gt = sb("gt", [P, NB, HEADS])
        em = sb("em", [P, NB, HEADS])
        H = sb("H", [P, NB, HEADS, HD + 1])
        with nc.sbuf_tensor("l3x_XN", [P, NB * DM], F32) as XN:
            normalise_all(nc, C, sems, "l3x_n", X, XN)
            turn_all(nc, C, sems, "l3x_t", XN, XT)
        with ExitStack() as y:
            sy = lambda n, shape: y.enter_context(nc.sbuf_tensor(f"l3x1_{n}", shape, F32))
            CT = sy("CT", [P, NB * DM])
            GT = sy("GT", [2 * HEADS, NB * P])
            it, ft, u, v, w = [sy(n, [P, 2, P]) for n in ("it", "ft", "u", "v", "w")]
            G = [y.enter_context(nc.psum_tensor(f"l3x1_G{i}", [P, 512], F32)) for i in range(2)]
            T = y.enter_context(nc.psum_tensor("l3x1_T", [P, 512], F32))
            (w_in, kv_done, g_mm, g_done, g_out, g_in, steps, abs_done, ln_done, em_done, m_out,
             t_mm, exp_done) = sems(13)
            with nc.Block() as block:
                @block.sync
                def _(sp):
                    sp.dma_start(wg[:, :, :], d["l3x_wg"]).then_inc(w_in, 16)
                    sp.dma_start(gb[:, :], d["l3x_gb"]).then_inc(w_in, 16)
                    sp.dma_start(CT[:, :], d["ctxT_rows"]).then_inc(w_in, 16)
                    for i, n in enumerate(("l3x_gnw", "l3x_gnb")):
                        sp.dma_start(gn[:, i, :], row_bcast(d[n], DM)).then_inc(w_in, 16)
                    sp.wait_ge(g_done, NB // 4)
                    sp.dma_start(g_dram, GT[:, :]).then_inc(g_out, 16)
                    sp.wait_ge(g_out, 16)
                    for i, t in enumerate((it, ft)):
                        rows = g_dram[HEADS * i:HEADS * i + HEADS].rearrange("h (b t) -> b h t", t=P)
                        for half in range(2):
                            sp.dma_start(t[:, half, :], rows[16 * half:16 * half + 16]).then_inc(g_in, 16)
                    sp.wait_ge(em_done, 1)
                    for half in range(2):
                        sp.dma_start(m_dram[16 * half:16 * half + 16].rearrange("b (h t) -> (b h) t", t=P),
                                     u[:, half, :]).then_inc(m_out, 16)
                    sp.wait_ge(m_out, 32)

                @block.tensor
                def _(pe):
                    pe.wait_ge(kv_done, 1)
                    for g in range(NB // 4):
                        part = slice(g * 512, (g + 1) * 512)
                        wait(pe, g_done, g - 1)
                        nc.tensor.matmul(G[g % 2][0:16, :], wg[:, 0, :], XT[:, part], start=True, stop=False)
                        nc.tensor.matmul(G[g % 2][0:16, :], wg[:, 1, :], CT[:, part], start=False,
                                         stop=True).then_inc(g_mm, 1)
                    pe.wait_ge(exp_done, 2)
                    for half in range(2):
                        nc.tensor.transpose(T[:, half * P:(half + 1) * P], it[:, half, :], C.ident)
                    for half in range(2):
                        mm = nc.tensor.transpose(T[:, (2 + half) * P:(3 + half) * P], ft[:, half, :], C.ident)
                    mm.then_inc(t_mm, 1)

                @block.scalar
                def _(act):
                    act.wait_ge(w_in, 80)
                    for g in range(NB // 4):
                        act.wait_ge(g_mm, g + 1)
                        nc.scalar.activation(GT[:, g * 512:(g + 1) * 512], G[g % 2][0:16, :], ACT.Identity,
                                             bias=gb[:, :]).then_inc(g_done, 1)
                    act.wait_ge(abs_done, 1)
                    nc.scalar.activation(u[:, :, :], u[:, :, :], ACT.Exp, scale=-1.0).then_inc(exp_done, 1)
                    act.wait_ge(exp_done, 1)
                    nc.scalar.activation(u[:, :, :], u[:, :, :], ACT.Ln, bias=C.ones[:, 0:1]).then_inc(ln_done, 1)
                    act.wait_ge(em_done, 1)
                    nc.scalar.activation(ft[:, :, :], ft[:, :, :], ACT.Exp, scale=-1.0).then_inc(exp_done, 1)

                @block.vector
                def _(dve):
                    chain = Chain(dve, steps)
                    dve.wait_ge(w_in, 80)
                    nc.vector.tensor_tensor(wg[:, 1, :], wg[:, 1, :], wg[:, 2, :], ALU.add).then_inc(kv_done, 1)
                    dve.wait_ge(g_in, 64)
                    nc.vector.scalar_tensor_tensor(u[:, :, :], ft[:, :, :], -1.0, ft[:, :, :], ALU.mult,
                                                   ALU.max).then_inc(abs_done, 1)
                    dve.wait_ge(ln_done, 1)
                    chain.add(nc.vector.scalar_tensor_tensor(ft[:, :, :], ft[:, :, :], 0.0, u[:, :, :], ALU.min,
                                                             ALU.subtract))
                    F = running(nc, chain, ft, v, w, ALU.add)
                    chain.wait()
                    chain.add(nc.vector.tensor_tensor(it[:, :, :], it[:, :, :], F[:, :, :], ALU.subtract))
                    chain.wait()
                    M = running(nc, chain, it, u, w if F is v else v, ALU.max)
                    assert M is u
                    chain.wait()
                    nc.vector.tensor_tensor(ft[:, :, :], M[:, :, :], F[:, :, :], ALU.add).then_inc(em_done, 1)
                    dve.wait_ge(t_mm, 1)
                    flat = lambda t: t[:, :, :].rearrange("p b h -> p (b h)")
                    nc.vector.tensor_copy(flat(gt), T[:, 0:ROWS])
                    nc.vector.tensor_copy(flat(em), T[:, ROWS:2 * ROWS])
            sems.clear()

        with ExitStack() as y:
            sy = lambda n, shape: y.enter_context(nc.sbuf_tensor(f"l3x2_{n}", shape, F32))
            Mb = sy("Mb", [P, 2, HEADS, P])
            W = sy("W", [P, 2, HEADS, P])
            Q = sy("Q", [P, 2, HEADS, P])
            Ct = sy("Ct", [P, 2, HEADS, P])
            ctxT = sy("ctxT", [P, 2, P])
            vn = sy("vn", [P, 2, DM])
            vx = sy("vx", [P, 2, HEADS, HD + 1])
            S = [y.enter_context(nc.psum_tensor(f"l3x2_S{i}", [P, 512], F32)) for i in range(4)]
            O = [y.enter_context(nc.psum_tensor(f"l3x2_O{i}", [P, 512], F32)) for i in range(2)]
            (in0, in1, vones_done, w_done, exp_done, mask_done, q_done, vx_done, s_mm, c_done, o_mm, o_done,
             pad) = sems(13)
            loaded = [in0, in1]
            flat = lambda t, s: t[:, s, :, :].rearrange("p h k -> p (h k)")
            with nc.Block() as block:
                @block.sync
                def _(sp):
                    def load(b, s):
                        wait(sp, w_done, count(b, 1, -1))
                        settle(sp, pad)
                        wait(sp, s_mm, count(b, 2, -2))
                        settle(sp, pad)
                        wait(sp, vx_done, count(b, 1, -1))
                        settle(sp, pad)
                        row = m_dram[b:b + 1] if isinstance(b, int) else m_dram[bass.ds(b[0] * 2 + b[1], 1)]
                        sp.dma_start(flat(Mb, s), row.to_broadcast([P, HEADS * P])).then_inc(loaded[s], 16)
                        sp.dma_start(ctxT[:, s, :], dram_of(d["ctxT"], b)).then_inc(loaded[s], 16)
                        sp.dma_start(vn[:, s, :], dram_of(d["ctx"], b)).then_inc(loaded[s], 16)
                    each(sp, load)

                @block.gpsimd
                def _(pool):
                    def spread(b, s):
                        wait(pool, s_mm, count(b, 2, -2))
                        settle(pool, pad)
                        pool.tensor_tensor(Q[:, s, :, :], bcast_mid(tile_of(XT, b), HEADS), bcast_in(C.hmask16, P),
                                           ALU.mult).then_inc(q_done, 1)

                    def mask(b, s):
                        wait(pool, exp_done, count(b, 1, 1))
                        pool.tensor_tensor(W[:, s, :, :], W[:, s, :, :], bcast_mid(C.tri, HEADS),
                                           ALU.mult).then_inc(mask_done, 1)

                    def f(b, s):
                        spread(b, s)
                        mask(b, s)
                    pool.memset(vx[:, :, :, :], 1.0).then_inc(vones_done, 1)
                    each(pool, f)

                @block.tensor
                def _(pe):
                    def scores(b, s):
                        wait(pe, loaded[s], count_own(b, 48, 48))
                        wait(pe, q_done, count(b, 1, 1))
                        for q in range(2):
                            wait(pe, c_done, count(b, 2, -2))
                            nc.tensor.matmul(S[2 * s + q][:, :], ctxT[:, s, :],
                                             Q[:, s, 4 * q:4 * q + 4, :].rearrange("p h k -> p (h k)"),
                                             start=True, stop=True).then_inc(s_mm, 1)

                    def sum_keys(b, s):
                        wait(pe, o_done, count(b, 1, 0))
                        wait(pe, vx_done, count(b, 1, 1))
                        wait(pe, c_done, count(b, 2, 2))
                        for h in range(HEADS):
                            mm = nc.tensor.matmul(O[s][:, h * (HD + 1):(h + 1) * (HD + 1)], Ct[:, s, h, :],
                                                  vx[:, s, h, :], start=True, stop=True)
                        mm.then_inc(o_mm, 1)

                    def step(b, s, tail, head, front):
                        if head:
                            scores(b, s)
                        if tail:
                            sum_keys(shift(b, -1), 1 - s)
                    pipeline(pe, step)

                @block.vector
                def _(dve):
                    def exponents(b, s):
                        wait(dve, c_done, count(b, 2, -2))
                        wait(dve, loaded[s], count_own(b, 48, 48))
                        for h in range(HEADS):
                            g = gt[:, b, h:h + 1] if isinstance(b, int) else gt[:, bass.ds(b[0] * 2 + b[1], 1), h]
                            ins = nc.vector.tensor_scalar(W[:, s, h, :], Mb[:, s, h, :], g, 0.0, ALU.subtract, ALU.max)
                        ins.then_inc(w_done, 1)

                    def weigh(b, s):
                        wait(dve, mask_done, count(b, 1, 1))
                        wait(dve, o_mm, count(b, 1, -1))
                        for q in range(2):
                            wait(dve, s_mm, count(b, 2, q + 1))
                            part = lambda t: t[:, s, 4 * q:4 * q + 4, :].rearrange("p h k -> p (h k)")
                            nc.vector.tensor_tensor(part(Ct), part(W), S[2 * s + q][:, :], ALU.mult).then_inc(c_done, 1)

                    def step(b, s, tail, head, front):
                        if front:
                            exponents(shift(b, 1), 1 - s)
                        if head:
                            weigh(b, s)
                    exponents(0, 0)
                    pipeline(dve, step)

                @block.scalar
                def _(act):
                    def exps(b, s):
                        wait(act, w_done, count(b, 1, 1))
                        nc.scalar.activation(flat(W, s), flat(W, s), ACT.Exp, scale=-1.0).then_inc(exp_done, 1)

                    def values(b, s):
                        wait(act, o_mm, count(b, 1, -1))
                        wait(act, loaded[s], count_own(b, 48, 48))
                        nc.scalar.copy(vx[:, s, :, 0:HD], vn[:, s, :].rearrange("p (h k) -> p h k", k=HD)
                                       ).then_inc(vx_done, 1)

                    def copy_sums(b, s):
                        wait(act, o_mm, count(b, 1, 1))
                        settle(act, pad)
                        o = O[s][:, 0:HEADS * (HD + 1)]
                        dst = H[:, b, :, :] if isinstance(b, int) else H[:, bass.ds(b[0] * 2 + b[1], 1), :, :]
                        dst = dst.rearrange("p h k -> p (h k)" if isinstance(b, int) else "p a h k -> p (a h k)")
                        nc.scalar.copy(dst, o).then_inc(o_done, 1)

                    def step(b, s, tail, head, front):
                        if front:
                            values(shift(b, 1), 1 - s)
                            exps(shift(b, 1), 1 - s)
                        if tail:
                            copy_sums(shift(b, -1), 1 - s)
                    act.wait_ge(vones_done, 1)
                    values(0, 0)
                    exps(0, 0)
                    pipeline(act, step)
            sems.clear()

        n = sb("n", [P, ROWS])
        o = sb("o", [P, ROWS, HD])
        o2 = sb("o2", [P, ROWS, HD])
        mean = sb("mean", [P, ROWS])
        var = sb("var", [P, ROWS])
        rstd = sb("rstd", [P, ROWS])
        PARTS = 4
        per = ROWS // PARTS
        steps, var_done, ve_done, rstd_done, scaled, out_done = sems(6)
        sums = H[:, :, :, :].rearrange("p b h k -> p (b h) k")
        with nc.Block() as block:
            @block.vector
            def _(dve):
                chain = Chain(dve, steps)

                def step(f, *args):
                    chain.wait()
                    chain.add(f(*args))
                chain.add(nc.vector.scalar_tensor_tensor(n[:, :], sums[:, :, HD], -1.0, sums[:, :, HD], ALU.mult, ALU.max))
                step(nc.vector.tensor_tensor, n[:, :], n[:, :], em[:, :, :].rearrange("p b h -> p (b h)"), ALU.max)
                step(nc.vector.tensor_scalar, n[:, :], n[:, :], 1e-6, 1.0, ALU.add, ALU.mult)
                step(nc.vector.reciprocal, n[:, :], n[:, :])

                def add(q):
                    dve.wait_ge(out_done, q + 1)
                    part = X[:, q * per * HD:(q + 1) * per * HD]
                    nc.vector.tensor_tensor(part, part, o[:, q * per:(q + 1) * per, :].rearrange("p c k -> p (c k)"),
                                            ALU.add)
                for q in range(PARTS):
                    r = slice(q * per, (q + 1) * per)
                    step(nc.vector.tensor_tensor, o[:, r, :], sums[:, r, 0:HD], bcast_in(n[:, r], HD), ALU.mult)
                    step(nc.vector.tensor_reduce, mean[:, r], o[:, r, :], AXX, ALU.add)
                    step(nc.vector.tensor_scalar, mean[:, r], mean[:, r], 1.0 / HD, 0.0, ALU.mult, ALU.add)
                    step(nc.vector.tensor_tensor, o[:, r, :], o[:, r, :], bcast_in(mean[:, r], HD), ALU.subtract)
                    step(nc.vector.tensor_tensor, o2[:, r, :], o[:, r, :], o[:, r, :], ALU.mult)
                    step(nc.vector.tensor_reduce, var[:, r], o2[:, r, :], AXX, ALU.add)
                    chain.wait()
                    nc.vector.tensor_scalar(var[:, r], var[:, r], 1.0 / HD, LN_EPS, ALU.mult, ALU.add).then_inc(var_done, 1)
                    if q > 0:
                        add(q - 1)
                add(PARTS - 1)

            @block.gpsimd
            def _(pool):
                for q in range(PARTS):
                    r = slice(q * per, (q + 1) * per)
                    pool.wait_ge(var_done, q + 1)
                    pool.tensor_tensor(rstd[:, r], var[:, r], C.neghalf.to_broadcast([P, per]), ALU.pow).then_inc(rstd_done, 1)
                    pool.wait_ge(rstd_done, q + 1)
                    pool.tensor_tensor(o[:, r, :], o[:, r, :], bcast_in(rstd[:, r], HD), ALU.mult).then_inc(scaled, 1)
                    part = o[:, r, :].rearrange("p (b h) k -> p b (h k)", h=HEADS)
                    pool.wait_ge(scaled, 2 * q + 1)
                    pool.tensor_tensor(part, part, bcast_mid(gn[:, 0, :], per // HEADS), ALU.mult).then_inc(scaled, 1)
                    pool.wait_ge(scaled, 2 * q + 2)
                    pool.tensor_tensor(part, part, bcast_mid(gn[:, 1, :], per // HEADS), ALU.add).then_inc(out_done, 1)
        sems.clear()


STAGES = [stage_l0_attn, stage_l0_xattn, stage_l0_ffn, stage_l1_attn, stage_l1_xattn, stage_l1_ffn, stage_l2_attn,
          stage_l2_xattn, stage_l2_ffn, stage_l3_attn, stage_l3_xattn, stage_l3_ffn]



def build(nc, d, x_dram, out_dram, stages=None):
    with ExitStack() as ctx:
        X = ctx.enter_context(nc.sbuf_tensor("x_sbuf", [P, NB * DM], F32))
        C = Consts(nc, ctx)
        x_in = ctx.enter_context(nc.semaphore("x_in"))
        x_out = ctx.enter_context(nc.semaphore("x_out"))
        sems = Sems(nc, ctx, 40)
        with nc.Block() as block:
            @block.sync
            def _(sp):
                sp.dma_start(C.tile[:, :], d["consts"]).then_inc(x_in, 16)
                sp.dma_start(X[:, :], x_dram).then_inc(x_in, 16)
                sp.wait_ge(x_in, 32)
        for stage in (STAGES if stages is None else stages):
            stage(nc, C, sems, d, X)
        with nc.Block() as block:
            @block.sync
            def _(sp):
                sp.dma_start(out_dram, X[:, :]).then_inc(x_out, 16)
                sp.wait_ge(x_out, 16)



def arrange(v):
    t = lambda a: np.ascontiguousarray(np.swapaxes(a, -1, -2))
    cols = lambda arrays: np.ascontiguousarray(np.stack(arrays, axis=1))
    a = {"consts": Consts.values()}
    a["l0a_w"] = cols([t(v["L0_attn_W" + n]) for n in "qkvo"])
    a["l0a_a"] = cols([v["L0_attn_A" + n] for n in "qkvo"])
    a["l0a_b"] = cols([t(v["L0_attn_B" + n]) for n in "qkvo"])
    a["l0a_bo"] = v["L0_attn_bo"][None]
    a["ctxT"] = t(v["ctx_1024"])
    a["ctxT_rows"] = v["ctx_1024"].transpose(2, 0, 1).reshape(P, NB * P)
    a["l0x_w"] = cols([t(v["L0_xattn_w" + n]) for n in "qkvo"])
    a["l0f_phiT"] = t(v["L0_ffn_phi_w"])
    a["l0f_phi_b"] = v["L0_ffn_phi_b"]
    a["l0f_ew"] = v["L0_ffn_expert_w"].transpose(1, 0, 2)
    a["l0f_eb"] = v["L0_ffn_expert_b"]
    a["l1a_w"] = cols([t(v["L1_attn_W" + n]) for n in "qkvgo"])
    a["l1a_conv"] = np.concatenate([v["L1_attn_conv_" + n] for n in "qkv"]).T.reshape(-1)
    blocks = np.zeros((16, 8, 16, 8), np.float32)
    blocks[np.arange(16), :, np.arange(16), :] = v["L1_attn_W_init"][0]
    a["l1a_w0"] = blocks.reshape(P, P)
    a["l1a_gb"] = np.concatenate([v["L1_attn_ln_gamma"], v["L1_attn_ln_beta"]])
    a["l2a_w"] = np.concatenate([v["L2_attn_w_qkv"].T, v["L2_attn_w_out"].T], axis=1)
    chunks = lambda m: m.reshape(8, P, -1).transpose(1, 0, 2)
    a["l1x_w"] = cols([v["L1_xattn_W" + n] for n in "qkv"])
    a["l1x_wf"] = chunks(v["L1_xattn_Wf"])
    a["l1x_b"] = cols([v["L1_xattn_b" + n].reshape(8, P).T for n in "qkv"])
    a["l1x_bf"] = v["L1_xattn_bf"][None]
    a["l3a_w"] = cols([v["L3_attn_w_" + n].reshape(8 * P, P).T for n in "qkv"])
    a["l3a_wf"] = chunks(v["L3_attn_w_o"].T)
    a["l2x_w"] = cols([t(v["L2_xattn_W" + n]) for n in "qkvo"])
    a["l2x_b"] = cols([v["L2_xattn_b" + n] for n in "qkv"])
    a["l2x_bo"] = v["L2_xattn_bo"][None]
    a["l1f_w"], a["l1f_b"] = v["L1_ffn_weight"], v["L1_ffn_bias"]
    a["l2f_wr"], a["l2f_rb"] = v["L2_ffn_router_w"].T, v["L2_ffn_router_bias"]
    shared = lambda w: v[w].reshape(4, P, P)
    for n, name in (("wg", "gate_w"), ("wu", "up_w")):
        stack = np.concatenate([v["L2_ffn_" + name], shared("L2_ffn_s" + name)])
        a["l2f_" + n] = stack.transpose(2, 0, 1)
    down = np.concatenate([v["L2_ffn_down_w"], v["L2_ffn_sdown_w"].reshape(P, 4, P).transpose(1, 0, 2)])
    a["l2f_wd"] = down.transpose(2, 0, 1)
    a["l3f_w"] = cols([*np.split(v["L3_ffn_w_qkv"], 3, axis=1), v["L3_ffn_w_o"]])
    a["l3f_v"] = cols([v["L3_ffn_ln" + n] for n in ("1_w", "1_b", "2_w", "2_b")] + np.split(v["L3_ffn_b_qkv"], 3))
    a["l3f_bo"] = v["L3_ffn_b_o"][None]
    a["l3f_wg"], a["l3f_b2"] = v["L3_ffn_w_gate"], v["L3_ffn_b2"]
    a["l3f_w1"] = v["L3_ffn_w1"].reshape(8, P, 4, P).transpose(1, 0, 2, 3).reshape(P, 32, P)
    a["l3f_w2"] = v["L3_ffn_w2"].reshape(32, P, P).transpose(1, 0, 2)
    a["l3f_b1"] = v["L3_ffn_b1"].reshape(32, P).T
    gates = np.concatenate([v["L3_xattn_Wi_w"], v["L3_xattn_Wf_w"]]).reshape(16, 3, P)
    a["l3x_wg"] = gates.transpose(2, 1, 0)
    a["l3x_gb"] = np.concatenate([v["L3_xattn_Wi_b"], v["L3_xattn_Wf_b"]])[:, None]
    a["l3x_gnw"], a["l3x_gnb"] = v["L3_xattn_gn_w"], v["L3_xattn_gn_b"]
    a["ctx"] = v["ctx_1024"]
    a["l0x_b"] = cols([v["L0_xattn_b" + n][None] for n in "qkvo"])
    return a


def kernel(**inputs):
    import concourse.bacc as bacc
    from concourse.bass_utils import run_bass_kernel_spmd

    v = {n: np.asarray(a) for n, a in inputs.items()}
    arrays = {n: np.ascontiguousarray(a) for n, a in arrange(v).items()}
    arrays["x_tokens"] = np.ascontiguousarray(v["x"].transpose(1, 0, 2).reshape(P, NB * DM))
    nc = bacc.Bacc("TRN2", target_bir_lowering=False, num_devices=1)
    d = {n: nc.dram_tensor("in_" + n, a.shape, F32, kind="ExternalInput").ap() for n, a in arrays.items()}
    out = nc.dram_tensor("out", (P, NB * DM), F32, kind="ExternalOutput").ap()
    build(nc, d, d["x_tokens"], out)
    r = run_bass_kernel_spmd(nc, [{"in_" + n: a for n, a in arrays.items()}], core_ids=[0])
    return np.ascontiguousarray(r.results[0]["out"].reshape(P, NB, DM).transpose(1, 0, 2))
```

```python
from contextlib import ExitStack

import numpy as np

import concourse.bass as bass
from concourse import mybir

F32 = mybir.dt.float32
ALU = mybir.AluOpType
ACT = mybir.ActivationFunctionType
AXX = mybir.AxisListType.X

P = 128
NB = 32
DM = 128
LN_EPS = 1e-5
NEG = -1.0e30
PAIRS = (NB - 4) // 2



def shift(b, d):
    return b + d if isinstance(b, int) else (b[0], b[1] + d)


def count(b, per, off):
    if isinstance(b, int):
        return per * b + off
    return b[0] * (2 * per) + (per * b[1] + off)


def count_own(b, per, off):
    if isinstance(b, int):
        return per * (b // 2) + off
    return b[0] * per + (per * (b[1] // 2) + off)


def wait(eng, sem, value):
    if isinstance(value, int) and value <= 0:
        return
    eng.wait_ge(sem, value)


def settle(eng, pad):
    eng.sem_inc(pad, 1)


def tile_of(t, b, width=DM):
    if isinstance(b, int):
        return t[:, b * width:(b + 1) * width]
    return t[:, bass.ts(b[0] * 2 + b[1], width)]


def dram_of(t, b):
    if isinstance(b, int):
        return t[b]
    return t[bass.ds(b[0] * 2 + b[1], 1)].rearrange("a p n -> (a p) n")


def pipeline(eng, step):
    step(0, 0, False, True, True)
    step(1, 1, True, True, True)
    with eng.Fori(0, PAIRS) as i:
        step((i, 2), 0, True, True, True)
        step((i, 3), 1, True, True, True)
    step(NB - 2, 0, True, True, True)
    step(NB - 1, 1, True, True, False)
    step(NB, 0, True, False, False)


def ahead(b):
    return not isinstance(b, int) or b + 2 < NB


class Sems:

    def __init__(self, nc, ctx, n):
        self.nc = nc
        self.pool = [ctx.enter_context(nc.semaphore(f"stage_sem_{i}")) for i in range(n)]
        self.used = 0

    def __call__(self, n):
        got = self.pool[self.used:self.used + n]
        assert len(got) == n
        self.used += n
        return got

    def clear(self):
        for s in self.pool[:self.used]:
            self.nc.gpsimd.sem_clear(s)
        self.used = 0
        self.nc.all_engine_barrier()


def bcast_mid(ap2, n):
    return ap2.unsqueeze(1).to_broadcast([ap2.shape[0], n, ap2.shape[1]])


def bcast_in(ap2, n):
    return ap2.unsqueeze(2).to_broadcast([ap2.shape[0], ap2.shape[1], n])


def row_bcast(dram, n):
    return dram.rearrange("(a n) -> a n", a=1).to_broadcast([P, n])


def col(dram):
    return dram.rearrange("(p a) -> p a", a=1)


def each(eng, f):
    f(0, 0)
    f(1, 1)
    with eng.Fori(0, PAIRS) as i:
        f((i, 2), 0)
        f((i, 3), 1)
    f(NB - 2, 0)
    f(NB - 1, 1)


def dram_mid(t, b):
    if isinstance(b, int):
        return t[:, b, :]
    return t[:, bass.ds(b[0] * 2 + b[1], 1), :].rearrange("p a n -> p (a n)")


def small_head_attention(nc, C, sems, tag, *, src, dests, wq, wk, wv, wo, ctx_dram=None, q_bias=None,
                         k_bias=None, out_bias=None, affine=None, permuted=None):
    with ExitStack() as x:
        sb = lambda n, shape: x.enter_context(nc.sbuf_tensor(f"{tag}_{n}", shape, F32))
        ps = lambda n: x.enter_context(nc.psum_tensor(f"{tag}_{n}", [P, 512], F32))
        stat = sb("stat", [P, 2, 6])
        mv = sb("mv", [P, 2, 2])
        ve = sb("ve", [P, 2, 2])
        xn = sb("xn", [P, 2, DM])
        xnT = sb("xnT", [P, 2, P])
        ctxT = sb("ctxT", [P, 2, P])
        qkv = sb("qkv", [P, 2, 3 * P])
        Kexp = sb("Kexp", [P, 2, 16, P])
        nmx = sb("nmx", [P, 2, 16])
        den = sb("den", [P, 2, 16])
        Pr = sb("Pr", [P, 2, 4, P])
        PT = sb("PT", [P, 2, 16, P])
        num = sb("num", [P, 4, P])
        on = sb("on", [P, 2, DM])
        onT = sb("onT", [P, P])
        qin = sb("qin", [P, 2, P])
        A, NUM, O = ps("A"), ps("NUM"), ps("O")
        S = [ps("S0"), ps("S1")]
        TP = [ps("TP0"), ps("TP1")]
        (pad, stats_done, stat_done, ve_done, rstd_done, xn_done, xnt_mm, xnt_done, ctx_in0, ctx_in1, qkv_mm,
         qkv_done, kexp_done, s_mm, max_done, exp_done, tp_mm, pt_done, pv_mm, num_done, gather_mm, inv_done,
         on_done, ont_mm, ont_done, out_mm, x_done, stored, v_in0, v_in1) = sems(30)
        ctx_in, v_in = [ctx_in0, ctx_in1], [v_in0, v_in1]

        with nc.Block() as block:

            @block.sync
            def _(sp):
                def load_ctx(b, s):
                    wait(sp, qkv_mm, count(b, 1, -1))
                    sp.dma_start(ctxT[:, s, :], dram_of(ctx_dram, b)).then_inc(ctx_in[s], 16)
                    if permuted is not None:
                        sp.dma_start(qin[:, s, :], dram_mid(permuted[0], b)).then_inc(ctx_in[s], 16)
                        wait(sp, pv_mm, count(b, 1, -1))
                        sp.dma_start(qkv[:, s, 2 * P:3 * P], dram_mid(permuted[1], b)).then_inc(v_in[s], 16)

                def store(b, s):
                    wait(sp, on_done, count(b, 1, 1))
                    sp.dma_start(dram_mid(permuted[2], b), on[:, s, :]).then_inc(stored, 16)

                def step(b, s, tail, head, front):
                    if front:
                        load_ctx(shift(b, 1), 1 - s)
                    if tail and permuted is not None:
                        store(shift(b, -1), 1 - s)
                if ctx_dram is not None:
                    load_ctx(0, 0)
                    pipeline(sp, step)
                if permuted is not None:
                    wait(sp, stored, 16 * NB)

            @block.gpsimd
            def _(pool):
                def rstd(b, s):
                    wait(pool, stat_done, count(b, 1, 1))
                    pool.tensor_tensor(ve[:, s, 0:1], mv[:, s, 1:2], C.eps, ALU.add).then_inc(ve_done, 1)
                    wait(pool, ve_done, count(b, 1, 1))
                    pool.tensor_tensor(ve[:, s, 1:2], ve[:, s, 0:1], C.neghalf, ALU.pow).then_inc(rstd_done, 1)

                def spread(b, s):
                    wait(pool, qkv_done, count(b, 1, 1))
                    for q in range(4):
                        wait(pool, s_mm, count(b, 4, q - 3))
                        quad = slice(4 * q, 4 * q + 4)
                        pool.tensor_tensor(Kexp[:, s, quad, :], bcast_mid(qkv[:, s, P:2 * P], 4),
                                           bcast_in(C.kmask[:, quad], P), ALU.mult).then_inc(kexp_done, 1)

                def step(b, s, tail, head, front):
                    if front:
                        if permuted is None and ahead(b):
                            rstd(shift(b, 2), s)
                        spread(shift(b, 1), 1 - s)
                if permuted is None:
                    rstd(0, 0)
                    rstd(1, 1)
                spread(0, 0)
                pipeline(pool, step)

            @block.tensor
            def _(pe):
                def normed_T(b, s):
                    if permuted is not None:
                        return
                    wait(pe, qkv_done, count(b, 1, 0))
                    wait(pe, xn_done, count(b, 1, 1))
                    nc.tensor.transpose(A[:, 0:P], xn[:, s, :], C.ident).then_inc(xnt_mm, 1)

                def project(b, s):
                    if permuted is not None:
                        wait(pe, qkv_done, count(b, 1, 0))
                        wait(pe, ctx_in[s], count_own(b, 32, 32))
                        nc.tensor.transpose(A[:, P:2 * P], qin[:, s, :], C.ident)
                        nc.tensor.matmul(A[:, 2 * P:3 * P], C.ones[0:1, :], k_bias, start=True, stop=False)
                        nc.tensor.matmul(A[:, 2 * P:3 * P], ctxT[:, s, :], wk, start=False,
                                         stop=True).then_inc(qkv_mm, 1)
                        return
                    if ctx_dram is not None:
                        wait(pe, ctx_in[s], count_own(b, 16, 16))
                    wait(pe, xnt_done, count(b, 1, 1))
                    kv = xnT[:, s, :] if ctx_dram is None else ctxT[:, s, :]
                    nc.tensor.matmul(A[:, P:2 * P], wq, xnT[:, s, :], start=True, stop=True)
                    nc.tensor.matmul(A[:, 2 * P:3 * P], wk, kv, start=True, stop=True)
                    nc.tensor.matmul(A[:, 3 * P:4 * P], kv, wv, start=True, stop=True).then_inc(qkv_mm, 1)

                def scores(b, s, q):
                    wait(pe, kexp_done, count(b, 4, q + 1))
                    wait(pe, exp_done, count(b, 4, q - 1))
                    nc.tensor.matmul(S[q % 2][:, :], qkv[:, s, 0:P],
                                     Kexp[:, s, 4 * q:4 * q + 4, :].rearrange("p h k -> p (h k)"),
                                     start=True, stop=True).then_inc(s_mm, 1)

                def turn(b, q):
                    wait(pe, pt_done, count(b, 4, q - 1))
                    wait(pe, exp_done, count(b, 4, q + 1))
                    for h in range(4):
                        mm = nc.tensor.transpose(TP[q % 2][:, h * P:(h + 1) * P], Pr[:, q % 2, h, :], C.ident)
                    mm.then_inc(tp_mm, 1)

                def sum_keys(b, s):
                    if permuted is not None:
                        wait(pe, v_in[s], count_own(b, 16, 16))
                    wait(pe, num_done, count(b, 1, 0))
                    wait(pe, pt_done, count(b, 4, 4))
                    for q in range(4):
                        mm = nc.tensor.matmul(NUM[32 * q:32 * q + 32, :], qkv[:, s, 2 * P + 32 * q:2 * P + 32 * q + 32],
                                              PT[:, s, 4 * q:4 * q + 4, :].rearrange("p h k -> p (h k)"),
                                              start=True, stop=True)
                    mm.then_inc(pv_mm, 1)

                def gather(b):
                    wait(pe, x_done if permuted is None else on_done, count(b, 1, 0))
                    wait(pe, num_done, count(b, 1, 1))
                    for j in range(4):
                        mm = nc.tensor.matmul(O[:, 0:DM], num[:, j, :], C.id4[:, j * P:(j + 1) * P],
                                              start=(j == 0), stop=(j == 3))
                    mm.then_inc(gather_mm, 1)

                def turn_out(b, s):
                    if permuted is not None:
                        return
                    wait(pe, on_done, count(b, 1, 1))
                    nc.tensor.transpose(O[:, DM:2 * DM], on[:, s, :], C.ident).then_inc(ont_mm, 1)

                def project_out(b):
                    if permuted is not None:
                        return
                    wait(pe, ont_done, count(b, 1, 1))
                    out = O[:, 2 * DM:3 * DM]
                    if out_bias is not None:
                        nc.tensor.matmul(out, C.ones[0:1, :], out_bias, start=True, stop=False)
                    nc.tensor.matmul(out, onT[:, :], wo, start=out_bias is None, stop=True).then_inc(out_mm, 1)

                def step(b, s, tail, head, front):
                    prev, nxt = shift(b, -1), shift(b, 1)
                    if head:
                        scores(b, s, 0)
                    if front:
                        normed_T(nxt, 1 - s)
                    if tail:
                        turn(prev, 3)
                    if head:
                        scores(b, s, 1)
                    if front and permuted is None:
                        project(nxt, 1 - s)
                    if head:
                        turn(b, 0)
                    if tail:
                        sum_keys(prev, 1 - s)
                    if head:
                        scores(b, s, 2)
                    if front and permuted is not None:
                        project(nxt, 1 - s)
                    if head:
                        turn(b, 1)
                    if tail:
                        gather(prev)
                    if head:
                        scores(b, s, 3)
                    if tail:
                        turn_out(prev, 1 - s)
                    if head:
                        turn(b, 2)
                    if tail:
                        project_out(prev)
                normed_T(0, 0)
                project(0, 0)
                pipeline(pe, step)

            @block.vector
            def _(dve):
                def stats(b, s):
                    if permuted is not None:
                        return
                    nc.vector.bn_stats(stat[:, s, :], tile_of(src, b)).then_inc(stats_done, 1)
                    wait(dve, stats_done, count(b, 1, 1))
                    settle(dve, pad)
                    nc.vector.bn_aggr(mv[:, s, :], stat[:, s, :]).then_inc(stat_done, 1)

                def normed(b, s):
                    if permuted is not None:
                        return
                    wait(dve, xnt_mm, count(b, 1, -1))
                    wait(dve, rstd_done, count(b, 1, 1))
                    nc.vector.tensor_scalar(xn[:, s, :], tile_of(src, b), mv[:, s, 0:1], ve[:, s, 1:2],
                                            ALU.subtract, ALU.mult).then_inc(xn_done, 1)

                def less_max(b, s, q):
                    wait(dve, s_mm, count(b, 4, q + 1))
                    nc.vector.tensor_reduce(nmx[:, s, 4 * q:4 * q + 4], S[q % 2][:, :].rearrange("p (h k) -> p h k", h=4),
                                            AXX, ALU.max, None, None, True).then_inc(max_done, 1)

                def copy_turned(b, s, q):
                    if q == 0:
                        wait(dve, pv_mm, count(b, 1, -1))
                    wait(dve, tp_mm, count(b, 4, q + 1))
                    nc.vector.tensor_copy(PT[:, s, 4 * q:4 * q + 4, :].rearrange("p h k -> p (h k)"),
                                          TP[q % 2][:, :]).then_inc(pt_done, 1)

                def invert(b, s):
                    wait(dve, exp_done, count(b, 4, 4))
                    nc.vector.reciprocal(den[:, s, :], den[:, s, :]).then_inc(inv_done, 1)

                def divide(b, s):
                    wait(dve, inv_done, count(b, 1, 1))
                    if permuted is None:
                        wait(dve, ont_mm, count(b, 1, 0))
                    else:
                        wait(dve, stored, count(b, 16, 0))
                    wait(dve, gather_mm, count(b, 1, 1))
                    nc.vector.tensor_tensor(on[:, s, :].rearrange("p (h k) -> p h k", k=8),
                                            O[:, 0:DM].rearrange("p (h k) -> p h k", k=8),
                                            bcast_in(den[:, s, :], 8), ALU.mult).then_inc(on_done, 1)

                def add(b, s):
                    if permuted is not None:
                        return
                    wait(dve, out_mm, count(b, 1, 1))
                    for dst in dests:
                        ins = nc.vector.tensor_tensor(tile_of(dst, b), tile_of(dst, b), O[:, 2 * DM:3 * DM], ALU.add)
                    ins.then_inc(x_done, 1)

                def step(b, s, tail, head, front):
                    prev, nxt = shift(b, -1), shift(b, 1)
                    if head:
                        less_max(b, s, 0)
                    if tail:
                        invert(prev, 1 - s)
                        copy_turned(prev, 1 - s, 3)
                    if head:
                        less_max(b, s, 1)
                        copy_turned(b, s, 0)
                    if front and ahead(b):
                        stats(shift(b, 2), s)
                    if head:
                        less_max(b, s, 2)
                        copy_turned(b, s, 1)
                    if tail:
                        divide(prev, 1 - s)
                    if head:
                        less_max(b, s, 3)
                        copy_turned(b, s, 2)
                    if front and ahead(b):
                        normed(shift(b, 2), s)
                    if tail:
                        add(prev, 1 - s)
                for n in range(2):
                    stats(n, n)
                    normed(n, n)
                pipeline(dve, step)

            @block.scalar
            def _(act):
                def copy_normed(b, s):
                    if permuted is not None:
                        return
                    wait(act, qkv_mm, count(b, 1, -1))
                    wait(act, xnt_mm, count(b, 1, 1))
                    if affine is None:
                        nc.scalar.copy(xnT[:, s, :], A[:, 0:P]).then_inc(xnt_done, 1)
                    else:
                        nc.scalar.activation(xnT[:, s, :], A[:, 0:P], ACT.Identity, bias=affine[1],
                                             scale=affine[0]).then_inc(xnt_done, 1)

                def copy_qkv(b, s):
                    wait(act, pv_mm, count(b, 1, -1))
                    wait(act, kexp_done, count(b, 4, -4))
                    wait(act, s_mm, count(b, 4, -4))
                    wait(act, qkv_mm, count(b, 1, 1))
                    if permuted is not None:
                        nc.scalar.copy(qkv[:, s, 0:2 * P], A[:, P:3 * P]).then_inc(qkv_done, 1)
                    elif q_bias is None:
                        nc.scalar.copy(qkv[:, s, :], A[:, P:4 * P]).then_inc(qkv_done, 1)
                    else:
                        nc.scalar.activation(qkv[:, s, 0:P], A[:, P:2 * P], ACT.Identity, bias=q_bias)
                        nc.scalar.activation(qkv[:, s, P:2 * P], A[:, 2 * P:3 * P], ACT.Identity, bias=k_bias)
                        nc.scalar.copy(qkv[:, s, 2 * P:3 * P], A[:, 3 * P:4 * P]).then_inc(qkv_done, 1)

                def exps(b, s, q):
                    if q == 0:
                        wait(act, inv_done, count(b, 1, -1))
                        wait(act, on_done, count(b, 1, -1))
                    wait(act, tp_mm, count(b, 4, q - 1))
                    wait(act, max_done, count(b, 4, q + 1))
                    for h in range(4):
                        g = 4 * q + h
                        ins = nc.scalar.activation(Pr[:, q % 2, h, :], S[q % 2][:, h * P:(h + 1) * P], ACT.Exp,
                                                   bias=nmx[:, s, g:g + 1], accum_out=den[:, s, g:g + 1])
                    ins.then_inc(exp_done, 1)

                def copy_sums(b):
                    wait(act, gather_mm, count(b, 1, 0))
                    wait(act, pv_mm, count(b, 1, 1))
                    nc.scalar.copy(num[:, :, :].rearrange("p j q -> p (j q)"), NUM[:, :]).then_inc(num_done, 1)

                def copy_out(b):
                    if permuted is not None:
                        return
                    wait(act, out_mm, count(b, 1, 0))
                    wait(act, ont_mm, count(b, 1, 1))
                    nc.scalar.copy(onT[:, :], O[:, DM:2 * DM]).then_inc(ont_done, 1)

                def step(b, s, tail, head, front):
                    prev, nxt = shift(b, -1), shift(b, 1)
                    if front:
                        copy_normed(nxt, 1 - s)
                    if head:
                        exps(b, s, 0)
                    if head:
                        exps(b, s, 1)
                    if tail:
                        copy_sums(prev)
                    if front:
                        copy_qkv(nxt, 1 - s)
                    if head:
                        exps(b, s, 2)
                    if tail:
                        copy_out(prev)
                    if head:
                        exps(b, s, 3)
                copy_normed(0, 0)
                copy_qkv(0, 0)
                pipeline(act, step)
        sems.clear()


class Consts:

    PARTS = {"ident": P, "hmask": 16, "ones": P, "eps": 1, "neghalf": 1,
             "tri": P, "causal": P, "l2eps": 1, "hmask16": 8, "kmask": 16, "id4": 4 * P, "id2": 2 * P}

    def __init__(self, nc, ctx):
        self.tile = ctx.enter_context(nc.sbuf_tensor("const_tile", [P, sum(self.PARTS.values())], F32))
        starts = dict(zip(self.PARTS, np.cumsum([0] + list(self.PARTS.values()))))
        part = lambda name: self.tile[:, int(starts[name]):int(starts[name]) + self.PARTS[name]]
        self.ident, self.hmask, self.ones = part("ident"), part("hmask"), part("ones")
        self.eps, self.neghalf, self.l2eps = part("eps"), part("neghalf"), part("l2eps")
        self.kmask = part("kmask")
        self.id2 = part("id2")
        self.id4 = part("id4")
        self.hmask16 = part("hmask16")
        self.tri, self.causal = part("tri"), part("causal")

    @classmethod
    def values(cls):
        p = np.arange(P)
        parts = {
            "ident": np.eye(P),
            "hmask": p[:, None] // 8 == np.arange(16)[None],
            "kmask": 8 ** -0.5 * (p[:, None] // 8 == np.arange(16)[None]),
            "ones": np.ones((P, P)),
            "eps": np.full((P, 1), LN_EPS),
            "neghalf": np.full((P, 1), -0.5),
            "tri": p[:, None] <= p[None],
            "causal": np.where(p[:, None] >= p[None], 0.0, NEG),
            "l2eps": np.full((P, 1), 1e-12),
            "id4": (((p[:, None] % 32) // 8 == np.arange(4)[None])[:, :, None] * np.eye(P)[:, None]).reshape(P, 4 * P),
            "id2": (((p[:, None] % 32) // 16 == np.arange(2)[None])[:, :, None] * np.eye(P)[:, None]).reshape(P, 2 * P),
            "hmask16": 0.25 * (p[:, None] // 16 == np.arange(8)[None]),
        }
        return np.concatenate([parts[n] for n in cls.PARTS], axis=1).astype(np.float32)


class LayerNorm:

    def __init__(self, nc, sb):
        self.stat = sb("ln_stat", [P, 2, 6])
        self.mv = sb("ln_mv", [P, 2, 2])
        self.ve = sb("ln_ve", [P, 2, 2])
        self.xn = sb("ln_xn", [P, 2, DM])

    def sems(self, sems):
        (self.pad, self.stats, self.moments, self.var_eps, self.rstd_done, self.done) = sems(6)

    def rstd(self, pool, b, s, C):
        wait(pool, self.moments, count(b, 1, 1))
        pool.tensor_tensor(self.ve[:, s, 0:1], self.mv[:, s, 1:2], C.eps, ALU.add).then_inc(self.var_eps, 1)
        wait(pool, self.var_eps, count(b, 1, 1))
        pool.tensor_tensor(self.ve[:, s, 1:2], self.ve[:, s, 0:1], C.neghalf, ALU.pow).then_inc(self.rstd_done, 1)

    def moments_of(self, nc, dve, b, s, src):
        nc.vector.bn_stats(self.stat[:, s, :], tile_of(src, b)).then_inc(self.stats, 1)
        wait(dve, self.stats, count(b, 1, 1))
        settle(dve, self.pad)
        nc.vector.bn_aggr(self.mv[:, s, :], self.stat[:, s, :]).then_inc(self.moments, 1)

    def scale(self, nc, dve, b, s, src, reader):
        wait(dve, reader, count(b, 1, -1))
        wait(dve, self.rstd_done, count(b, 1, 1))
        nc.vector.tensor_scalar(self.xn[:, s, :], tile_of(src, b), self.mv[:, s, 0:1], self.ve[:, s, 1:2],
                                ALU.subtract, ALU.mult).then_inc(self.done, 1)

    def normalise(self, nc, dve, b, s, src, reader):
        self.moments_of(nc, dve, b, s, src)
        self.scale(nc, dve, b, s, src, reader)


def stage_l0_attn(nc, C, sems, d, X):
    with ExitStack() as x:
        sb = lambda n, shape: x.enter_context(nc.sbuf_tensor(f"l0a_{n}", shape, F32))
        w = sb("w", [P, 4, DM])
        la = sb("la", [16, 4, DM])
        lb = sb("lb", [16, 4, DM])
        bo = sb("bo", [1, DM])
        with nc.psum_tensor("l0a_fold", [P, 512], F32) as fold, nc.Block() as block:
            w_in, fold_mm, w_done = sems(3)

            @block.sync
            def _(sp):
                sp.dma_start(w[:, :, :], d["l0a_w"]).then_inc(w_in, 16)
                sp.dma_start(la[:, :, :], d["l0a_a"]).then_inc(w_in, 16)
                sp.dma_start(lb[:, :, :], d["l0a_b"]).then_inc(w_in, 16)
                sp.dma_start(bo[:, :], d["l0a_bo"]).then_inc(w_in, 16)

            @block.tensor
            def _(pe):
                pe.wait_ge(w_in, 64)
                for n in range(4):
                    mm = nc.tensor.matmul(fold[:, n * DM:(n + 1) * DM], la[:, n, :], lb[:, n, :],
                                          start=True, stop=True)
                mm.then_inc(fold_mm, 1)

            @block.vector
            def _(dve):
                dve.wait_ge(fold_mm, 1)
                nc.vector.scalar_tensor_tensor(w[:, :, :].rearrange("p n c -> p (n c)"), fold[:, :], 1.0 / 16,
                                               w[:, :, :].rearrange("p n c -> p (n c)"),
                                               ALU.mult, ALU.add).then_inc(w_done, 1)
        sems.clear()
        small_head_attention(nc, C, sems, "l0a", src=X, dests=[X], wq=w[:, 0, :], wk=w[:, 1, :], wv=w[:, 2, :],
                             wo=w[:, 3, :], out_bias=bo[0:1, :])


def regroup(eng, per, nat, done, back=False):
    n = nat.rearrange("b (h r) (c j) -> r c (b h) j", r=8, c=16)
    p = per.rearrange("(r c) b (h j) -> r c (b h) j", r=8, h=16)
    for r in range(8):
        dst, src = (n, p) if back else (p, n)
        eng.dma_start(dst[r], src[r]).then_inc(done, 16)


def project_out_to_dram(nc, C, sems, tag, XT, w, bias, out, nat):
    with ExitStack() as x:
        Q = [x.enter_context(nc.psum_tensor(f"{tag}_Q{i}", [P, 512], F32)) for i in range(2)]
        q_mm, q_done, stored = sems(3)
        with nc.Block() as block:
            @block.tensor
            def _(pe):
                for g in range(NB // 4):
                    wait(pe, q_done, g - 1)
                    for k in range(4):
                        mm = nc.tensor.matmul(Q[g % 2][:, k * P:(k + 1) * P], tile_of(XT, 4 * g + k), w,
                                              start=True, stop=True)
                    mm.then_inc(q_mm, 1)

            @block.vector
            def _(dve):
                for g in range(NB // 4):
                    dve.wait_ge(q_mm, g + 1)
                    nc.vector.tensor_tensor(out[:, g * 512:(g + 1) * 512].rearrange("p (b n) -> p b n", b=4),
                                            Q[g % 2][:, :].rearrange("p (b n) -> p b n", b=4), bcast_mid(bias, 4),
                                            ALU.add).then_inc(q_done, 1)

            @block.sync
            def _(sp):
                for g in range(NB // 4):
                    sp.wait_ge(q_done, g + 1)
                    sp.dma_start(nat[4 * g:4 * g + 4].rearrange("b p n -> p b n"),
                                 out[:, g * 512:(g + 1) * 512].rearrange("p (b n) -> p b n", b=4)).then_inc(stored, 16)
                sp.wait_ge(stored, 16 * NB // 4)
        sems.clear()


def stage_l0_values(nc, C, sems, d, X):
    C.l0x_dram = {n: nc.dram_tensor(f"l0x_dram_{n}", (P, NB, DM) if n[1] == "p" else (NB, P, DM), F32,
                                    kind="Internal").ap() for n in ("qn", "vn", "on", "qp", "vp", "op")}
    with ExitStack() as x:
        sb = lambda n, shape: x.enter_context(nc.sbuf_tensor(f"l0v_{n}", shape, F32))
        CT = sb("CT", [P, NB * P])
        V = sb("V", [P, NB * DM])
        w = sb("w", [P, DM])
        bias = sb("bias", [P, DM])
        (w_in,) = sems(1)
        with nc.Block() as block:
            @block.sync
            def _(sp):
                sp.dma_start(CT[:, :], d["ctxT_rows"]).then_inc(w_in, 16)
                sp.dma_start(w[:, :], d["l0x_w"][:, 2, :]).then_inc(w_in, 16)
                sp.dma_start(bias[:, :], d["l0x_b"][:, 2, :].to_broadcast([P, DM])).then_inc(w_in, 16)
                sp.wait_ge(w_in, 48)
        sems.clear()
        project_out_to_dram(nc, C, sems, "l0v", CT, w[:, :], bias[:, :], V, C.l0x_dram["vn"])
        with nc.Block() as block:
            @block.sync
            def _(sp):
                regroup(sp, C.l0x_dram["vp"], C.l0x_dram["vn"], C.v_moved)


def stage_l0_xattn(nc, C, sems, d, X):
    q_nat, o_nat, q_per, v_per, o_per = [C.l0x_dram[n] for n in ("qn", "on", "qp", "vp", "op")]
    with ExitStack() as x:
        sb = lambda n, shape: x.enter_context(nc.sbuf_tensor(f"l0x_{n}", shape, F32))
        w = sb("w", [P, 4, DM])
        rows = sb("rows", [1, 4, DM])
        with ExitStack() as y:
            XT = y.enter_context(nc.sbuf_tensor("l0x_XT", [P, NB * DM], F32))
            XN = y.enter_context(nc.sbuf_tensor("l0x_XN", [P, NB * DM], F32))
            q_bias = y.enter_context(nc.sbuf_tensor("l0x_q_bias", [P, DM], F32))
            (w_in,) = sems(1)
            with nc.Block() as block:
                @block.sync
                def _(sp):
                    sp.dma_start(w[:, :, :], d["l0x_w"]).then_inc(w_in, 16)
                    sp.dma_start(rows[:, :, :], d["l0x_b"]).then_inc(w_in, 16)
                    sp.dma_start(q_bias[:, :], d["l0x_b"][:, 0, :].to_broadcast([P, DM])).then_inc(w_in, 16)
                    sp.wait_ge(w_in, 48)
            sems.clear()
            normalise_all(nc, C, sems, "l0x_n", X, XN)
            turn_all(nc, C, sems, "l0x_t", XN, XT)
            project_out_to_dram(nc, C, sems, "l0x_p", XT, w[:, 0, :], q_bias[:, :], XN, q_nat)
            (moved,) = sems(1)
            with nc.Block() as block:
                @block.sync
                def _(sp):
                    regroup(sp, q_per, q_nat, moved)
                    sp.wait_ge(moved, 8 * 16)
                    sp.wait_ge(C.v_moved, 8 * 16)
            sems.clear()
        small_head_attention(nc, C, sems, "l0x", src=None, dests=None, wq=None, wk=w[:, 1, :], wv=None, wo=None,
                             ctx_dram=d["ctxT"], k_bias=rows[:, 1, :],
                             permuted=(q_per, v_per, o_per))
        with ExitStack() as y:
            O = y.enter_context(nc.sbuf_tensor("l0x_heads", [P, NB * DM], F32))
            OT = y.enter_context(nc.sbuf_tensor("l0x_headsT", [P, NB * DM], F32))
            o_bias = y.enter_context(nc.sbuf_tensor("l0x_o_bias", [P, DM], F32))
            moved, bias_in, o_in, x_biased = sems(4)
            with nc.Block() as block:
                @block.sync
                def _(sp):
                    sp.dma_start(o_bias[:, :], d["l0x_b"][:, 3, :].to_broadcast([P, DM])).then_inc(bias_in, 16)
                    regroup(sp, o_per, o_nat, moved, back=True)
                    sp.wait_ge(moved, 8 * 16)
                    for g in range(NB // 4):
                        sp.dma_start(O[:, g * 512:(g + 1) * 512].rearrange("p (b n) -> p b n", b=4),
                                     o_nat[4 * g:4 * g + 4].rearrange("b p n -> p b n")).then_inc(o_in, 16)
                    sp.wait_ge(o_in, 16 * NB // 4)

                @block.gpsimd
                def _(pool):
                    pool.wait_ge(bias_in, 16)
                    part = X[:, :].rearrange("p (b n) -> p b n", b=NB)
                    pool.tensor_tensor(part, part, bcast_mid(o_bias[:, :], NB), ALU.add).then_inc(x_biased, 1)
            sems.clear()
            turn_all(nc, C, sems, "l0x_ot", O, OT)
            add_product(nc, C, sems, "l0x_y", OT, w[:, 3, :], X)


SLOTS = 2048
EXPERTS, PER = 64, 32


def slot_softmax(nc, C, sems, tag, X, phiT, phi_b, over, acc=None, zero=None, values=None):
    slots = over == "slots"
    with ExitStack() as x:
        sb = lambda n, shape: x.enter_context(nc.sbuf_tensor(f"{tag}_{n}", shape, F32))
        ps = lambda n: x.enter_context(nc.psum_tensor(f"{tag}_{n}", [P, 512], F32))
        ln = LayerNorm(nc, sb)
        xnT = sb("xnT", [P, 2, P])
        xk = sb("xk", [P, 2, DM])
        Z = sb("Z", [P, 2, SLOTS])
        mx = sb("mx", [P, 2, 5, 32])
        sm = sb("sm", [P, 2, 5, 32])
        T = ps("T")
        L = [ps("L0"), ps("L1")]
        if not slots:
            CT = sb("CT", [P, 4, 512])
            TP = [ps("TP0"), ps("TP1")]
            Y = ps("Y")
        (xnt_mm, xnt_done, keep_done, l_mm, add_done, part_max, max_done, sub_done, exp_done, part_sum, sum_done,
         inv_done, w_done, tail_mm, tp_mm, ct_done, x_done) = sems(17)
        ln.sems(sems)

        def quarter(s, q):
            return Z[:, s, q * 512:(q + 1) * 512].rearrange("p (e m) -> p e m", m=PER)

        def grouped(s, q):
            return quarter(s, q) if slots else quarter(s, q).rearrange("p e m -> p m e")

        def result(t, s, q):
            return t[:, s, q, 0:16] if slots else t[:, s, q, :]

        def spread(t, s, q):
            return bcast_in(t[:, s, q, 0:16], PER) if slots else bcast_mid(t[:, s, 4, :], 16)

        def whole(t, s):
            return t[:, s, 0:4, :].rearrange("p q m -> p m q")

        def finished(q):
            return (4, q + 1) if slots else (1, 1)

        with nc.Block() as block:

            @block.gpsimd
            def _(pool):
                def subtract(b, s, q):
                    wait(pool, max_done, count(b, *finished(q)))
                    pool.tensor_tensor(quarter(s, q), quarter(s, q), spread(mx, s, q), ALU.subtract).then_inc(sub_done, 1)

                def normalise(b, s, q):
                    wait(pool, inv_done, count(b, *finished(q)))
                    pool.tensor_tensor(quarter(s, q), quarter(s, q), spread(sm, s, q), ALU.mult).then_inc(w_done, 1)

                def step(b, s, tail, head, front):
                    if slots:
                        for q in range(4):
                            if front and ahead(b) and q == 1:
                                ln.rstd(pool, shift(b, 2), s, C)
                            if tail:
                                normalise(shift(b, -1), 1 - s, q)
                            if head:
                                subtract(b, s, q)
                    else:
                        for q in range(4):
                            if tail:
                                normalise(shift(b, -1), 1 - s, q)
                        for q in range(4):
                            if head:
                                subtract(b, s, q)
                        if front and ahead(b):
                            ln.rstd(pool, shift(b, 2), s, C)
                ln.rstd(pool, 0, 0, C)
                ln.rstd(pool, 1, 1, C)
                pipeline(pool, step)

            @block.tensor
            def _(pe):
                def normed_T(b, s):
                    wait(pe, xnt_done, count(b, 1, 0))
                    wait(pe, ln.done, count(b, 1, 1))
                    nc.tensor.transpose(T[:, 0:P], ln.xn[:, s, :], C.ident).then_inc(xnt_mm, 1)

                def logits(b, s, q):
                    wait(pe, xnt_done, count(b, 1, 1))
                    wait(pe, add_done, count(b, 4, q - 1))
                    nc.tensor.matmul(L[q % 2][:, :], xnT[:, s, :], phiT[:, q * 512:(q + 1) * 512],
                                     start=True, stop=True).then_inc(l_mm, 1)

                def dispatch(b, s, q):
                    wait(pe, w_done, count(b, 4, q + 1))
                    wait(pe, keep_done, count(b, 1, 1))
                    for k in range(4):
                        c = 4 * q + k
                        mm = nc.tensor.matmul(acc[q][:, k * P:(k + 1) * P], Z[:, s, c * P:(c + 1) * P],
                                              xk[:, s, :], start=False, stop=False, skip_group_check=True)
                    mm.then_inc(tail_mm, 1)

                def turn(b, s, q):
                    wait(pe, w_done, count(b, 4, q + 1))
                    wait(pe, ct_done, count(b, 4, max(q - 1, 0)))
                    for k in range(4):
                        mm = nc.tensor.transpose(TP[q % 2][:, k * P:(k + 1) * P],
                                                 Z[:, s, (4 * q + k) * P:(4 * q + k + 1) * P], C.ident)
                    mm.then_inc(tp_mm, 1)

                def combine(b, q):
                    if q == 0:
                        wait(pe, x_done, count(b, 1, 0))
                    wait(pe, ct_done, count(b, 4, q + 1))
                    for k in range(4):
                        mm = nc.tensor.matmul(Y[:, 0:DM], CT[:, q, k * P:(k + 1) * P], values[:, 4 * q + k, :],
                                              start=(q == 0 and k == 0), stop=(q == 3 and k == 3))
                    mm.then_inc(tail_mm, 1)

                def step(b, s, tail, head, front):
                    prev = shift(b, -1)
                    for q in range(4):
                        if head:
                            logits(b, s, q)
                        if front and q == 1:
                            normed_T(shift(b, 1), 1 - s)
                        if tail and slots and q > 0:
                            dispatch(prev, 1 - s, q - 1)
                    if tail and slots:
                        dispatch(prev, 1 - s, 3)
                    if tail and not slots:
                        for q in range(6):
                            if q < 4:
                                turn(prev, 1 - s, q)
                            if q > 1:
                                combine(prev, q - 2)
                if slots:
                    for k in range(4):
                        nc.tensor.matmul(acc[k][:, :], zero[:, 0:P], zero[:, :], start=True, stop=False,
                                         skip_group_check=True)
                normed_T(0, 0)
                pipeline(pe, step)

            @block.vector
            def _(dve):
                def add_max(b, s, q):
                    wait(dve, tail_mm, count(b, 4, -4))
                    wait(dve, l_mm, count(b, 4, q + 1))
                    part = slice(q * 512, (q + 1) * 512)
                    nc.vector.tensor_tensor(Z[:, s, part], L[q % 2][:, :], phi_b[:, part], ALU.add).then_inc(add_done, 1)
                    wait(dve, add_done, count(b, 4, q + 1))
                    nc.vector.tensor_reduce(result(mx, s, q), grouped(s, q), AXX,
                                            ALU.max).then_inc(max_done if slots else part_max, 1)

                def whole_max(b, s):
                    wait(dve, part_max, count(b, 4, 4))
                    nc.vector.tensor_reduce(mx[:, s, 4, :], whole(mx, s), AXX, ALU.max).then_inc(max_done, 1)

                def sums(b, s, q):
                    wait(dve, exp_done, count(b, 4, q + 1))
                    nc.vector.tensor_reduce(result(sm, s, q), grouped(s, q), AXX, ALU.add).then_inc(part_sum, 1)
                    if slots:
                        wait(dve, part_sum, count(b, 4, q + 1))
                        nc.vector.reciprocal(sm[:, s, q, 0:16], sm[:, s, q, 0:16]).then_inc(inv_done, 1)

                def whole_sum(b, s):
                    wait(dve, part_sum, count(b, 4, 4))
                    nc.vector.tensor_reduce(sm[:, s, 4, :], whole(sm, s), AXX, ALU.add).then_inc(sum_done, 1)
                    wait(dve, sum_done, count(b, 1, 1))
                    nc.vector.reciprocal(sm[:, s, 4, :], sm[:, s, 4, :]).then_inc(inv_done, 1)

                def add_x(b):
                    wait(dve, tail_mm, count(b, 4, 4))
                    nc.vector.tensor_tensor(tile_of(X, b), tile_of(X, b), Y[:, 0:DM], ALU.add).then_inc(x_done, 1)

                def scale(b, s):
                    if slots:
                        wait(dve, keep_done, count(b, 1, -1))
                    ln.scale(nc, dve, b, s, X, xnt_mm)

                def step(b, s, tail, head, front):
                    prev = shift(b, -1)
                    if front and ahead(b):
                        ln.moments_of(nc, dve, shift(b, 2), s, X)
                    for q in range(4):
                        if tail and slots:
                            sums(prev, 1 - s, q)
                        if head:
                            add_max(b, s, q)
                    if head and not slots:
                        whole_max(b, s)
                        sums(b, s, 0)
                    if tail and not slots:
                        add_x(prev)
                    if head and not slots:
                        for q in range(1, 4):
                            sums(b, s, q)
                        whole_sum(b, s)
                    if front and ahead(b):
                        scale(shift(b, 2), s)
                for n in range(2):
                    ln.moments_of(nc, dve, n, n, X)
                    scale(n, n)
                pipeline(dve, step)

            @block.scalar
            def _(act):
                def copy_normed(b, s):
                    wait(act, l_mm, count(b, 4, -4))
                    wait(act, xnt_mm, count(b, 1, 1))
                    nc.scalar.copy(xnT[:, s, :], T[:, 0:P]).then_inc(xnt_done, 1)

                def keep(b, s):
                    wait(act, tail_mm, count(b, 4, -4))
                    nc.scalar.copy(xk[:, s, :], ln.xn[:, s, :]).then_inc(keep_done, 1)

                def exps(b, s, q):
                    wait(act, sub_done, count(b, 4, q + 1))
                    nc.scalar.activation(quarter(s, q), quarter(s, q), ACT.Exp).then_inc(exp_done, 1)

                def copy_turned(b, q):
                    wait(act, tail_mm, count(b, 4, 0))
                    wait(act, tp_mm, count(b, 4, q + 1))
                    nc.scalar.copy(CT[:, q, :], TP[q % 2][:, :]).then_inc(ct_done, 1)

                def step(b, s, tail, head, front):
                    if head and slots:
                        keep(b, s)
                    if slots:
                        for q in range(4):
                            if head:
                                exps(b, s, q)
                            if front and q == 0:
                                copy_normed(shift(b, 1), 1 - s)
                    else:
                        if front:
                            copy_normed(shift(b, 1), 1 - s)
                        for q in range(4):
                            if tail:
                                copy_turned(shift(b, -1), q)
                        for q in range(4):
                            if head:
                                exps(b, s, q)
                copy_normed(0, 0)
                pipeline(act, step)
        sems.clear()


def stage_l0_ffn(nc, C, sems, d, X):
    with ExitStack() as x:
        sb = lambda n, shape: x.enter_context(nc.sbuf_tensor(f"l0f_{n}", shape, F32))
        phiT = sb("phiT", [P, SLOTS])
        phi_b = sb("phi_b", [P, SLOTS])
        zero = sb("zero", [P, 512])
        val = sb("val", [P, 16, DM])
        with ExitStack() as y:
            sy = lambda n, shape: y.enter_context(nc.sbuf_tensor(f"l0f_{n}", shape, F32))
            ps = lambda n: y.enter_context(nc.psum_tensor(f"l0f_{n}", [P, 512], F32))
            acc = [ps(f"acc{k}") for k in range(4)]
            w_in, z_done = sems(2)
            with nc.Block() as block:
                @block.sync
                def _(sp):
                    sp.dma_start(phiT[:, :], d["l0f_phiT"]).then_inc(w_in, 16)
                    sp.dma_start(phi_b[:, :], row_bcast(d["l0f_phi_b"], SLOTS)).then_inc(w_in, 16)
                    sp.wait_ge(w_in, 32)

                @block.vector
                def _(dve):
                    nc.vector.memset(zero[:, :], 0.0)
            sems.clear()
            slot_softmax(nc, C, sems, "l0f_d", X, phiT, phi_b, "slots", acc=acc, zero=zero)

            T = [ps("T0"), ps("T1")]
            Yp = [ps("Y0"), ps("Y1")]
            ew = sy("ew", [P, EXPERTS, DM])
            eb = sy("eb", [P, 16, DM])
            xt = sy("xt", [P, 16, DM])
            xtT = sy("xtT", [P, 16, P])
            st = sy("st", [P, 16, 6])
            mv = sy("mv", [P, 16, 2])
            r = sy("r", [P, 2, 16])
            (w_in, clip_done, st_done, mv_done, pad, ve_done, r_done, n_done, tanh_done, t_mm, t_done, y_mm,
             y_done) = sems(13)
            with nc.Block() as block:
                @block.sync
                def _(sp):
                    sp.dma_start(ew[:, :, :], d["l0f_ew"]).then_inc(w_in, 16)
                    eb_d = d["l0f_eb"].rearrange("(k a) h -> a k h", a=4)
                    for a in range(4):
                        sp.dma_start(eb[32 * a:32 * a + 32, :, :],
                                     eb_d[a:a + 1].to_broadcast([32, 16, DM])).then_inc(w_in, 16)

                @block.vector
                def _(dve):
                    for q in range(4):
                        nc.vector.tensor_scalar(xt[:, 4 * q:4 * q + 4, :].rearrange("p k n -> p (k n)"), acc[q][:, :],
                                                -33000.0, 65000.0, ALU.max, ALU.min).then_inc(clip_done, 1)
                    dve.wait_ge(clip_done, 4)
                    for k in range(16):
                        ins = nc.vector.bn_stats(st[:, k, :], xt[:, k, :])
                    ins.then_inc(st_done, 1)
                    dve.wait_ge(st_done, 1)
                    for k in range(16):
                        ins = nc.vector.bn_aggr(mv[:, k, :], st[:, k, :])
                    ins.then_inc(mv_done, 1)
                    dve.wait_ge(r_done, 1)
                    for k in range(16):
                        nc.vector.tensor_scalar(xt[:, k, :], xt[:, k, :], mv[:, k, 0:1], r[:, 1, k:k + 1],
                                                ALU.subtract, ALU.mult).then_inc(n_done, 1)
                    for q in range(4):
                        dve.wait_ge(y_mm, q + 1)
                        part = slice(4 * q, 4 * q + 4)
                        if q == 0:
                            dve.wait_ge(w_in, 80)
                        nc.vector.tensor_tensor(val[:, part, :].rearrange("p k h -> p (k h)"), Yp[q % 2][:, :],
                                                eb[:, part, :].rearrange("p k h -> p (k h)"),
                                                ALU.add).then_inc(y_done, 1)

                @block.gpsimd
                def _(pool):
                    pool.wait_ge(mv_done, 1)
                    pool.tensor_tensor(r[:, 0, :], mv[:, :, 1], C.eps.to_broadcast([P, 16]), ALU.add).then_inc(ve_done, 1)
                    pool.wait_ge(ve_done, 1)
                    pool.tensor_tensor(r[:, 1, :], r[:, 0, :], C.neghalf.to_broadcast([P, 16]),
                                       ALU.pow).then_inc(r_done, 1)

                @block.scalar
                def _(act):
                    for q in range(5):
                        if q < 4:
                            act.wait_ge(n_done, 4 * q + 4)
                            part = xt[:, 4 * q:4 * q + 4, :]
                            nc.scalar.activation(part, part, ACT.Tanh).then_inc(tanh_done, 1)
                        if q > 0:
                            act.wait_ge(t_mm, q)
                            nc.scalar.copy(xtT[:, 4 * q - 4:4 * q, :].rearrange("p k n -> p (k n)"),
                                           T[(q - 1) % 2][:, :]).then_inc(t_done, 1)

                @block.tensor
                def _(pe):
                    for q in range(5):
                        if q < 4:
                            pe.wait_ge(tanh_done, q + 1)
                            if q >= 2:
                                pe.wait_ge(t_done, q - 1)
                            for k in range(4):
                                mm = nc.tensor.transpose(T[q % 2][:, k * P:(k + 1) * P], xt[:, 4 * q + k, :], C.ident)
                            mm.then_inc(t_mm, 1)
                        if q > 0:
                            pe.wait_ge(t_done, q)
                            if q == 1:
                                pe.wait_ge(w_in, 80)
                            if q >= 3:
                                pe.wait_ge(y_done, q - 2)
                            for k in range(4):
                                for a in range(4):
                                    n = 16 * (q - 1) + 4 * k + a
                                    mm = nc.tensor.matmul(Yp[(q - 1) % 2][32 * a:32 * a + 32, k * P:(k + 1) * P],
                                                          xtT[:, n // 4, 32 * a:32 * a + 32], ew[:, n, :],
                                                          start=True, stop=True)
                            mm.then_inc(y_mm, 1)
            sems.clear()
        slot_softmax(nc, C, sems, "l0f_c", X, phiT, phi_b, "experts", values=val)


def linear_attention(nc, C, sems, tag, X, w, woT, kind, w0=None, wg=None, gamma=None, beta=None):
    delta = kind == "delta"
    with ExitStack() as x:
        sb = lambda n, shape: x.enter_context(nc.sbuf_tensor(f"{tag}_{n}", shape, F32))
        ps = lambda n: x.enter_context(nc.psum_tensor(f"{tag}_{n}", [P, 512], F32))
        ln = LayerNorm(nc, sb)
        xb = sb("xb", [P, 2, 3 + P])
        raw = sb("raw", [P, 2, 3 * P])
        low = sb("low", [P, 2 * P])
        inv = sb("inv", [P, 2, 32])
        qkT = sb("qkT", [P, 2, 2 * P])
        gate = sb("gate", [P, 2, P])
        gate_kept = sb("gate_kept", [P, P])
        gg = sb("gg", [P, P])
        gbeta = sb("gbeta", [P, P])
        Qexp = sb("Qexp", [P, 2, 16, P])
        PT = sb("PT", [P, 2, 16, P])
        nd = sb("nd", [P, 2, 4, P])
        small = sb("small", [P, 4, 16])
        oc = sb("oc", [P, P])
        osq = sb("osq", [P, P])
        oT = sb("oT", [P, P])
        A, T, S, NUM, DEN, O, Y = ps("A"), ps("T"), [ps("S0"), ps("S1")], ps("NUM"), ps("DEN"), ps("O"), ps("Y")
        (xnt_mm, xnt_done, proj_mm, raw_done, sq_done, ssum_done, root_done, inv_done, unit_done, qkt_mm,
         qk_done, low_done, low_exp, qexp_done, s_mm, p_done, pv_mm, nd_done, o_mm, mean_done, oc_done,
         osq_done, var_done, keep_done, r_done, on_done, ot_mm, ot_done, y_mm, x_done, zeros_done, dev_done, affine, gates_done) = sems(34)
        ln.sems(sems)
        heads = lambda ap: ap.rearrange("p (h n) -> p h n", n=8)

        with nc.Block() as block:

            @block.gpsimd
            def _(pool):
                def square(b, s):
                    wait(pool, raw_done, count(b, 1, 1))
                    wait(pool, ssum_done, count(b, 1, 0))
                    pool.tensor_tensor(low[:, :], raw[:, s, 0:2 * P], raw[:, s, 0:2 * P], ALU.mult).then_inc(sq_done, 1)

                def spread(b, s):
                    wait(pool, s_mm, count(b, 4, -4))
                    if delta:
                        wait(pool, pv_mm, count(b, 1, -1))
                    wait(pool, qk_done, count(b, 1, 1))
                    for q in range(4):
                        quad = slice(4 * q, 4 * q + 4)
                        pool.tensor_tensor(Qexp[:, s, quad, :], bcast_mid(qkT[:, s, 0:P], 4),
                                           bcast_in(C.hmask[:, quad], P), ALU.mult).then_inc(qexp_done, 1)

                def square_centred(b):
                    wait(pool, oc_done, count(b, 1, 1))
                    pool.tensor_tensor(osq[:, :], oc[:, :], oc[:, :], ALU.mult).then_inc(osq_done, 1)

                def gate_affine(b):
                    wait(pool, on_done, count(b, 1, 0))
                    wait(pool, keep_done, count(b, 1, 1))
                    pool.tensor_tensor(heads(gg[:, :]), heads(gate_kept[:, :]), bcast_mid(gamma, 16), ALU.mult)
                    pool.tensor_tensor(heads(gbeta[:, :]), heads(gate_kept[:, :]), bcast_mid(beta, 16),
                                       ALU.mult).then_inc(gates_done, 1)

                def step(b, s, tail, head, front):
                    if tail and delta:
                        gate_affine(shift(b, -1))
                    if front and delta:
                        square(shift(b, 1), 1 - s)
                    if front and ahead(b):
                        ln.rstd(pool, shift(b, 2), s, C)
                    if tail and delta:
                        square_centred(shift(b, -1))
                    if front:
                        spread(shift(b, 1), 1 - s)
                for n in range(2):
                    ln.rstd(pool, n, n, C)
                if delta:
                    square(0, 0)
                spread(0, 0)
                pipeline(pool, step)

            @block.tensor
            def _(pe):
                def normed_T(b, s):
                    wait(pe, xnt_done, count(b, 1, 0))
                    wait(pe, qk_done, count(b, 1, 0))
                    wait(pe, ln.done, count(b, 1, 1))
                    nc.tensor.transpose(T[:, 0:P], ln.xn[:, s, :], C.ident).then_inc(xnt_mm, 1)

                def project(b, s):
                    wait(pe, raw_done, count(b, 1, 0))
                    wait(pe, xnt_done, count(b, 1, 1))
                    xT = xb[:, s, 3:3 + P]
                    if delta:
                        if isinstance(b, int) and b == 0:
                            pe.wait_ge(zeros_done, 1)
                        nc.tensor.matmul(A[:, 3 * P:4 * P], xT, wg, start=True, stop=True)
                        for j in range(4):
                            mm = nc.tensor.matmul(A[:, 0:3 * P], xb[:, s, j:j + P], w[:, j, :], start=(j == 0),
                                                  stop=(j == 3))
                    else:
                        nc.tensor.matmul(A[:, 0:P], w[:, 0:P], xT, start=True, stop=True)
                        nc.tensor.matmul(A[:, P:2 * P], w[:, P:2 * P], xT, start=True, stop=True)
                        mm = nc.tensor.matmul(A[:, 2 * P:3 * P], xT, w[:, 2 * P:3 * P], start=True, stop=True)
                    mm.then_inc(proj_mm, 1)

                def turn_qk(b, s):
                    wait(pe, unit_done, count(b, 1, 1))
                    nc.tensor.transpose(T[:, P:2 * P], raw[:, s, 0:P], C.ident)
                    nc.tensor.transpose(T[:, 2 * P:3 * P], raw[:, s, P:2 * P], C.ident).then_inc(qkt_mm, 1)

                def weights(b, s, q):
                    wait(pe, qexp_done, count(b, 4, q + 1))
                    wait(pe, p_done, count(b, 4, q - 1))
                    nc.tensor.matmul(S[q % 2][:, :], qkT[:, s, P:2 * P],
                                     Qexp[:, s, 4 * q:4 * q + 4, :].rearrange("p h k -> p (h k)"),
                                     start=True, stop=True).then_inc(s_mm, 1)

                def sum_keys(b, s):
                    wait(pe, nd_done, count(b, 1, 0))
                    wait(pe, p_done, count(b, 4, 4))
                    quad = lambda t, q: t[:, s, 4 * q:4 * q + 4, :].rearrange("p h k -> p (h k)")
                    for q in range(4):
                        mm = nc.tensor.matmul(NUM[32 * q:32 * q + 32, :],
                                              raw[:, s, 2 * P + 32 * q:2 * P + 32 * q + 32],
                                              quad(PT, q), start=True, stop=not delta)
                    for q in range(4):
                        if delta:
                            mm = nc.tensor.matmul(NUM[32 * q:32 * q + 32, :], w0[:, 32 * q:32 * q + 32],
                                                  quad(Qexp, q), start=False, stop=True)
                        else:
                            mm = nc.tensor.matmul(DEN[32 * q:32 * q + 32, :], C.ones[:, 0:32], quad(PT, q),
                                                  start=True, stop=True)
                    mm.then_inc(pv_mm, 1)

                def gather_heads(b):
                    wait(pe, on_done, count(b, 1, 0))
                    wait(pe, nd_done, count(b, 1, 1))
                    for n in range(1 if delta else 2):
                        for j in range(4):
                            mm = nc.tensor.matmul(O[:, n * P:(n + 1) * P], nd[:, n, j, :], C.id4[:, j * P:(j + 1) * P],
                                                  start=(j == 0), stop=(j == 3))
                    mm.then_inc(o_mm, 1)

                def project_out(b):
                    wait(pe, x_done, count(b, 1, 0))
                    wait(pe, on_done, count(b, 1, 1))
                    nc.tensor.transpose(Y[:, 0:P], oc[:, :], C.ident).then_inc(ot_mm, 1)
                    wait(pe, ot_done, count(b, 1, 1))
                    nc.tensor.matmul(Y[:, P:2 * P], oT[:, :], woT, start=True, stop=True).then_inc(y_mm, 1)

                def step(b, s, tail, head, front):
                    prev, nxt = shift(b, -1), shift(b, 1)
                    if head:
                        weights(b, s, 0)
                    if front:
                        normed_T(nxt, 1 - s)
                    if head:
                        weights(b, s, 1)
                    if front and delta:
                        project(nxt, 1 - s)
                    if tail:
                        sum_keys(prev, 1 - s)
                    if front and not delta:
                        project(nxt, 1 - s)
                    if head:
                        weights(b, s, 2)
                    if tail:
                        gather_heads(prev)
                    if head:
                        weights(b, s, 3)
                    if front and delta:
                        turn_qk(nxt, 1 - s)
                    if tail:
                        project_out(prev)
                normed_T(0, 0)
                project(0, 0)
                if delta:
                    turn_qk(0, 0)
                pipeline(pe, step)

            @block.vector
            def _(dve):
                def lengths(b, s):
                    wait(dve, sq_done, count(b, 1, 1))
                    nc.vector.tensor_reduce(inv[:, s, :], heads(low[:, :]), AXX, ALU.add).then_inc(ssum_done, 1)

                def unit(b, s):
                    wait(dve, root_done, count(b, 1, 1))
                    nc.vector.reciprocal(inv[:, s, :], inv[:, s, :]).then_inc(inv_done, 1)
                    wait(dve, inv_done, count(b, 1, 1))
                    qk = heads(raw[:, s, 0:2 * P])
                    nc.vector.tensor_tensor(qk, qk, bcast_in(inv[:, s, :], 8), ALU.mult).then_inc(unit_done, 1)

                def below(b, s):
                    wait(dve, raw_done, count(b, 1, 1))
                    nc.vector.tensor_scalar(low[:, :], raw[:, s, 0:2 * P], 0.0, None, ALU.min).then_inc(low_done, 1)

                def phi(b, s):
                    wait(dve, s_mm, count(b, 4, -4))
                    wait(dve, qexp_done, count(b, 4, -4))
                    wait(dve, low_exp, count(b, 1, 1))
                    nc.vector.scalar_tensor_tensor(qkT[:, s, :], raw[:, s, 0:2 * P], 0.0, low[:, :], ALU.max,
                                                   ALU.add).then_inc(qk_done, 1)

                def mask(b, s, q):
                    if q == 0:
                        wait(dve, pv_mm, count(b, 1, -1))
                    wait(dve, s_mm, count(b, 4, q + 1))
                    nc.vector.tensor_tensor(PT[:, s, 4 * q:4 * q + 4, :],
                                            S[q % 2][:, :].rearrange("p (h k) -> p h k", h=4),
                                            bcast_mid(C.tri, 4), ALU.mult).then_inc(p_done, 1)

                def divide(b):
                    wait(dve, o_mm, count(b, 1, 1))
                    nc.vector.tensor_scalar(small[:, 0, :], heads(O[:, P:2 * P])[:, :, 0], 1e-6, None,
                                            ALU.max).then_inc(mean_done, 1)
                    wait(dve, mean_done, count(b, 1, 1))
                    nc.vector.reciprocal(small[:, 1, :], small[:, 0, :]).then_inc(var_done, 1)
                    wait(dve, ot_mm, count(b, 1, 0))
                    wait(dve, var_done, count(b, 1, 1))
                    nc.vector.tensor_tensor(heads(oc[:, :]), heads(O[:, 0:P]), bcast_in(small[:, 1, :], 8),
                                            ALU.mult).then_inc(on_done, 1)

                def centre(b):
                    wait(dve, o_mm, count(b, 1, 1))
                    nc.vector.tensor_reduce(small[:, 0, :], heads(O[:, 0:P]), AXX, ALU.add).then_inc(mean_done, 1)
                    wait(dve, ot_mm, count(b, 1, 0))
                    wait(dve, mean_done, count(b, 1, 1))
                    nc.vector.scalar_tensor_tensor(heads(oc[:, :]), bcast_in(small[:, 0, :], 8), -1.0 / 8,
                                                   heads(O[:, 0:P]), ALU.mult, ALU.add).then_inc(oc_done, 1)

                def variance(b):
                    wait(dve, osq_done, count(b, 1, 1))
                    nc.vector.tensor_reduce(small[:, 1, :], heads(osq[:, :]), AXX, ALU.add).then_inc(var_done, 1)

                def invert_deviation(b):
                    wait(dve, dev_done, count(b, 1, 1))
                    nc.vector.reciprocal(small[:, 3, :], small[:, 2, :]).then_inc(r_done, 1)

                def head_affine(b):
                    wait(dve, r_done, count(b, 1, 1))
                    nc.vector.tensor_tensor(heads(oc[:, :]), heads(oc[:, :]), bcast_in(small[:, 3, :], 8),
                                            ALU.mult).then_inc(affine, 1)
                    wait(dve, gates_done, count(b, 1, 1))
                    wait(dve, affine, count(b, 2, 1))
                    nc.vector.tensor_tensor(oc[:, :], oc[:, :], gg[:, :], ALU.mult).then_inc(affine, 1)
                    wait(dve, affine, count(b, 2, 2))
                    nc.vector.tensor_tensor(oc[:, :], oc[:, :], gbeta[:, :], ALU.add).then_inc(on_done, 1)

                def add(b):
                    wait(dve, y_mm, count(b, 1, 1))
                    nc.vector.tensor_tensor(tile_of(X, b), tile_of(X, b), Y[:, P:2 * P], ALU.add).then_inc(x_done, 1)

                def step(b, s, tail, head, front):
                    prev, nxt = shift(b, -1), shift(b, 1)
                    if head:
                        mask(b, s, 0)
                        mask(b, s, 1)
                    if front and ahead(b):
                        ln.moments_of(nc, dve, shift(b, 2), s, X)
                    if front:
                        (lengths if delta else below)(nxt, 1 - s)
                    if head:
                        mask(b, s, 2)
                    if tail:
                        (centre if delta else divide)(prev)
                    if front:
                        (unit if delta else phi)(nxt, 1 - s)
                    if tail and delta:
                        variance(prev)
                    if head:
                        mask(b, s, 3)
                    if tail and delta:
                        invert_deviation(prev)
                        head_affine(prev)
                    if front and ahead(b):
                        ln.scale(nc, dve, shift(b, 2), s, X, xnt_mm)
                    if tail:
                        add(prev)
                if delta:
                    nc.vector.memset(xb[:, :, 0:3], 0.0).then_inc(zeros_done, 1)
                for n in range(2):
                    ln.moments_of(nc, dve, n, n, X)
                    ln.scale(nc, dve, n, n, X, xnt_mm)
                (lengths if delta else below)(0, 0)
                (unit if delta else phi)(0, 0)
                pipeline(dve, step)

            @block.scalar
            def _(act):
                def copy_normed(b, s):
                    wait(act, proj_mm, count(b, 1, -1))
                    wait(act, xnt_mm, count(b, 1, 1))
                    nc.scalar.copy(xb[:, s, 3:3 + P], T[:, 0:P]).then_inc(xnt_done, 1)

                def copy_raw(b, s):
                    wait(act, pv_mm, count(b, 1, -1))
                    wait(act, proj_mm, count(b, 1, 1))
                    if delta:
                        wait(act, keep_done, count(b, 1, -1))
                        wait(act, qkt_mm, count(b, 1, -1))
                        nc.scalar.copy(gate[:, s, :], A[:, 3 * P:4 * P])
                        nc.scalar.activation(raw[:, s, :], A[:, 0:3 * P], ACT.Silu).then_inc(raw_done, 1)
                    else:
                        wait(act, qk_done, count(b, 1, -1))
                        nc.scalar.copy(raw[:, s, :], A[:, 0:3 * P]).then_inc(raw_done, 1)

                def keep_gate(b, s):
                    wait(act, gates_done, count(b, 1, 0))
                    nc.scalar.copy(gate_kept[:, :], gate[:, s, :]).then_inc(keep_done, 1)

                def root_lengths(b, s):
                    wait(act, ssum_done, count(b, 1, 1))
                    nc.scalar.activation(inv[:, s, :], inv[:, s, :], ACT.Sqrt, bias=C.l2eps).then_inc(root_done, 1)

                def deviation(b):
                    wait(act, var_done, count(b, 1, 1))
                    nc.scalar.activation(small[:, 2, :], small[:, 1, :], ACT.Sqrt, bias=C.eps,
                                         scale=1.0 / 8).then_inc(dev_done, 1)

                def exp_low(b):
                    wait(act, low_done, count(b, 1, 1))
                    nc.scalar.activation(low[:, :], low[:, :], ACT.Exp).then_inc(low_exp, 1)

                def copy_qk(b, s):
                    wait(act, s_mm, count(b, 4, -4))
                    wait(act, qexp_done, count(b, 4, -4))
                    wait(act, qkt_mm, count(b, 1, 1))
                    nc.scalar.copy(qkT[:, s, :], T[:, P:3 * P]).then_inc(qk_done, 1)

                def copy_sums(b):
                    wait(act, o_mm, count(b, 1, 0))
                    wait(act, pv_mm, count(b, 1, 1))
                    flat = lambda t: t.rearrange("p j q -> p (j q)")
                    ins = nc.scalar.copy(flat(nd[:, 0, :, :]), NUM[:, :])
                    if not delta:
                        ins = nc.scalar.copy(flat(nd[:, 1, :, :]), DEN[:, :])
                    ins.then_inc(nd_done, 1)

                def copy_out(b):
                    wait(act, y_mm, count(b, 1, 0))
                    wait(act, ot_mm, count(b, 1, 1))
                    nc.scalar.copy(oT[:, :], Y[:, 0:P]).then_inc(ot_done, 1)

                def step(b, s, tail, head, front):
                    prev, nxt = shift(b, -1), shift(b, 1)
                    if tail and delta:
                        keep_gate(prev, 1 - s)
                    if front:
                        copy_normed(nxt, 1 - s)
                    if front and delta:
                        copy_raw(nxt, 1 - s)
                    if tail:
                        copy_sums(prev)
                    if front and not delta:
                        copy_raw(nxt, 1 - s)
                    if front:
                        (root_lengths(nxt, 1 - s) if delta else exp_low(nxt))
                    if tail and delta:
                        deviation(prev)
                    if front and delta:
                        copy_qk(nxt, 1 - s)
                    if tail:
                        copy_out(prev)
                copy_normed(0, 0)
                copy_raw(0, 0)
                if delta:
                    root_lengths(0, 0)
                    copy_qk(0, 0)
                else:
                    exp_low(0)
                pipeline(act, step)
        sems.clear()


def stage_l1_attn(nc, C, sems, d, X):
    with ExitStack() as x:
        sb = lambda n, shape: x.enter_context(nc.sbuf_tensor(f"l1a_{n}", shape, F32))
        w = sb("w", [P, 5, DM])
        taps = sb("taps", [P, 4, 3 * DM])
        conv = sb("conv", [P, 4, 3 * DM])
        w0 = sb("w0", [P, P])
        gb = sb("gb", [P, 2, 8])
        w_in, t_done = sems(2)
        with nc.Block() as block:
            @block.sync
            def _(sp):
                sp.dma_start(w[:, :, :], d["l1a_w"]).then_inc(w_in, 16)
                sp.dma_start(conv[:, :, :].rearrange("p j n -> p (j n)"), row_bcast(d["l1a_conv"], 12 * DM)).then_inc(w_in, 16)
                sp.dma_start(w0[:, :], d["l1a_w0"]).then_inc(w_in, 16)
                sp.dma_start(gb[:, :, :].rearrange("p j n -> p (j n)"), row_bcast(d["l1a_gb"], 16)).then_inc(w_in, 16)

            @block.vector
            def _(dve):
                dve.wait_ge(w_in, 64)
                wt = w[:, 0:3, :].rearrange("p n c -> p (n c)")
                for j in range(4):
                    ins = nc.vector.tensor_tensor(taps[:, j, :], wt, conv[:, j, :], ALU.mult)
                ins.then_inc(t_done, 1)
                dve.wait_ge(t_done, 1)
                nc.vector.tensor_tensor(taps[:, 3, :], taps[:, 3, :], wt, ALU.add)
        sems.clear()
        linear_attention(nc, C, sems, "l1a", X, taps, w[:, 4, :], "delta", w0=w0, wg=w[:, 3, :],
                         gamma=gb[:, 0, :], beta=gb[:, 1, :])


def stage_l2_attn(nc, C, sems, d, X):
    with ExitStack() as x:
        sb = lambda n, shape: x.enter_context(nc.sbuf_tensor(f"l2a_{n}", shape, F32))
        w = sb("w", [P, 4 * DM])
        (w_in,) = sems(1)
        with nc.Block() as block:
            @block.sync
            def _(sp):
                sp.dma_start(w[:, :], d["l2a_w"]).then_inc(w_in, 16)
                sp.wait_ge(w_in, 16)
        sems.clear()
        linear_attention(nc, C, sems, "l2a", X, w, w[:, 3 * DM:4 * DM], "phi")


def wide_head_attention(nc, C, sems, tag, X, wq, wk, wv, wf, scale, out_bias=None, ctx_dram=None,
                        q_bias=None, k_bias=None):
    with ExitStack() as x:
        sb = lambda n, shape: x.enter_context(nc.sbuf_tensor(f"{tag}_{n}", shape, F32))
        ps = lambda n: x.enter_context(nc.psum_tensor(f"{tag}_{n}", [P, 512], F32))
        ln = LayerNorm(nc, sb)
        xnT = sb("xnT", [P, 2, P])
        ctxT = sb("ctxT", [P, 2, P])
        qT = sb("qT", [P, 2, 8, P])
        Kexp = sb("Kexp", [P, 2, 8, 2, P])
        V = sb("V", [P, 2, 8 * P])
        Sx = sb("Sx", [P, 2, 16, P])
        nmx = sb("nmx", [P, 2, 16])
        sm = sb("sm", [P, 2, 16])
        PT = sb("PT", [P, 2, 4, P])
        oT = sb("oT", [P, 8, P])
        A, S, TP, NUM, TO = [ps("A0"), ps("A1")], [ps("S0"), ps("S1")], ps("TP"), [ps("N0"), ps("N1")], ps("TO")
        (zeros_done, xnt_mm, xnt_done, ctx_in0, ctx_in1, proj_mm, q_done, k_done, v_done, s_mm, add_done, max_done,
         exp_done, inv_done, w_done, tp_mm, pt_done, pv_mm, num_done, y_mm, x_done) = sems(21)
        ctx_in = [ctx_in0, ctx_in1]
        ln.sems(sems)
        flat = lambda t: t.rearrange("p h k -> p (h k)")
        quad = lambda t, s, q: t[:, s, 4 * q:4 * q + 4, :]

        with nc.Block() as block:

            @block.sync
            def _(sp):
                def load_ctx(b, s):
                    wait(sp, proj_mm, count(b, 6, -6))
                    sp.dma_start(ctxT[:, s, :], dram_of(ctx_dram, b)).then_inc(ctx_in[s], 16)
                if ctx_dram is not None:
                    each(sp, load_ctx)

            @block.gpsimd
            def _(pool):
                def normalise(b, s, q):
                    wait(pool, inv_done, count(b, 4, q + 1))
                    pool.tensor_tensor(quad(Sx, s, q), quad(Sx, s, q), bcast_in(sm[:, s, 4 * q:4 * q + 4], P),
                                       ALU.mult).then_inc(w_done, 1)

                def step(b, s, tail, head, front):
                    if tail:
                        normalise(shift(b, -1), 1 - s, 3)
                    if front and ahead(b):
                        ln.rstd(pool, shift(b, 2), s, C)
                    if head:
                        for q in range(3):
                            normalise(b, s, q)
                pool.memset(Kexp[:, :, :, :, :], 0.0).then_inc(zeros_done, 1)
                ln.rstd(pool, 0, 0, C)
                ln.rstd(pool, 1, 1, C)
                pipeline(pool, step)

            @block.tensor
            def _(pe):
                def normed_T(b, s):
                    wait(pe, x_done, count(b, 1, -2))
                    wait(pe, ln.done, count(b, 1, 1))
                    nc.tensor.transpose(TO[:, P:2 * P], ln.xn[:, s, :], C.ident).then_inc(xnt_mm, 1)

                def project_q(b, s):
                    wait(pe, xnt_done, count(b, 1, 1))
                    wait(pe, v_done, count(b, 2, 0))
                    for n in range(2):
                        for c in range(4 * n, 4 * n + 4):
                            mm = nc.tensor.matmul(A[n][:, (c % 4) * P:(c % 4 + 1) * P], wq[:, c * P:(c + 1) * P],
                                                  xnT[:, s, :], start=True, stop=True)
                        mm.then_inc(proj_mm, 1)

                def project_k(b, s):
                    if ctx_dram is not None:
                        wait(pe, ctx_in[s], count_own(b, 16, 16))
                    for n in range(2):
                        wait(pe, q_done, count(b, 2, n + 1))
                        for c in range(4 * n, 4 * n + 4):
                            mm = nc.tensor.matmul(A[n][:, (c % 4) * P:(c % 4 + 1) * P], wk[:, c * P:(c + 1) * P],
                                                  (xnT if ctx_dram is None else ctxT)[:, s, :], start=True, stop=True)
                        mm.then_inc(proj_mm, 1)

                def project_v(b, s, n):
                    wait(pe, k_done, count(b, 2, n + 1))
                    nc.tensor.matmul(A[n][:, :], (xnT if ctx_dram is None else ctxT)[:, s, :],
                                     wv[:, n * 512:(n + 1) * 512], start=True, stop=True).then_inc(proj_mm, 1)

                def scores(b, s, q):
                    wait(pe, add_done, count(b, 4, q - 1))
                    for c in (2 * q, 2 * q + 1):
                        mm = nc.tensor.matmul(S[q % 2][:, (c % 2) * 256:(c % 2) * 256 + 256], qT[:, s, c, :],
                                              Kexp[:, s, c, :, :].rearrange("p h k -> p (h k)"), start=True, stop=True)
                    mm.then_inc(s_mm, 1)

                def turn(b, s, q):
                    wait(pe, pt_done, count(b, 4, q))
                    wait(pe, w_done, count(b, 4, q + 1))
                    for h in range(4):
                        mm = nc.tensor.transpose(TP[:, h * P:(h + 1) * P], Sx[:, s, 4 * q + h, :], C.ident)
                    mm.then_inc(tp_mm, 1)

                def sum_keys(b, s, q):
                    if q == 0:
                        wait(pe, num_done, count(b, 2, 0))
                    wait(pe, pt_done, count(b, 4, q + 1))
                    for h in range(4 * q, 4 * q + 4):
                        r, c = 64 * (h % 2), h // 2
                        mm = nc.tensor.matmul(NUM[q // 2][r:r + 64, (c % 4) * P:(c % 4 + 1) * P],
                                              V[:, s, h * 64:h * 64 + 64], PT[:, q % 2, h % 4, :],
                                              start=True, stop=True)
                    mm.then_inc(pv_mm, 1)

                def project_out(b):
                    wait(pe, xnt_done, min(b + 2, NB) if isinstance(b, int) else count(b, 1, 2))
                    wait(pe, num_done, count(b, 2, 2))
                    if out_bias is not None:
                        nc.tensor.matmul(TO[:, 0:P], C.ones[0:1, :], out_bias, start=True, stop=False)
                    for c in range(8):
                        mm = nc.tensor.matmul(TO[:, 0:P], oT[:, c, :], wf[:, c, :],
                                              start=(c == 0 and out_bias is None), stop=(c == 7))
                    mm.then_inc(y_mm, 1)

                def step(b, s, tail, head, front):
                    prev, nxt = shift(b, -1), shift(b, 1)
                    for q in range(4):
                        if head:
                            scores(b, s, q)
                        if front and q == 0:
                            normed_T(nxt, 1 - s)
                        if tail:
                            turn(prev, 1 - s, q)
                            if q > 0:
                                sum_keys(prev, 1 - s, q - 1)
                        if front and q in (1, 2):
                            (project_q, project_k)[q - 1](nxt, 1 - s)
                    if front:
                        project_v(nxt, 1 - s, 0)
                    if tail:
                        sum_keys(prev, 1 - s, 3)
                    if front:
                        project_v(nxt, 1 - s, 1)
                    if tail:
                        project_out(prev)
                normed_T(0, 0)
                project_q(0, 0)
                project_k(0, 0)
                for n in range(2):
                    project_v(0, 0, n)
                pipeline(pe, step)

            @block.vector
            def _(dve):
                def copy_keys(b, s):
                    wait(dve, s_mm, count(b, 4, -4))
                    if isinstance(b, int) and b == 0:
                        dve.wait_ge(zeros_done, 1)
                    for n in range(2):
                        wait(dve, proj_mm, count(b, 6, 3 + n))
                        for h in range(2):
                            rows = slice(64 * h, 64 * h + 64)
                            src = A[n][rows, :].rearrange("p (c k) -> p c k", c=4)
                            dst = Kexp[rows, s, 4 * n:4 * n + 4, h, :]
                            if k_bias is None:
                                ins = nc.vector.tensor_copy(dst, src)
                            else:
                                ins = nc.vector.tensor_tensor(dst, src, bcast_in(k_bias[rows, 4 * n:4 * n + 4], P),
                                                              ALU.add)
                        ins.then_inc(k_done, 1)

                def mask_max(b, s, q):
                    if q == 0:
                        wait(dve, tp_mm, count(b, 4, -4))
                    wait(dve, s_mm, count(b, 4, q + 1))
                    nc.vector.tensor_tensor(quad(Sx, s, q), S[q % 2][:, :].rearrange("p (h k) -> p h k", h=4),
                                            bcast_mid(C.causal, 4), ALU.add).then_inc(add_done, 1)
                    wait(dve, add_done, count(b, 4, q + 1))
                    nc.vector.tensor_reduce(nmx[:, s, 4 * q:4 * q + 4], quad(Sx, s, q), AXX, ALU.max, None, None,
                                            True).then_inc(max_done, 1)

                def invert(b, s, q):
                    wait(dve, exp_done, count(b, 4, q + 1))
                    part = sm[:, s, 4 * q:4 * q + 4]
                    nc.vector.reciprocal(part, part).then_inc(inv_done, 1)

                def add(b):
                    wait(dve, y_mm, count(b, 1, 1))
                    nc.vector.tensor_tensor(tile_of(X, b), tile_of(X, b), TO[:, 0:P], ALU.add).then_inc(x_done, 1)

                def step(b, s, tail, head, front):
                    prev, nxt = shift(b, -1), shift(b, 1)
                    if tail:
                        invert(prev, 1 - s, 3)
                    if front and ahead(b):
                        ln.moments_of(nc, dve, shift(b, 2), s, X)
                    for q in range(4):
                        if head:
                            mask_max(b, s, q)
                            if q > 0:
                                invert(b, s, q - 1)
                        if front and ahead(b) and q == 1:
                            ln.scale(nc, dve, shift(b, 2), s, X, xnt_mm)
                        if front and q == 2:
                            copy_keys(nxt, 1 - s)
                    if tail:
                        add(prev)
                for n in range(2):
                    ln.moments_of(nc, dve, n, n, X)
                    ln.scale(nc, dve, n, n, X, xnt_mm)
                copy_keys(0, 0)
                pipeline(dve, step)

            @block.scalar
            def _(act):
                def copy_normed(b, s):
                    wait(act, proj_mm, count(b, 6, -6))
                    wait(act, xnt_mm, count(b, 1, 1))
                    nc.scalar.copy(xnT[:, s, :], TO[:, P:2 * P]).then_inc(xnt_done, 1)

                def copy_q(b, s):
                    wait(act, s_mm, count(b, 4, -4))
                    for n in range(2):
                        wait(act, proj_mm, count(b, 6, 1 + n))
                        if q_bias is None:
                            ins = nc.scalar.activation(flat(qT[:, s, 4 * n:4 * n + 4, :]), A[n][:, :], ACT.Copy,
                                                       scale=scale)
                        else:
                            for c in range(4 * n, 4 * n + 4):
                                ins = nc.scalar.activation(qT[:, s, c, :], A[n][:, (c % 4) * P:(c % 4 + 1) * P],
                                                           ACT.Identity, bias=q_bias[:, c:c + 1], scale=scale)
                        ins.then_inc(q_done, 1)

                def copy_v(b, s, n):
                    wait(act, pv_mm, count(b, 4, -4))
                    wait(act, proj_mm, count(b, 6, 5 + n))
                    nc.scalar.copy(V[:, s, n * 512:(n + 1) * 512], A[n][:, :]).then_inc(v_done, 1)

                def exps(b, s, q):
                    if q == 0:
                        wait(act, w_done, count(b, 4, -4))
                    wait(act, max_done, count(b, 4, q + 1))
                    for h in range(4 * q, 4 * q + 4):
                        ins = nc.scalar.activation(Sx[:, s, h, :], Sx[:, s, h, :], ACT.Exp, bias=nmx[:, s, h:h + 1],
                                                   accum_out=sm[:, s, h:h + 1])
                    ins.then_inc(exp_done, 1)

                def copy_turned(b, q):
                    wait(act, pv_mm, count(b, 4, max(q - 1, 0)))
                    wait(act, tp_mm, count(b, 4, q + 1))
                    nc.scalar.copy(flat(PT[:, q % 2, :, :]), TP[:, :]).then_inc(pt_done, 1)

                def copy_sum(b, n):
                    wait(act, y_mm, count(b, 1, 0))
                    wait(act, pv_mm, count(b, 4, 2 * n + 2))
                    nc.scalar.copy(flat(oT[:, 4 * n:4 * n + 4, :]), NUM[n][:, :]).then_inc(num_done, 1)

                def step(b, s, tail, head, front):
                    prev, nxt = shift(b, -1), shift(b, 1)
                    for q in range(4):
                        if tail:
                            copy_turned(prev, q)
                        if front and q == 0:
                            copy_normed(nxt, 1 - s)
                        if tail and q == 3:
                            copy_sum(prev, 0)
                        if front and q == 3:
                            copy_v(nxt, 1 - s, 0)
                        if tail and q == 3:
                            copy_sum(prev, 1)
                        if head:
                            exps(b, s, q)
                        if front and q == 1:
                            copy_q(nxt, 1 - s)
                    if front:
                        copy_v(nxt, 1 - s, 1)
                copy_normed(0, 0)
                copy_q(0, 0)
                for n in range(2):
                    copy_v(0, 0, n)
                pipeline(act, step)
        sems.clear()


def stage_l1_xattn(nc, C, sems, d, X):
    with ExitStack() as x:
        sb = lambda n, shape: x.enter_context(nc.sbuf_tensor(f"l1x_{n}", shape, F32))
        w = sb("w", [P, 3, 8 * DM])
        wf = sb("wf", [P, 8, DM])
        b = sb("b", [P, 3, 8])
        bf = sb("bf", [1, DM])
        w_in, b_mm, b_done = sems(3)
        with nc.psum_tensor("l1x_pb", [P, 512], F32) as pb, nc.Block() as block:
            @block.sync
            def _(sp):
                sp.dma_start(w[:, :, :], d["l1x_w"]).then_inc(w_in, 16)
                sp.dma_start(wf[:, :, :], d["l1x_wf"]).then_inc(w_in, 16)
                sp.dma_start(b[:, :, :], d["l1x_b"]).then_inc(w_in, 16)
                sp.dma_start(bf[:, :], d["l1x_bf"]).then_inc(w_in, 16)

            @block.tensor
            def _(pe):
                pe.wait_ge(w_in, 64)
                for c in range(8):
                    mm = nc.tensor.matmul(pb[0:1, 0:DM], b[:, 2, c:c + 1], wf[:, c, :], start=(c == 0), stop=(c == 7))
                mm.then_inc(b_mm, 1)

            @block.vector
            def _(dve):
                dve.wait_ge(b_mm, 1)
                nc.vector.tensor_tensor(bf[:, :], bf[:, :], pb[0:1, 0:DM], ALU.add).then_inc(b_done, 1)
                nc.vector.tensor_scalar(b[:, 0, :], b[:, 0, :], 1.0 / 16, 0.0, ALU.mult, ALU.add)
        sems.clear()
        wide_head_attention(nc, C, sems, "l1x", X, w[:, 0, :], w[:, 1, :], w[:, 2, :], wf, 1.0 / 16,
                            out_bias=bf[0:1, :], ctx_dram=d["ctxT"], q_bias=b[:, 0, :], k_bias=b[:, 1, :])


def stage_l3_attn(nc, C, sems, d, X):
    with ExitStack() as x:
        sb = lambda n, shape: x.enter_context(nc.sbuf_tensor(f"l3a_{n}", shape, F32))
        w = sb("w", [P, 3, 8 * DM])
        wf = sb("wf", [P, 8, DM])
        (w_in,) = sems(1)
        with nc.Block() as block:
            @block.sync
            def _(sp):
                sp.dma_start(w[:, :, :], d["l3a_w"]).then_inc(w_in, 16)
                sp.dma_start(wf[:, :, :], d["l3a_wf"]).then_inc(w_in, 16)
                sp.wait_ge(w_in, 32)
        sems.clear()
        wide_head_attention(nc, C, sems, "l3a", X, w[:, 0, :], w[:, 1, :], w[:, 2, :], wf, 1.0 / 8)


def stage_l2_xattn(nc, C, sems, d, X):
    with ExitStack() as x:
        sb = lambda n, shape: x.enter_context(nc.sbuf_tensor(f"l2x_{n}", shape, F32))
        w = sb("w", [P, 4, DM])
        b = sb("b", [P, 3])
        bo = sb("bo", [1, DM])
        w_in, b_mm, b_done = sems(3)
        with nc.psum_tensor("l2x_pb", [P, 512], F32) as pb, nc.Block() as block:
            @block.sync
            def _(sp):
                sp.dma_start(w[:, :, :], d["l2x_w"]).then_inc(w_in, 16)
                sp.dma_start(b[:, :], d["l2x_b"]).then_inc(w_in, 16)
                sp.dma_start(bo[:, :], d["l2x_bo"]).then_inc(w_in, 16)

            @block.tensor
            def _(pe):
                pe.wait_ge(w_in, 48)
                nc.tensor.matmul(pb[0:1, 0:DM], b[:, 2:3], w[:, 3, :], start=True, stop=True).then_inc(b_mm, 1)

            @block.vector
            def _(dve):
                dve.wait_ge(b_mm, 1)
                nc.vector.tensor_tensor(bo[:, :], bo[:, :], pb[0:1, 0:DM], ALU.add).then_inc(b_done, 1)
        sems.clear()
        small_head_attention(nc, C, sems, "l2x", src=X, dests=[X], wq=w[:, 0, :], wk=w[:, 1, :], wv=w[:, 2, :],
                             wo=w[:, 3, :], out_bias=bo[0:1, :], ctx_dram=d["ctxT"],
                             q_bias=b[:, 0:1], k_bias=b[:, 1:2])


class Chain:

    def __init__(self, eng, done):
        self.eng, self.done, self.steps = eng, done, 0

    def add(self, ins):
        ins.then_inc(self.done, 1)
        self.steps += 1

    def wait(self):
        self.eng.wait_ge(self.done, self.steps)


def running(nc, chain, a, b, c, op):
    n, dist, other = a.shape[-1], 1, c
    while dist < n:
        chain.wait()
        chain.add(nc.vector.tensor_copy(b[:, :, 0:dist], a[:, :, 0:dist]))
        chain.add(nc.vector.tensor_tensor(b[:, :, dist:n], a[:, :, dist:n], a[:, :, 0:n - dist], op))
        a, b, other, dist = b, other, b, 2 * dist
    return a


def normalise_all(nc, C, sems, tag, src, dst):
    with ExitStack() as x:
        sb = lambda n, shape: x.enter_context(nc.sbuf_tensor(f"{tag}_{n}", shape, F32))
        stat = sb("stat", [P, NB, 6])
        mv = sb("mv", [P, NB, 2])
        dev = sb("dev", [P, NB])
        rstd = sb("rstd", [P, NB])
        stats_done, moments_done, dev_done, rstd_done, centred = sems(5)

        def part(q):
            return dst[:, q * 8 * DM:(q + 1) * 8 * DM].rearrange("p (b k) -> p b k", k=DM)

        def scale(eng, q):
            eng.tensor_tensor(part(q), part(q), bcast_in(rstd[:, 8 * q:8 * q + 8], DM), ALU.mult)

        with nc.Block() as block:
            @block.vector
            def _(dve):
                for b in range(NB):
                    nc.vector.bn_stats(stat[:, b, :], tile_of(src, b)).then_inc(stats_done, 1)
                dve.wait_ge(stats_done, NB)
                for b in range(NB):
                    nc.vector.bn_aggr(mv[:, b, :], stat[:, b, :]).then_inc(moments_done, 1)
                dve.wait_ge(moments_done, NB)
                for q in range(4):
                    nc.vector.tensor_tensor(part(q), src[:, q * 8 * DM:(q + 1) * 8 * DM].rearrange("p (b k) -> p b k", k=DM),
                                            bcast_in(mv[:, 8 * q:8 * q + 8, 0], DM), ALU.subtract).then_inc(centred, 1)
                    if q == 1:
                        dve.wait_ge(dev_done, 1)
                        nc.vector.reciprocal(rstd[:, :], dev[:, :]).then_inc(rstd_done, 1)
                dve.wait_ge(rstd_done, 1)
                for q in (2, 3):
                    dve.wait_ge(centred, q + 1)
                    scale(dve, q)

            @block.scalar
            def _(act):
                act.wait_ge(moments_done, NB)
                nc.scalar.activation(dev[:, :], mv[:, :, 1], ACT.Sqrt, bias=C.eps).then_inc(dev_done, 1)

            @block.gpsimd
            def _(pool):
                pool.wait_ge(rstd_done, 1)
                for q in (0, 1):
                    pool.wait_ge(centred, q + 1)
                    scale(pool, q)
        sems.clear()


def turn_all(nc, C, sems, tag, src, dst, affine=None):
    with ExitStack() as x:
        T = [x.enter_context(nc.psum_tensor(f"{tag}_T{i}", [P, 512], F32)) for i in range(2)]
        t_mm, t_done = sems(2)
        with nc.Block() as block:
            @block.tensor
            def _(pe):
                for g in range(NB // 4):
                    wait(pe, t_done, g - 1)
                    for k in range(4):
                        mm = nc.tensor.transpose(T[g % 2][:, k * P:(k + 1) * P], tile_of(src, 4 * g + k), C.ident)
                    mm.then_inc(t_mm, 1)

            @block.scalar
            def _(act):
                for g in range(NB // 4):
                    act.wait_ge(t_mm, g + 1)
                    if affine is None:
                        nc.scalar.copy(dst[:, g * 512:(g + 1) * 512], T[g % 2][:, :]).then_inc(t_done, 1)
                    else:
                        nc.scalar.activation(dst[:, g * 512:(g + 1) * 512], T[g % 2][:, :], ACT.Identity,
                                             bias=affine[1], scale=affine[0]).then_inc(t_done, 1)
        sems.clear()


def add_product(nc, C, sems, tag, XT, w, X):
    with ExitStack() as x:
        Y = [x.enter_context(nc.psum_tensor(f"{tag}_Y{i}", [P, 512], F32)) for i in range(2)]
        y_mm, x_done = sems(2)
        with nc.Block() as block:
            @block.tensor
            def _(pe):
                for g in range(NB // 4):
                    wait(pe, x_done, g - 1)
                    for k in range(4):
                        mm = nc.tensor.matmul(Y[g % 2][:, k * P:(k + 1) * P], tile_of(XT, 4 * g + k), w,
                                              start=True, stop=True)
                    mm.then_inc(y_mm, 1)

            @block.vector
            def _(dve):
                for g in range(NB // 4):
                    dve.wait_ge(y_mm, g + 1)
                    part = X[:, g * 512:(g + 1) * 512]
                    nc.vector.tensor_tensor(part, part, Y[g % 2][:, :], ALU.add).then_inc(x_done, 1)
        sems.clear()


QUANT_STEPS = 17


def quantise(nc, dve, chain, v, m, r, t):
    n = v.shape[1]
    blocks = lambda a: a.rearrange("p (c k) -> p c k", k=32)
    y, z, c = [t[:, i, 0:n] for i in range(3)]

    def step(f, *args):
        chain.wait()
        chain.add(f(*args))
    step(nc.vector.tensor_reduce, m, blocks(v), AXX, ALU.max, True)
    step(nc.vector.tensor_scalar, m, m, 1 / 7.5, 1e-30, ALU.mult, ALU.max)
    step(nc.vector.reciprocal, r, m)
    step(nc.vector.tensor_tensor, blocks(y), blocks(v), bcast_in(r, 32), ALU.mult)
    step(nc.vector.tensor_tensor, v, y, y, ALU.mult)
    step(nc.vector.tensor_scalar, c, v, 16.0, 1.0, ALU.is_ge, ALU.mult)
    chain.add(nc.vector.tensor_scalar(z, v, 4.0, 1.0, ALU.is_ge, ALU.mult))
    chain.wait()
    chain.add(nc.vector.scalar_tensor_tensor(v, c, 2.0, z, ALU.mult, ALU.add))
    step(nc.vector.scalar_tensor_tensor, z, z, 2.0, c, ALU.mult, ALU.add)
    chain.add(nc.vector.tensor_scalar(v, v, 1.0, 0.125, ALU.add, ALU.mult))
    step(nc.vector.tensor_scalar, z, z, -2.0, 8.0, ALU.mult, ALU.add)
    step(nc.vector.tensor_tensor, z, y, z, ALU.mult)
    step(nc.vector.tensor_scalar, y, z, 12582912.0, -12582912.0, ALU.add, ALU.add)
    step(nc.vector.tensor_tensor, z, y, z, ALU.subtract)
    step(nc.vector.scalar_tensor_tensor, y, z, 0.5, y, ALU.is_ge, ALU.subtract)
    step(nc.vector.scalar_tensor_tensor, v, y, -1.0, v, ALU.mult, ALU.mult)
    step(nc.vector.tensor_tensor, blocks(v), blocks(v), bcast_in(m, 32), ALU.mult)


def stage_l1_ffn(nc, C, sems, d, X):
    with ExitStack() as x:
        sb = lambda n, shape: x.enter_context(nc.sbuf_tensor(f"l1f_{n}", shape, F32))
        w = sb("w", [P, DM])
        wT = sb("wT", [P, DM])
        bias = sb("bias", [P, DM])
        XN = sb("XN", [P, NB * DM])
        XT = sb("XT", [P, NB * DM])
        CH = 8 * DM
        m = sb("m", [P, CH // 32])
        r = sb("r", [P, CH // 32])
        t = sb("t", [P, 3, CH])
        normalise_all(nc, C, sems, "l1f_n", X, XN)
        w_in, steps, x_biased, w_mm, wt_done = sems(5)
        with nc.psum_tensor("l1f_W", [P, 512], F32) as W, nc.Block() as block:
            @block.sync
            def _(sp):
                sp.dma_start(w[:, :], d["l1f_w"]).then_inc(w_in, 16)
                sp.dma_start(bias[:, :], row_bcast(d["l1f_b"], DM)).then_inc(w_in, 16)

            @block.vector
            def _(dve):
                chain = Chain(dve, steps)
                dve.wait_ge(w_in, 32)
                quantise(nc, dve, chain, w[:, :], m[:, 0:4], r[:, 0:4], t)
                for q in range(4):
                    quantise(nc, dve, chain, XN[:, q * CH:(q + 1) * CH], m[:, :], r[:, :], t)
                dve.wait_ge(w_mm, 1)
                nc.vector.tensor_copy(wT[:, :], W[:, 0:P]).then_inc(wt_done, 1)

            @block.gpsimd
            def _(pool):
                pool.wait_ge(w_in, 32)
                for q in range(4):
                    part = X[:, q * CH:(q + 1) * CH].rearrange("p (b k) -> p b k", k=DM)
                    pool.tensor_tensor(part, part, bcast_mid(bias[:, :], 8), ALU.add).then_inc(x_biased, 1)

            @block.tensor
            def _(pe):
                pe.wait_ge(steps, QUANT_STEPS)
                nc.tensor.transpose(W[:, 0:P], w[:, :], C.ident).then_inc(w_mm, 1)
        sems.clear()
        turn_all(nc, C, sems, "l1f_t", XN, XT)
        add_product(nc, C, sems, "l1f_y", XT, wT[:, :], X)


def route(nc, C, sems, tag, XT, wr, bias, share, experts, k):
    n = NB * experts
    with ExitStack() as x:
        sb = lambda nm, shape: x.enter_context(nc.sbuf_tensor(f"{tag}_{nm}", shape, F32))
        s, eq, cum, cum2 = [sb(nm, [P, NB, experts]) for nm in ("s", "eq", "cum", "cum2")]
        top = sb("top", [P, NB, 8])
        mx = sb("mx", [P, NB])
        left = sb("left", [P, NB])
        per = 512 // experts
        banks = -(-NB // per)
        L = [x.enter_context(nc.psum_tensor(f"{tag}_L{i}", [P, 512], F32)) for i in range(banks)]
        l_mm, steps, exp_done = sems(3)
        with nc.Block() as block:
            @block.tensor
            def _(pe):
                for b in range(NB):
                    nc.tensor.matmul(L[b // per][:, (b % per) * experts:(b % per + 1) * experts], tile_of(XT, b), wr,
                                     start=True, stop=True).then_inc(l_mm, 1)

            @block.vector
            def _(dve):
                chain = Chain(dve, steps)

                def step(f, *args):
                    chain.wait()
                    chain.add(f(*args))
                dve.wait_ge(l_mm, NB)
                for i in range(banks):
                    b0, b1 = i * per, min(NB, (i + 1) * per)
                    logits = L[i][:, 0:(b1 - b0) * experts].rearrange("p (b e) -> p b e", e=experts)
                    if bias is None:
                        chain.add(nc.vector.tensor_copy(s[:, b0:b1, :], logits))
                    else:
                        chain.add(nc.vector.tensor_tensor(s[:, b0:b1, :], logits, bcast_mid(bias, b1 - b0), ALU.add))
                flat = lambda a: a[:, :, :].rearrange("p b e -> p (b e)")
                step(nc.vector.tensor_reduce, mx[:, :], s[:, :, :], AXX, ALU.max)
                step(nc.vector.tensor_tensor, s[:, :, :], s[:, :, :], bcast_in(mx[:, :], experts), ALU.subtract)
                chain.wait()
                dve.wait_ge(exp_done, 1)
                chain.add(nc.vector.tensor_reduce(mx[:, :], s[:, :, :], AXX, ALU.add))
                step(nc.vector.reciprocal, mx[:, :], mx[:, :])
                step(nc.vector.tensor_tensor, s[:, :, :], s[:, :, :], bcast_in(mx[:, :], experts), ALU.mult)
                chain.wait()
                for b in range(NB):
                    chain.add(nc.vector.max(top[:, b, :], s[:, b, :]))
                chain.wait()
                kth = bcast_in(top[:, :, k - 1], experts)
                chain.add(nc.vector.tensor_tensor(eq[:, :, :], s[:, :, :], kth, ALU.is_equal))
                chain.add(nc.vector.tensor_tensor(share, s[:, :, :], kth, ALU.is_gt))
                chain.wait()
                chain.add(nc.vector.tensor_reduce(left[:, :], share, AXX, ALU.add))
                step(nc.vector.tensor_scalar, left[:, :], left[:, :], -1.0, float(k), ALU.mult, ALU.add)
                a = running(nc, chain, eq, cum, cum2, ALU.add)
                b_ = cum2 if a is cum else cum
                step(nc.vector.tensor_tensor, b_[:, :, :], a[:, :, :], bcast_in(left[:, :], experts), ALU.is_le)
                step(nc.vector.tensor_tensor, flat(eq), flat(eq), flat(b_), ALU.mult)
                step(nc.vector.tensor_tensor, share, share, eq[:, :, :], ALU.add)
                step(nc.vector.tensor_tensor, share, share, s[:, :, :], ALU.mult)
                step(nc.vector.tensor_reduce, left[:, :], share, AXX, ALU.add)
                step(nc.vector.tensor_scalar, left[:, :], left[:, :], 1e-12, 0.0, ALU.max, ALU.add)
                step(nc.vector.reciprocal, left[:, :], left[:, :])
                step(nc.vector.tensor_tensor, share, share, bcast_in(left[:, :], experts), ALU.mult)
                chain.wait()
            @block.scalar
            def _(act):
                act.wait_ge(steps, banks + 2)
                nc.scalar.activation(s[:, :, :], s[:, :, :], ACT.Exp).then_inc(exp_done, 1)
        sems.clear()


def experts_sum(nc, C, sems, tag, X, XT, share, n_experts, chunks, w1, wu, w2, b1=None):
    units = n_experts * chunks
    GROUPS = NB // 4
    with ExitStack() as x:
        sb = lambda n, shape: x.enter_context(nc.sbuf_tensor(f"{tag}_{n}", shape, F32))
        ps = lambda n: x.enter_context(nc.psum_tensor(f"{tag}_{n}", [P, 512], F32))
        G, U, Y = [ps("G0"), ps("G1")], [ps("U0"), ps("U1")], [ps("Y0"), ps("Y1")]
        sg = sb("sg", [P, 2, 512])
        h = sb("h", [P, 2, 512])
        u_mm, silu_done, h_done, down_mm, x_done = sems(5)

        with nc.Block() as block:

            @block.tensor
            def _(pe):
                def up(i, n):
                    pe.wait_ge(h_done, i * units + (n + 1))
                    rhs = XT[:, bass.ts(i, 512)]
                    mm = nc.tensor.matmul(G[n % 2][:, :], w1[:, n, :], rhs, start=True, stop=True)
                    if wu is not None:
                        mm = nc.tensor.matmul(U[n % 2][:, :], wu[:, n, :], rhs, start=True, stop=True)
                    mm.then_inc(u_mm, 1)

                def down(i, n):
                    e, c = n // chunks, n % chunks
                    if c == 0:
                        pe.wait_ge(x_done, i * n_experts + (e + 1))
                    pe.wait_ge(h_done, i * units + (n + 3))
                    for k in range(4):
                        mm = nc.tensor.matmul(Y[e % 2][:, k * P:(k + 1) * P], h[:, n % 2, k * P:(k + 1) * P],
                                              w2[:, n, :], start=(c == 0 and k == 0), stop=(c == chunks - 1),
                                              skip_group_check=True)
                    mm.then_inc(down_mm, 1)
                with pe.Fori(0, GROUPS) as i:
                    up(i, 0)
                    for n in range(1, units):
                        up(i, n)
                        down(i, n - 1)
                    down(i, units - 1)

            @block.scalar
            def _(act):
                if wu is None:
                    act.sem_inc(h_done, 2)

                def hidden(i, n):
                    act.wait_ge(u_mm, i * units + (n + 1))
                    if wu is None:
                        act.wait_ge(down_mm, i * units + (n + 1))
                        nc.scalar.activation(h[:, n % 2, :], G[n % 2][:, :], ACT.Gelu_apprx_tanh,
                                             bias=b1[:, n:n + 1]).then_inc(h_done, 1)
                    else:
                        act.wait_ge(h_done, i * units + (n + 1))
                        nc.scalar.activation(sg[:, n % 2, :], G[n % 2][:, :], ACT.Silu).then_inc(silu_done, 1)
                with act.Fori(0, GROUPS) as i:
                    for n in range(units):
                        hidden(i, n)

            @block.gpsimd
            def _(pool):
                pool.sem_inc(down_mm, 2)
                pool.sem_inc(x_done, 2)

            @block.vector
            def _(dve):
                if wu is not None:
                    dve.sem_inc(h_done, 2)

                def product(i, n):
                    dve.wait_ge(down_mm, i * units + (n + 1))
                    dve.wait_ge(silu_done, i * units + (n + 1))
                    nc.vector.tensor_tensor(h[:, n % 2, :], sg[:, n % 2, :], U[n % 2][:, :],
                                            ALU.mult).then_inc(h_done, 1)

                def add(i, e):
                    dve.wait_ge(x_done, i * n_experts + (e + 2))
                    dve.wait_ge(down_mm, i * units + (chunks * (e + 1) + 2))
                    for k in range(4):
                        dst = X[:, bass.ds(i * 512 + k * P, P)]
                        ins = nc.vector.scalar_tensor_tensor(dst, Y[e % 2][:, k * P:(k + 1) * P],
                                                             share[:, bass.ds(i * 4 + k, 1), e], dst,
                                                             ALU.mult, ALU.add)
                    ins.then_inc(x_done, 1)
                with dve.Fori(0, GROUPS) as i:
                    for n in range(units):
                        if wu is not None:
                            product(i, n)
                        if n >= 2 and (n - 1) % chunks == 0:
                            add(i, (n - 1) // chunks - 1)
                    for e in range((units - 2) // chunks, n_experts):
                        add(i, e)
        sems.clear()


def stage_l2_ffn(nc, C, sems, d, X):
    E, SHARED = 32, 4
    with ExitStack() as x:
        sb = lambda n, shape: x.enter_context(nc.sbuf_tensor(f"l2f_{n}", shape, F32))
        XT = sb("XT", [P, NB * DM])
        share = sb("share", [P, NB, E + SHARED])
        wr = sb("wr", [P, E])
        rb = sb("rb", [P, E])
        wg, wu, wd = [sb(n, [P, E + SHARED, DM]) for n in ("wg", "wu", "wd")]
        w_in, ones_done = sems(2)
        with nc.Block() as block:
            @block.sync
            def _(sp):
                sp.dma_start(wr[:, :], d["l2f_wr"]).then_inc(w_in, 16)
                sp.dma_start(rb[:, :], row_bcast(d["l2f_rb"], E)).then_inc(w_in, 16)
                for w, n in ((wg, "l2f_wg"), (wu, "l2f_wu"), (wd, "l2f_wd")):
                    sp.dma_start(w[:, :, :], d[n]).then_inc(C.experts_in, 16)
                sp.wait_ge(w_in, 32)

            @block.gpsimd
            def _(pool):
                pool.memset(share[:, :, E:E + SHARED], 1.0).then_inc(ones_done, 1)
        sems.clear()
        with nc.sbuf_tensor("l2f_XN", [P, NB * DM], F32) as XN:
            normalise_all(nc, C, sems, "l2f_n", X, XN)
            turn_all(nc, C, sems, "l2f_t", XN, XT)
            route(nc, C, sems, "l2f_r", XT, wr[:, :], rb[:, :], share[:, :, 0:E], E, 4)
        with nc.Block() as block:
            @block.sync
            def _(sp):
                sp.wait_ge(C.experts_in, 3 * 16)
        experts_sum(nc, C, sems, "l2f_e", X, XT, share, E + SHARED, 1, wg, wu, wd)


def stage_l3_ffn(nc, C, sems, d, X):
    E, CH = 8, 4
    with ExitStack() as x:
        sb = lambda n, shape: x.enter_context(nc.sbuf_tensor(f"l3f_{n}", shape, F32))
        H = sb("H", [P, NB * DM])
        v = sb("v", [P, 7])
        bo = sb("bo", [1, DM])
        wg = sb("wg", [P, E])
        b2 = sb("b2", [E, DM])
        w1 = sb("w1", [P, E * CH, DM])
        w2 = sb("w2", [P, E * CH, DM])
        b1 = sb("b1", [P, E * CH])
        normalise_all(nc, C, sems, "l3f_u", X, H)
        with ExitStack() as y:
            w = y.enter_context(nc.sbuf_tensor("l3f_w", [P, 4, DM], F32))
            w_in, b_mm, b_done, x_done = sems(4)
            with nc.psum_tensor("l3f_pb", [P, 512], F32) as pb, nc.Block() as block:
                @block.sync
                def _(sp):
                    sp.dma_start(w[:, :, :], d["l3f_w"]).then_inc(w_in, 16)
                    sp.dma_start(v[:, :], d["l3f_v"]).then_inc(w_in, 16)
                    sp.dma_start(bo[:, :], d["l3f_bo"]).then_inc(w_in, 16)
                    for t, n in ((wg[:, :], "wg"), (b2[:, :], "b2"), (w1[:, :, :], "w1"), (w2[:, :, :], "w2"),
                                 (b1[:, :], "b1")):
                        sp.dma_start(t, d["l3f_" + n]).then_inc(C.experts_in, 16)

                @block.tensor
                def _(pe):
                    pe.wait_ge(w_in, 48)
                    nc.tensor.matmul(pb[0:1, 0:DM], v[:, 6:7], w[:, 3, :], start=True, stop=True).then_inc(b_mm, 1)

                @block.gpsimd
                def _(pool):
                    pool.tensor_tensor(X[:, :], X[:, :], H[:, :], ALU.add).then_inc(x_done, 1)

                @block.vector
                def _(dve):
                    dve.wait_ge(b_mm, 1)
                    nc.vector.tensor_tensor(bo[:, :], bo[:, :], pb[0:1, 0:DM], ALU.add).then_inc(b_done, 1)
            sems.clear()
            small_head_attention(nc, C, sems, "l3f", src=H, dests=[X, H], wq=w[:, 0, :], wk=w[:, 1, :],
                                 wv=w[:, 2, :], wo=w[:, 3, :], out_bias=bo[0:1, :],
                                 q_bias=v[:, 4:5], k_bias=v[:, 5:6], affine=(v[:, 0:1], v[:, 1:2]))
        XT = sb("XT", [P, NB * DM])
        share = sb("share", [P, NB, E])
        with nc.Block() as block:
            @block.sync
            def _(sp):
                sp.wait_ge(C.experts_in, (3 + 5) * 16)
        normalise_all(nc, C, sems, "l3f_n", H, H)
        turn_all(nc, C, sems, "l3f_t", H, XT, affine=(v[:, 2:3], v[:, 3:4]))
        route(nc, C, sems, "l3f_r", XT, wg[:, :], None, share[:, :, :], E, 2)
        t_mm, t_done, y_mm, x_done = sems(4)
        with ExitStack() as y:
            T, Y = [[y.enter_context(nc.psum_tensor(f"l3f_{n}{i}", [P, 512], F32)) for i in range(2)] for n in "TY"]
            sT = y.enter_context(nc.sbuf_tensor("l3f_sT", [E, NB, P], F32))
            with nc.Block() as block:
                @block.tensor
                def _(pe):
                    for g in range(NB // 4):
                        wait(pe, t_done, g - 1)
                        for k in range(4):
                            mm = nc.tensor.transpose(T[g % 2][0:E, k * P:(k + 1) * P], share[:, 4 * g + k, :], C.ident)
                        mm.then_inc(t_mm, 1)
                    for g in range(NB // 4):
                        wait(pe, x_done, g - 1)
                        pe.wait_ge(t_done, g + 1)
                        for k in range(4):
                            mm = nc.tensor.matmul(Y[g % 2][:, k * P:(k + 1) * P], sT[:, 4 * g + k, :], b2[:, :],
                                                  start=True, stop=True)
                        mm.then_inc(y_mm, 1)

                @block.scalar
                def _(act):
                    for g in range(NB // 4):
                        act.wait_ge(t_mm, g + 1)
                        nc.scalar.copy(sT[:, 4 * g:4 * g + 4, :].rearrange("e b t -> e (b t)"),
                                       T[g % 2][0:E, :]).then_inc(t_done, 1)

                @block.vector
                def _(dve):
                    for g in range(NB // 4):
                        dve.wait_ge(y_mm, g + 1)
                        part = X[:, g * 512:(g + 1) * 512]
                        nc.vector.tensor_tensor(part, part, Y[g % 2][:, :], ALU.add).then_inc(x_done, 1)
            sems.clear()
        experts_sum(nc, C, sems, "l3f_e", X, XT, share, E, CH, w1, None, w2, b1)


def stage_l3_xattn(nc, C, sems, d, X):
    HEADS, HD = 8, 16
    ROWS = NB * HEADS
    g_dram = nc.dram_tensor("l3x_dram_gates", (2 * HEADS, NB * P), F32, kind="Internal").ap()
    m_dram = nc.dram_tensor("l3x_dram_max", (NB, HEADS * P), F32, kind="Internal").ap()
    with ExitStack() as x:
        sb = lambda n, shape: x.enter_context(nc.sbuf_tensor(f"l3x_{n}", shape, F32))
        XT = sb("XT", [P, NB * DM])
        wg = sb("wg", [P, 3, 2 * HEADS])
        gb = sb("gb", [2 * HEADS, 1])
        gn = sb("gn", [P, 2, DM])
        gt = sb("gt", [P, NB, HEADS])
        em = sb("em", [P, NB, HEADS])
        H = sb("H", [P, NB, HEADS, HD + 1])
        with nc.sbuf_tensor("l3x_XN", [P, NB * DM], F32) as XN:
            normalise_all(nc, C, sems, "l3x_n", X, XN)
            turn_all(nc, C, sems, "l3x_t", XN, XT)
        with ExitStack() as y:
            sy = lambda n, shape: y.enter_context(nc.sbuf_tensor(f"l3x1_{n}", shape, F32))
            CT = sy("CT", [P, NB * DM])
            GT = sy("GT", [2 * HEADS, NB * P])
            it, ft, u, v, w = [sy(n, [P, 2, P]) for n in ("it", "ft", "u", "v", "w")]
            G = [y.enter_context(nc.psum_tensor(f"l3x1_G{i}", [P, 512], F32)) for i in range(2)]
            T = y.enter_context(nc.psum_tensor("l3x1_T", [P, 512], F32))
            (w_in, kv_done, g_mm, g_done, g_out, g_in, steps, abs_done, ln_done, em_done, m_out,
             t_mm, exp_done) = sems(13)
            with nc.Block() as block:
                @block.sync
                def _(sp):
                    sp.dma_start(wg[:, :, :], d["l3x_wg"]).then_inc(w_in, 16)
                    sp.dma_start(gb[:, :], d["l3x_gb"]).then_inc(w_in, 16)
                    sp.dma_start(CT[:, :], d["ctxT_rows"]).then_inc(w_in, 16)
                    for i, n in enumerate(("l3x_gnw", "l3x_gnb")):
                        sp.dma_start(gn[:, i, :], row_bcast(d[n], DM)).then_inc(w_in, 16)
                    sp.wait_ge(g_done, NB // 4)
                    sp.dma_start(g_dram, GT[:, :]).then_inc(g_out, 16)
                    sp.wait_ge(g_out, 16)
                    for i, t in enumerate((it, ft)):
                        rows = g_dram[HEADS * i:HEADS * i + HEADS].rearrange("h (b t) -> b h t", t=P)
                        for half in range(2):
                            sp.dma_start(t[:, half, :], rows[16 * half:16 * half + 16]).then_inc(g_in, 16)
                    sp.wait_ge(em_done, 1)
                    for half in range(2):
                        sp.dma_start(m_dram[16 * half:16 * half + 16].rearrange("b (h t) -> (b h) t", t=P),
                                     u[:, half, :]).then_inc(m_out, 16)
                    sp.wait_ge(m_out, 32)

                @block.tensor
                def _(pe):
                    pe.wait_ge(kv_done, 1)
                    for g in range(NB // 4):
                        part = slice(g * 512, (g + 1) * 512)
                        wait(pe, g_done, g - 1)
                        nc.tensor.matmul(G[g % 2][0:16, :], wg[:, 0, :], XT[:, part], start=True, stop=False)
                        nc.tensor.matmul(G[g % 2][0:16, :], wg[:, 1, :], CT[:, part], start=False,
                                         stop=True).then_inc(g_mm, 1)
                    pe.wait_ge(exp_done, 2)
                    for half in range(2):
                        nc.tensor.transpose(T[:, half * P:(half + 1) * P], it[:, half, :], C.ident)
                    for half in range(2):
                        mm = nc.tensor.transpose(T[:, (2 + half) * P:(3 + half) * P], ft[:, half, :], C.ident)
                    mm.then_inc(t_mm, 1)

                @block.scalar
                def _(act):
                    act.wait_ge(w_in, 80)
                    for g in range(NB // 4):
                        act.wait_ge(g_mm, g + 1)
                        nc.scalar.activation(GT[:, g * 512:(g + 1) * 512], G[g % 2][0:16, :], ACT.Identity,
                                             bias=gb[:, :]).then_inc(g_done, 1)
                    act.wait_ge(abs_done, 1)
                    nc.scalar.activation(u[:, :, :], u[:, :, :], ACT.Exp, scale=-1.0).then_inc(exp_done, 1)
                    act.wait_ge(exp_done, 1)
                    nc.scalar.activation(u[:, :, :], u[:, :, :], ACT.Ln, bias=C.ones[:, 0:1]).then_inc(ln_done, 1)
                    act.wait_ge(em_done, 1)
                    nc.scalar.activation(ft[:, :, :], ft[:, :, :], ACT.Exp, scale=-1.0).then_inc(exp_done, 1)

                @block.vector
                def _(dve):
                    chain = Chain(dve, steps)
                    dve.wait_ge(w_in, 80)
                    nc.vector.tensor_tensor(wg[:, 1, :], wg[:, 1, :], wg[:, 2, :], ALU.add).then_inc(kv_done, 1)
                    dve.wait_ge(g_in, 64)
                    nc.vector.scalar_tensor_tensor(u[:, :, :], ft[:, :, :], -1.0, ft[:, :, :], ALU.mult,
                                                   ALU.max).then_inc(abs_done, 1)
                    dve.wait_ge(ln_done, 1)
                    chain.add(nc.vector.scalar_tensor_tensor(ft[:, :, :], ft[:, :, :], 0.0, u[:, :, :], ALU.min,
                                                             ALU.subtract))
                    F = running(nc, chain, ft, v, w, ALU.add)
                    chain.wait()
                    chain.add(nc.vector.tensor_tensor(it[:, :, :], it[:, :, :], F[:, :, :], ALU.subtract))
                    chain.wait()
                    M = running(nc, chain, it, u, w if F is v else v, ALU.max)
                    assert M is u
                    chain.wait()
                    nc.vector.tensor_tensor(ft[:, :, :], M[:, :, :], F[:, :, :], ALU.add).then_inc(em_done, 1)
                    dve.wait_ge(t_mm, 1)
                    flat = lambda t: t[:, :, :].rearrange("p b h -> p (b h)")
                    nc.vector.tensor_copy(flat(gt), T[:, 0:ROWS])
                    nc.vector.tensor_copy(flat(em), T[:, ROWS:2 * ROWS])
            sems.clear()

        with ExitStack() as y:
            sy = lambda n, shape: y.enter_context(nc.sbuf_tensor(f"l3x2_{n}", shape, F32))
            Mb = sy("Mb", [P, 2, HEADS, P])
            W = sy("W", [P, 2, HEADS, P])
            Q = sy("Q", [P, 2, HEADS, P])
            Ct = sy("Ct", [P, 2, HEADS, P])
            ctxT = sy("ctxT", [P, 2, P])
            vn = sy("vn", [P, 2, DM])
            nd = sy("nd", [P, 2, 4, P])
            S = [y.enter_context(nc.psum_tensor(f"l3x2_S{i}", [P, 512], F32)) for i in range(4)]
            ND = y.enter_context(nc.psum_tensor("l3x2_ND", [P, 512], F32))
            O = [y.enter_context(nc.psum_tensor(f"l3x2_O{i}", [P, 512], F32)) for i in range(2)]
            (in0, in1, w_done, exp_done, mask_done, q_done, s_mm, c_done, nd_mm, nd_done, o_mm, o_done,
             pad, v_in0, v_in1) = sems(15)
            loaded, v_in = [in0, in1], [v_in0, v_in1]
            flat = lambda t, s: t[:, s, :, :].rearrange("p h k -> p (h k)")
            with nc.Block() as block:
                @block.sync
                def _(sp):
                    def load(b, s):
                        wait(sp, w_done, count(b, 1, -1))
                        settle(sp, pad)
                        row = m_dram[b:b + 1] if isinstance(b, int) else m_dram[bass.ds(b[0] * 2 + b[1], 1)]
                        sp.dma_start(flat(Mb, s), row.to_broadcast([P, HEADS * P])).then_inc(loaded[s], 16)
                        wait(sp, s_mm, count(b, 2, -2))
                        settle(sp, pad)
                        sp.dma_start(ctxT[:, s, :], dram_of(d["ctxT"], b)).then_inc(loaded[s], 16)
                        wait(sp, nd_mm, count(b, 1, -1))
                        settle(sp, pad)
                        sp.dma_start(vn[:, s, :], dram_of(d["ctx"], b)).then_inc(v_in[s], 16)
                    each(sp, load)

                @block.gpsimd
                def _(pool):
                    def spread(b, s):
                        wait(pool, s_mm, count(b, 2, -2))
                        settle(pool, pad)
                        pool.tensor_tensor(Q[:, s, :, :], bcast_mid(tile_of(XT, b), HEADS), bcast_in(C.hmask16, P),
                                           ALU.mult).then_inc(q_done, 1)

                    def mask(b, s):
                        wait(pool, exp_done, count(b, 1, 1))
                        pool.tensor_tensor(W[:, s, :, :], W[:, s, :, :], bcast_mid(C.tri, HEADS),
                                           ALU.mult).then_inc(mask_done, 1)

                    def f(b, s):
                        spread(b, s)
                        mask(b, s)
                    each(pool, f)

                @block.tensor
                def _(pe):
                    def scores(b, s):
                        wait(pe, loaded[s], count_own(b, 32, 32))
                        wait(pe, q_done, count(b, 1, 1))
                        for q in range(2):
                            wait(pe, c_done, count(b, 2, -2))
                            nc.tensor.matmul(S[2 * s + q][:, :], ctxT[:, s, :],
                                             Q[:, s, 4 * q:4 * q + 4, :].rearrange("p h k -> p (h k)"),
                                             start=True, stop=True).then_inc(s_mm, 1)

                    def sum_keys(b, s):
                        wait(pe, nd_done, count(b, 1, 0))
                        wait(pe, c_done, count(b, 2, 2))
                        wait(pe, v_in[s], count_own(b, 16, 16))
                        for ones in range(2):
                            for c in range(4):
                                rows = slice(32 * c, 32 * c + 32)
                                mm = nc.tensor.matmul(ND[rows, ones * 256:ones * 256 + 256],
                                                      C.ones[:, 0:32] if ones else vn[:, s, rows],
                                                      Ct[:, s, 2 * c:2 * c + 2, :].rearrange("p h k -> p (h k)"),
                                                      start=True, stop=True)
                        mm.then_inc(nd_mm, 1)

                    def gather(b, s):
                        wait(pe, o_done, count(b, 1, 0))
                        wait(pe, nd_done, count(b, 1, 1))
                        for ones in range(2):
                            for j in range(2):
                                mm = nc.tensor.matmul(O[s][:, ones * P:(ones + 1) * P], nd[:, s, 2 * ones + j, :],
                                                      C.id2[:, j * P:(j + 1) * P], start=(j == 0), stop=(j == 1))
                        mm.then_inc(o_mm, 1)

                    def step(b, s, tail, head, front):
                        if tail:
                            sum_keys(shift(b, -1), 1 - s)
                        if head:
                            scores(b, s)
                        if tail:
                            gather(shift(b, -1), 1 - s)
                    pipeline(pe, step)

                @block.vector
                def _(dve):
                    def exponents(b, s):
                        wait(dve, c_done, count(b, 2, -2))
                        wait(dve, loaded[s], count_own(b, 32, 32))
                        for h in range(HEADS):
                            g = gt[:, b, h:h + 1] if isinstance(b, int) else gt[:, bass.ds(b[0] * 2 + b[1], 1), h]
                            ins = nc.vector.tensor_scalar(W[:, s, h, :], Mb[:, s, h, :], g, 0.0, ALU.subtract, ALU.max)
                        ins.then_inc(w_done, 1)

                    def weigh(b, s):
                        wait(dve, mask_done, count(b, 1, 1))
                        wait(dve, nd_mm, count(b, 1, -1))
                        for q in range(2):
                            wait(dve, s_mm, count(b, 2, q + 1))
                            part = lambda t: t[:, s, 4 * q:4 * q + 4, :].rearrange("p h k -> p (h k)")
                            nc.vector.tensor_tensor(part(Ct), part(W), S[2 * s + q][:, :], ALU.mult).then_inc(c_done, 1)

                    def step(b, s, tail, head, front):
                        if front:
                            exponents(shift(b, 1), 1 - s)
                        if head:
                            weigh(b, s)
                    exponents(0, 0)
                    pipeline(dve, step)

                @block.scalar
                def _(act):
                    def exps(b, s):
                        wait(act, w_done, count(b, 1, 1))
                        nc.scalar.activation(flat(W, s), flat(W, s), ACT.Exp, scale=-1.0).then_inc(exp_done, 1)

                    def copy_sums(b, s):
                        wait(act, o_mm, count(b, 1, 0))
                        wait(act, nd_mm, count(b, 1, 1))
                        nc.scalar.copy(nd[:, s, :, :].rearrange("p j q -> p (j q)"), ND[:, :]).then_inc(nd_done, 1)

                    def copy_out(b, s):
                        wait(act, o_mm, count(b, 1, 1))
                        settle(act, pad)
                        if isinstance(b, int):
                            values, weights = H[:, b, :, 0:HD], H[:, b, :, HD]
                        else:
                            at = bass.ds(b[0] * 2 + b[1], 1)
                            values = H[:, at, :, 0:HD].rearrange("p a h k -> p (a h) k")
                            weights = H[:, at, :, HD].rearrange("p a h -> p (a h)")
                        heads = lambda n: O[s][:, n * P:(n + 1) * P].rearrange("p (h k) -> p h k", k=HD)
                        nc.scalar.copy(values, heads(0))
                        nc.scalar.copy(weights, heads(1)[:, :, 0]).then_inc(o_done, 1)

                    def step(b, s, tail, head, front):
                        if tail:
                            copy_sums(shift(b, -1), 1 - s)
                        if front:
                            exps(shift(b, 1), 1 - s)
                        if tail:
                            copy_out(shift(b, -1), 1 - s)
                    exps(0, 0)
                    pipeline(act, step)
            sems.clear()

        n = sb("n", [P, ROWS])
        o = sb("o", [P, ROWS, HD])
        o2 = sb("o2", [P, ROWS, HD])
        mean = sb("mean", [P, ROWS])
        var = sb("var", [P, ROWS])
        rstd = sb("rstd", [P, ROWS])
        PARTS = 4
        per = ROWS // PARTS
        dev = sb("dev", [P, ROWS])
        steps, var_done, dev_done, rstd_done, scaled, out_done = sems(6)
        sums = H[:, :, :, :].rearrange("p b h k -> p (b h) k")
        with nc.Block() as block:
            @block.vector
            def _(dve):
                chain = Chain(dve, steps)

                def step(f, *args):
                    chain.wait()
                    chain.add(f(*args))
                chain.add(nc.vector.scalar_tensor_tensor(n[:, :], sums[:, :, HD], -1.0, sums[:, :, HD], ALU.mult, ALU.max))
                step(nc.vector.tensor_tensor, n[:, :], n[:, :], em[:, :, :].rearrange("p b h -> p (b h)"), ALU.max)
                step(nc.vector.tensor_scalar, n[:, :], n[:, :], 1e-6, 1.0, ALU.add, ALU.mult)
                step(nc.vector.reciprocal, n[:, :], n[:, :])

                def add(q):
                    dve.wait_ge(out_done, q + 1)
                    part = X[:, q * per * HD:(q + 1) * per * HD]
                    nc.vector.tensor_tensor(part, part, o[:, q * per:(q + 1) * per, :].rearrange("p c k -> p (c k)"),
                                            ALU.add)
                for q in range(PARTS):
                    r = slice(q * per, (q + 1) * per)
                    step(nc.vector.tensor_tensor, o[:, r, :], sums[:, r, 0:HD], bcast_in(n[:, r], HD), ALU.mult)
                    step(nc.vector.tensor_reduce, mean[:, r], o[:, r, :], AXX, ALU.add)
                    step(nc.vector.tensor_scalar, mean[:, r], mean[:, r], 1.0 / HD, 0.0, ALU.mult, ALU.add)
                    step(nc.vector.tensor_tensor, o[:, r, :], o[:, r, :], bcast_in(mean[:, r], HD), ALU.subtract)
                    step(nc.vector.tensor_tensor, o2[:, r, :], o[:, r, :], o[:, r, :], ALU.mult)
                    chain.wait()
                    nc.vector.tensor_reduce(var[:, r], o2[:, r, :], AXX, ALU.add).then_inc(var_done, 1)
                    dve.wait_ge(dev_done, q + 1)
                    nc.vector.reciprocal(rstd[:, r], dev[:, r]).then_inc(rstd_done, 1)
                    if q > 0:
                        add(q - 1)
                add(PARTS - 1)

            @block.scalar
            def _(act):
                for q in range(PARTS):
                    r = slice(q * per, (q + 1) * per)
                    act.wait_ge(var_done, q + 1)
                    nc.scalar.activation(dev[:, r], var[:, r], ACT.Sqrt, bias=C.eps, scale=1.0 / HD).then_inc(dev_done, 1)

            @block.gpsimd
            def _(pool):
                for q in range(PARTS):
                    r = slice(q * per, (q + 1) * per)
                    pool.wait_ge(rstd_done, q + 1)
                    pool.tensor_tensor(o[:, r, :], o[:, r, :], bcast_in(rstd[:, r], HD), ALU.mult).then_inc(scaled, 1)
                    part = o[:, r, :].rearrange("p (b h) k -> p b (h k)", h=HEADS)
                    pool.wait_ge(scaled, 2 * q + 1)
                    pool.tensor_tensor(part, part, bcast_mid(gn[:, 0, :], per // HEADS), ALU.mult).then_inc(scaled, 1)
                    pool.wait_ge(scaled, 2 * q + 2)
                    pool.tensor_tensor(part, part, bcast_mid(gn[:, 1, :], per // HEADS), ALU.add).then_inc(out_done, 1)
        sems.clear()


STAGES = [stage_l0_values, stage_l0_attn, stage_l0_xattn, stage_l0_ffn, stage_l1_attn, stage_l1_xattn, stage_l1_ffn, stage_l2_attn,
          stage_l2_xattn, stage_l2_ffn, stage_l3_attn, stage_l3_xattn, stage_l3_ffn]



def build(nc, d, x_dram, out_dram, stages=None):
    with ExitStack() as ctx:
        X = ctx.enter_context(nc.sbuf_tensor("x_sbuf", [P, NB * DM], F32))
        C = Consts(nc, ctx)
        x_in = ctx.enter_context(nc.semaphore("x_in"))
        x_out = ctx.enter_context(nc.semaphore("x_out"))
        C.v_moved = ctx.enter_context(nc.semaphore("l0x_v_moved"))
        C.experts_in = ctx.enter_context(nc.semaphore("experts_in"))
        sems = Sems(nc, ctx, 44)
        with nc.Block() as block:
            @block.sync
            def _(sp):
                sp.dma_start(C.tile[:, :], d["consts"]).then_inc(x_in, 16)
                sp.dma_start(X[:, :], x_dram).then_inc(x_in, 16)
                sp.wait_ge(x_in, 32)
        for stage in (STAGES if stages is None else stages):
            stage(nc, C, sems, d, X)
        with nc.Block() as block:
            @block.sync
            def _(sp):
                sp.dma_start(out_dram, X[:, :]).then_inc(x_out, 16)
                sp.wait_ge(x_out, 16)



def arrange(v):
    t = lambda a: np.ascontiguousarray(np.swapaxes(a, -1, -2))
    cols = lambda arrays: np.ascontiguousarray(np.stack(arrays, axis=1))
    a = {"consts": Consts.values()}
    a["l0a_w"] = cols([t(v["L0_attn_W" + n]) for n in "qkvo"])
    a["l0a_a"] = cols([v["L0_attn_A" + n] for n in "qkvo"])
    a["l0a_b"] = cols([t(v["L0_attn_B" + n]) for n in "qkvo"])
    a["l0a_bo"] = v["L0_attn_bo"][None]
    a["ctxT"] = t(v["ctx_1024"])
    a["ctxT_rows"] = v["ctx_1024"].transpose(2, 0, 1).reshape(P, NB * P)
    a["l0x_w"] = cols([t(v["L0_xattn_w" + n]) for n in "qkvo"])
    a["l0f_phiT"] = t(v["L0_ffn_phi_w"])
    a["l0f_phi_b"] = v["L0_ffn_phi_b"]
    a["l0f_ew"] = v["L0_ffn_expert_w"].transpose(1, 0, 2)
    a["l0f_eb"] = v["L0_ffn_expert_b"]
    a["l1a_w"] = cols([t(v["L1_attn_W" + n]) for n in "qkvgo"])
    a["l1a_conv"] = np.concatenate([v["L1_attn_conv_" + n] for n in "qkv"]).T.reshape(-1)
    blocks = np.zeros((16, 8, 16, 8), np.float32)
    blocks[np.arange(16), :, np.arange(16), :] = v["L1_attn_W_init"][0]
    a["l1a_w0"] = blocks.reshape(P, P)
    a["l1a_gb"] = np.concatenate([v["L1_attn_ln_gamma"], v["L1_attn_ln_beta"]])
    a["l2a_w"] = np.concatenate([v["L2_attn_w_qkv"].T, v["L2_attn_w_out"].T], axis=1)
    chunks = lambda m: m.reshape(8, P, -1).transpose(1, 0, 2)
    a["l1x_w"] = cols([v["L1_xattn_W" + n] for n in "qkv"])
    a["l1x_wf"] = chunks(v["L1_xattn_Wf"])
    a["l1x_b"] = cols([v["L1_xattn_b" + n].reshape(8, P).T for n in "qkv"])
    a["l1x_bf"] = v["L1_xattn_bf"][None]
    a["l3a_w"] = cols([v["L3_attn_w_" + n].reshape(8 * P, P).T for n in "qkv"])
    a["l3a_wf"] = chunks(v["L3_attn_w_o"].T)
    a["l2x_w"] = cols([t(v["L2_xattn_W" + n]) for n in "qkvo"])
    a["l2x_b"] = cols([v["L2_xattn_b" + n] for n in "qkv"])
    a["l2x_bo"] = v["L2_xattn_bo"][None]
    a["l1f_w"], a["l1f_b"] = v["L1_ffn_weight"], v["L1_ffn_bias"]
    a["l2f_wr"], a["l2f_rb"] = v["L2_ffn_router_w"].T, v["L2_ffn_router_bias"]
    shared = lambda w: v[w].reshape(4, P, P)
    for n, name in (("wg", "gate_w"), ("wu", "up_w")):
        stack = np.concatenate([v["L2_ffn_" + name], shared("L2_ffn_s" + name)])
        a["l2f_" + n] = stack.transpose(2, 0, 1)
    down = np.concatenate([v["L2_ffn_down_w"], v["L2_ffn_sdown_w"].reshape(P, 4, P).transpose(1, 0, 2)])
    a["l2f_wd"] = down.transpose(2, 0, 1)
    a["l3f_w"] = cols([*np.split(v["L3_ffn_w_qkv"], 3, axis=1), v["L3_ffn_w_o"]])
    a["l3f_v"] = cols([v["L3_ffn_ln" + n] for n in ("1_w", "1_b", "2_w", "2_b")] + np.split(v["L3_ffn_b_qkv"], 3))
    a["l3f_bo"] = v["L3_ffn_b_o"][None]
    a["l3f_wg"], a["l3f_b2"] = v["L3_ffn_w_gate"], v["L3_ffn_b2"]
    a["l3f_w1"] = v["L3_ffn_w1"].reshape(8, P, 4, P).transpose(1, 0, 2, 3).reshape(P, 32, P)
    a["l3f_w2"] = v["L3_ffn_w2"].reshape(32, P, P).transpose(1, 0, 2)
    a["l3f_b1"] = v["L3_ffn_b1"].reshape(32, P).T
    gates = np.concatenate([v["L3_xattn_Wi_w"], v["L3_xattn_Wf_w"]]).reshape(16, 3, P)
    a["l3x_wg"] = gates.transpose(2, 1, 0)
    a["l3x_gb"] = np.concatenate([v["L3_xattn_Wi_b"], v["L3_xattn_Wf_b"]])[:, None]
    a["l3x_gnw"], a["l3x_gnb"] = v["L3_xattn_gn_w"], v["L3_xattn_gn_b"]
    a["ctx"] = v["ctx_1024"]
    a["l0x_b"] = cols([v["L0_xattn_b" + n][None] for n in "qkvo"])
    return a


def kernel(**inputs):
    import concourse.bacc as bacc
    from concourse.bass_utils import run_bass_kernel_spmd

    v = {n: np.asarray(a) for n, a in inputs.items()}
    arrays = {n: np.ascontiguousarray(a) for n, a in arrange(v).items()}
    arrays["x_tokens"] = np.ascontiguousarray(v["x"].transpose(1, 0, 2).reshape(P, NB * DM))
    nc = bacc.Bacc("TRN2", target_bir_lowering=False, num_devices=1)
    d = {n: nc.dram_tensor("in_" + n, a.shape, F32, kind="ExternalInput").ap() for n, a in arrays.items()}
    out = nc.dram_tensor("out", (P, NB * DM), F32, kind="ExternalOutput").ap()
    build(nc, d, d["x_tokens"], out)
    r = run_bass_kernel_spmd(nc, [{"in_" + n: a for n, a in arrays.items()}], core_ids=[0])
    return np.ascontiguousarray(r.results[0]["out"].reshape(P, NB, DM).transpose(1, 0, 2))
```
